# Optimizing a Trainium2 kernel written in Bass

```python
import numpy as np
import jax
import jax.numpy as jnp

def _softmax(x, axis=-1):
    return jax.nn.softmax(x, axis=axis)

def _gelu(x):
    return jax.nn.gelu(x, approximate=True)

def _silu(x):
    return jax.nn.silu(x)

def _sigmoid(x):
    return jax.nn.sigmoid(x)

def _layernorm(x, axis=-1, eps=1e-05):
    m = jnp.mean(x, axis=axis, keepdims=True)
    v = jnp.var(x, axis=axis, keepdims=True)
    return (x - m) / jnp.sqrt(v + eps)

def _scatter_add(tgt, idx, src, axis=0):
    return tgt.at[idx].add(src)

def _segment_sum(src, seg, n):
    return jax.ops.segment_sum(src, seg, n)
kernel_name = 'mk_hybrid_d2_jaxref_r8_4616ba'

def setup_inputs(seed: int=0):
    np.random.seed(seed)
    _w = jnp.asarray

    def _L0_attn_a_setup():
        import jax, jax.numpy as jnp
        import numpy as np
        DIM = 256
        D_STATE = 128
        D_CONV = 4
        N_HEADS = 48
        N_GROUPS = 1
        D_HEAD = 64
        D_INNER = N_HEADS * D_HEAD
        EPS = 1e-05
        RES_MULT = 1.0
        SEQ = 128
        BATCH = 1

        def _rms(x, w, eps=EPS):
            return x * jax.lax.rsqrt(jnp.mean(x * x, axis=-1, keepdims=True) + eps) * w

        def _forward(x, norm_w, in_proj_w, conv_w, conv_b, dt_bias, A_log, D_param, inner_norm_w, out_proj_w, conv_state, ssm_state):
            b, s, _ = x.shape
            xn = _rms(x, norm_w)
            proj = xn @ in_proj_w.T
            gn = N_GROUPS * D_STATE
            z, xc, B, C, dt = jnp.split(proj, [D_INNER, 2 * D_INNER, 2 * D_INNER + gn, 2 * D_INNER + 2 * gn], axis=-1)
            xc = jnp.moveaxis(xc, 1, 2)
            xp = jnp.concatenate([jnp.broadcast_to(conv_state, (b, D_INNER, D_CONV - 1)), xc], axis=-1)
            conv_out = conv_b[None, :, None] + sum((conv_w[None, :, k, None] * xp[:, :, k:k + s] for k in range(D_CONV)))
            xc = jax.nn.silu(conv_out)
            x_ssm = jnp.moveaxis(xc, 1, 2).reshape(b, s, N_HEADS, D_HEAD)
            hpg = N_HEADS // N_GROUPS
            B = jnp.repeat(B.reshape(b, s, N_GROUPS, D_STATE), hpg, axis=2)
            C = jnp.repeat(C.reshape(b, s, N_GROUPS, D_STATE), hpg, axis=2)
            dt = jax.nn.softplus(dt + dt_bias)
            A = -jnp.exp(A_log)
            h0 = jnp.broadcast_to(ssm_state, (b, N_HEADS, D_STATE, D_HEAD))

            def step(h, ins):
                x_t, B_t, C_t, dt_t = ins
                dA = jnp.exp(A * dt_t)[..., None, None]
                h = dA * h + B_t[..., :, None] * x_t[..., None, :]
                y_t = jnp.einsum('bhnp,bhn->bhp', h, C_t) + D_param[None, :, None] * x_t
                return (h, y_t)
            _, ys = jax.lax.scan(step, h0, (jnp.moveaxis(x_ssm, 1, 0), jnp.moveaxis(B, 1, 0), jnp.moveaxis(C, 1, 0), jnp.moveaxis(dt, 1, 0)))
            y = jnp.moveaxis(ys, 0, 1).reshape(b, s, D_INNER)
            y = _rms(y, inner_norm_w)
            y = y * jax.nn.silu(z)
            out = y @ out_proj_w.T
            return x + out * RES_MULT
        key = jax.random.key(seed)
        ks = jax.random.split(key, 12)
        d_in_proj = 2 * D_INNER + 2 * N_GROUPS * D_STATE + N_HEADS
        return {'x': jax.random.normal(ks[0], (BATCH, SEQ, DIM), jnp.float32), 'norm_w': jnp.ones((DIM,), jnp.float32), 'in_proj_w': 0.02 * jax.random.normal(ks[1], (d_in_proj, DIM), jnp.float32), 'conv_w': 0.02 * jax.random.normal(ks[2], (D_INNER, D_CONV), jnp.float32), 'conv_b': 0.01 * jax.random.normal(ks[3], (D_INNER,), jnp.float32), 'dt_bias': 0.1 * jax.random.normal(ks[4], (N_HEADS,), jnp.float32), 'A_log': 0.1 * jax.random.normal(ks[5], (N_HEADS,), jnp.float32), 'D_param': 0.1 * jax.random.normal(ks[6], (N_HEADS,), jnp.float32), 'inner_norm_w': jnp.ones((D_INNER,), jnp.float32), 'out_proj_w': 0.02 * jax.random.normal(ks[7], (DIM, D_INNER), jnp.float32), 'conv_state': jnp.zeros((1, D_INNER, D_CONV - 1), jnp.float32), 'ssm_state': jnp.zeros((1, N_HEADS, D_STATE, D_HEAD), jnp.float32)}
    _L0_attn_a_in = _L0_attn_a_setup()

    def _L0_attn_b_setup():
        import jax, jax.numpy as jnp
        import numpy as np
        D_ATTN = 256
        D_STATE = 64
        SHIFT_FRAC = 0.5
        LN_EPS = 1e-05

        def _reference_tuple_inner(x, W_key, W_value, W_output, W_shift, gate, time_decay, time_first, ln_gamma, ln_beta):
            B, T, D = x.shape
            shift_len = max(1, int(T * SHIFT_FRAC))
            x_cat = jnp.roll(x, -shift_len, axis=1)
            g = jax.nn.sigmoid(gate)
            x_shift = jnp.einsum('btd,ed->bte', x_cat, W_shift) * g + x * (1.0 - g)
            mu = jnp.mean(x_shift, axis=-1, keepdims=True)
            var = jnp.var(x_shift, axis=-1, keepdims=True)
            x_norm = (x_shift - mu) * jax.lax.rsqrt(var + LN_EPS) * ln_gamma + ln_beta
            k = jnp.einsum('btd,sd->bts', x_norm, W_key)
            v = jnp.einsum('btd,sd->bts', x_norm, W_value)
            w = jnp.exp(time_decay)
            u = jnp.exp(time_first)
            wkv = jnp.exp(-u * jax.nn.sigmoid(k)) * v

            def step(state, wkv_t):
                state = state * w + wkv_t
                return (state, state)
            init = jnp.zeros((B, k.shape[-1]), x.dtype)
            last_state, states = jax.lax.scan(step, init, jnp.swapaxes(wkv, 0, 1))
            states = jnp.swapaxes(states, 0, 1)
            output = jnp.einsum('bts,ds->btd', states, W_output)
            return (output, jax.lax.stop_gradient(last_state))
        key = jax.random.key(seed)
        ks = jax.random.split(key, 8)
        B, T = (8, 256)
        s_attn = 1.0 / np.sqrt(D_ATTN)
        s_state = 1.0 / np.sqrt(D_STATE)
        x = jax.random.normal(ks[0], (B, T, D_ATTN), jnp.float32)
        W_key = jax.random.normal(ks[1], (D_STATE, D_ATTN), jnp.float32) * s_attn
        W_value = jax.random.normal(ks[2], (D_STATE, D_ATTN), jnp.float32) * s_attn
        W_output = jax.random.normal(ks[3], (D_ATTN, D_STATE), jnp.float32) * s_state
        W_shift = jax.random.normal(ks[4], (D_ATTN, D_ATTN), jnp.float32) * s_attn
        gate = jnp.ones((D_ATTN,), jnp.float32)
        time_decay = -jax.random.uniform(ks[5], (D_STATE,), jnp.float32, 0.05, 1.0)
        time_first = jax.random.normal(ks[6], (D_STATE,), jnp.float32) * 0.1
        ln_gamma = jnp.ones((D_ATTN,), jnp.float32)
        ln_beta = jnp.zeros((D_ATTN,), jnp.float32)
        return dict(x=x, W_key=W_key, W_value=W_value, W_output=W_output, W_shift=W_shift, gate=gate, time_decay=time_decay, time_first=time_first, ln_gamma=ln_gamma, ln_beta=ln_beta)
    _L0_attn_b_in = _L0_attn_b_setup()

    def _L0_ffn_setup():
        import jax, jax.numpy as jnp
        import numpy as np
        TOP_K = 4
        key = jax.random.key(seed)
        ks = jax.random.split(key, 8)
        B, S, D, E, H, HS = (2, 256, 256, 16, 128, 512)
        scaled = lambda k, shape, fan: jax.random.normal(k, shape, jnp.float32) * fan ** (-0.5)
        return {'x': jax.random.normal(ks[0], (B, S, D), jnp.float32), 'w_router': scaled(ks[1], (D, E), D), 'we1': scaled(ks[2], (E, D, H), D), 'we3': scaled(ks[3], (E, D, H), D), 'we2': scaled(ks[4], (E, H, D), H), 'ws1': scaled(ks[5], (D, HS), D), 'ws3': scaled(ks[6], (D, HS), D), 'ws2': scaled(ks[7], (HS, D), HS)}
    _L0_ffn_in = _L0_ffn_setup()

    def _L1_attn_a_setup():
        import jax, jax.numpy as jnp
        import numpy as np
        BLOCK = 32
        EPS = 1e-06

        def _silu(x):
            return x * jax.nn.sigmoid(x)
        key = jax.random.key(seed)
        k1, k2, k3, k4 = jax.random.split(key, 4)
        embed_dim, hidden_dim = (256, 256)
        b, n, h = (2, 512, 16)
        x = jax.random.normal(k1, (b, n, embed_dim), dtype=jnp.float32)
        slope_rate = jax.random.uniform(k2, (h, 1, 1), dtype=jnp.float32, minval=0.01, maxval=1.0)
        W_qkvu = jax.random.normal(k3, (4 * hidden_dim, embed_dim), dtype=jnp.float32) / np.sqrt(embed_dim)
        W_out = jax.random.normal(k4, (embed_dim, hidden_dim), dtype=jnp.float32) / np.sqrt(hidden_dim)
        return {'x': x, 'slope_rate': slope_rate, 'W_qkvu': W_qkvu, 'W_out': W_out}
    _L1_attn_a_in = _L1_attn_a_setup()

    def _L1_attn_b_setup():
        import jax, jax.numpy as jnp
        import numpy as np
        D_MODEL = 256
        NUM_HEADS = 16
        DILATION = 2
        SEG = 64
        HEAD_DIM = D_MODEL // NUM_HEADS

        def _dilated_attention(x):
            B, N, D = x.shape
            w, r, H, hd = (SEG, DILATION, NUM_HEADS, HEAD_DIM)
            pad = -N % w
            x = jnp.pad(x, ((0, 0), (0, pad), (0, 0)))
            Np = N + pad
            nseg = Np // w
            s = w // r
            xs = x.reshape(B, nseg, w, H, hd).transpose(0, 1, 3, 2, 4)
            offsets = jnp.arange(H) % r
            idx = offsets[:, None] + jnp.arange(s)[None, :] * r
            g = jnp.take_along_axis(xs, idx[None, None, :, :, None], axis=3)
            scale = jnp.asarray(hd, x.dtype) ** (-0.5)
            scores = jnp.einsum('bnhqd,bnhkd->bnhqk', g, g) * scale
            attn = jax.nn.softmax(scores, axis=-1)
            out = jnp.einsum('bnhqk,bnhkd->bnhqd', attn, g)
            out_full = jnp.zeros((B, nseg, H, w, hd), dtype=x.dtype)
            out_full = out_full.at[:, :, jnp.arange(H)[:, None], idx, :].set(out)
            out_full = out_full.transpose(0, 1, 3, 2, 4).reshape(B, Np, D)
            return out_full[:, :N, :]
        key = jax.random.key(seed)
        x = jax.random.normal(key, (4, 1024, D_MODEL), dtype=jnp.float32)
        return {'x': x}
    _L1_attn_b_in = _L1_attn_b_setup()

    def _L1_ffn_setup():
        import jax, jax.numpy as jnp
        import numpy as np
        D = 256
        H_TOTAL = 1024
        E = 8
        K = 2
        HE = H_TOTAL // E
        B, S = (2, 256)
        key = jax.random.key(seed)
        ks = jax.random.split(key, 8)
        scale_up = 1.0 / np.sqrt(D)
        scale_dn = 1.0 / np.sqrt(HE)
        return {'x': jax.random.normal(ks[0], (B, S, D), dtype=jnp.float32), 'Wg1': jax.random.normal(ks[1], (E, D), dtype=jnp.float32) * 0.02, 'Wg2': jax.random.normal(ks[2], (E, E), dtype=jnp.float32) * 0.2, 'Wup': jax.random.uniform(ks[3], (E, HE, D), dtype=jnp.float32, minval=-scale_up, maxval=scale_up), 'bup': jax.random.uniform(ks[4], (E, HE), dtype=jnp.float32, minval=-scale_up, maxval=scale_up), 'Wdown': jax.random.uniform(ks[5], (E, D, HE), dtype=jnp.float32, minval=-scale_dn, maxval=scale_dn), 'bdown': jax.random.uniform(ks[6], (E, D), dtype=jnp.float32, minval=-scale_dn, maxval=scale_dn)}
    _L1_ffn_in = _L1_ffn_setup()
    _d = {'L0_attn_a_x': _L0_attn_a_in['x'], 'L0_attn_a_norm_w': _L0_attn_a_in['norm_w'], 'L0_attn_a_in_proj_w': _L0_attn_a_in['in_proj_w'], 'L0_attn_a_conv_w': _L0_attn_a_in['conv_w'], 'L0_attn_a_conv_b': _L0_attn_a_in['conv_b'], 'L0_attn_a_dt_bias': _L0_attn_a_in['dt_bias'], 'L0_attn_a_A_log': _L0_attn_a_in['A_log'], 'L0_attn_a_D_param': _L0_attn_a_in['D_param'], 'L0_attn_a_inner_norm_w': _L0_attn_a_in['inner_norm_w'], 'L0_attn_a_out_proj_w': _L0_attn_a_in['out_proj_w'], 'L0_attn_a_conv_state': _L0_attn_a_in['conv_state'], 'L0_attn_a_ssm_state': _L0_attn_a_in['ssm_state'], 'L0_attn_b_W_key': _L0_attn_b_in['W_key'], 'L0_attn_b_W_value': _L0_attn_b_in['W_value'], 'L0_attn_b_W_output': _L0_attn_b_in['W_output'], 'L0_attn_b_W_shift': _L0_attn_b_in['W_shift'], 'L0_attn_b_gate': _L0_attn_b_in['gate'], 'L0_attn_b_time_decay': _L0_attn_b_in['time_decay'], 'L0_attn_b_time_first': _L0_attn_b_in['time_first'], 'L0_attn_b_ln_gamma': _L0_attn_b_in['ln_gamma'], 'L0_attn_b_ln_beta': _L0_attn_b_in['ln_beta'], 'L0_ffn_w_router': _L0_ffn_in['w_router'], 'L0_ffn_we1': _L0_ffn_in['we1'], 'L0_ffn_we3': _L0_ffn_in['we3'], 'L0_ffn_we2': _L0_ffn_in['we2'], 'L0_ffn_ws1': _L0_ffn_in['ws1'], 'L0_ffn_ws3': _L0_ffn_in['ws3'], 'L0_ffn_ws2': _L0_ffn_in['ws2'], 'L1_attn_a_slope_rate': _L1_attn_a_in['slope_rate'], 'L1_attn_a_W_qkvu': _L1_attn_a_in['W_qkvu'], 'L1_attn_a_W_out': _L1_attn_a_in['W_out'], 'L1_ffn_Wg1': _L1_ffn_in['Wg1'], 'L1_ffn_Wg2': _L1_ffn_in['Wg2'], 'L1_ffn_Wup': _L1_ffn_in['Wup'], 'L1_ffn_bup': _L1_ffn_in['bup'], 'L1_ffn_Wdown': _L1_ffn_in['Wdown'], 'L1_ffn_bdown': _L1_ffn_in['bdown']}
    _x0 = _d['L0_attn_a_x']
    _d['L0_attn_a_x'] = jax.random.normal(jax.random.fold_in(jax.random.key(seed), 1), (4, 256, 256), dtype=_x0.dtype)
    del _x0
    return _d

def reference(L0_attn_a_x, L0_attn_a_norm_w, L0_attn_a_in_proj_w, L0_attn_a_conv_w, L0_attn_a_conv_b, L0_attn_a_dt_bias, L0_attn_a_A_log, L0_attn_a_D_param, L0_attn_a_inner_norm_w, L0_attn_a_out_proj_w, L0_attn_a_conv_state, L0_attn_a_ssm_state, L0_attn_b_W_key, L0_attn_b_W_value, L0_attn_b_W_output, L0_attn_b_W_shift, L0_attn_b_gate, L0_attn_b_time_decay, L0_attn_b_time_first, L0_attn_b_ln_gamma, L0_attn_b_ln_beta, L0_ffn_w_router, L0_ffn_we1, L0_ffn_we3, L0_ffn_we2, L0_ffn_ws1, L0_ffn_ws3, L0_ffn_ws2, L1_attn_a_slope_rate, L1_attn_a_W_qkvu, L1_attn_a_W_out, L1_ffn_Wg1, L1_ffn_Wg2, L1_ffn_Wup, L1_ffn_bup, L1_ffn_Wdown, L1_ffn_bdown):

    def _L0_attn_a_ref(x, norm_w, in_proj_w, conv_w, conv_b, dt_bias, A_log, D_param, inner_norm_w, out_proj_w, conv_state, ssm_state):
        import jax, jax.numpy as jnp
        import numpy as np
        DIM = 256
        D_STATE = 128
        D_CONV = 4
        N_HEADS = 48
        N_GROUPS = 1
        D_HEAD = 64
        D_INNER = N_HEADS * D_HEAD
        EPS = 1e-05
        RES_MULT = 1.0
        SEQ = 128
        BATCH = 1

        def _rms(x, w, eps=EPS):
            return x * jax.lax.rsqrt(jnp.mean(x * x, axis=-1, keepdims=True) + eps) * w

        def _forward(x, norm_w, in_proj_w, conv_w, conv_b, dt_bias, A_log, D_param, inner_norm_w, out_proj_w, conv_state, ssm_state):
            b, s, _ = x.shape
            xn = _rms(x, norm_w)
            proj = xn @ in_proj_w.T
            gn = N_GROUPS * D_STATE
            z, xc, B, C, dt = jnp.split(proj, [D_INNER, 2 * D_INNER, 2 * D_INNER + gn, 2 * D_INNER + 2 * gn], axis=-1)
            xc = jnp.moveaxis(xc, 1, 2)
            xp = jnp.concatenate([jnp.broadcast_to(conv_state, (b, D_INNER, D_CONV - 1)), xc], axis=-1)
            conv_out = conv_b[None, :, None] + sum((conv_w[None, :, k, None] * xp[:, :, k:k + s] for k in range(D_CONV)))
            xc = jax.nn.silu(conv_out)
            x_ssm = jnp.moveaxis(xc, 1, 2).reshape(b, s, N_HEADS, D_HEAD)
            hpg = N_HEADS // N_GROUPS
            B = jnp.repeat(B.reshape(b, s, N_GROUPS, D_STATE), hpg, axis=2)
            C = jnp.repeat(C.reshape(b, s, N_GROUPS, D_STATE), hpg, axis=2)
            dt = jax.nn.softplus(dt + dt_bias)
            A = -jnp.exp(A_log)
            h0 = jnp.broadcast_to(ssm_state, (b, N_HEADS, D_STATE, D_HEAD))

            def step(h, ins):
                x_t, B_t, C_t, dt_t = ins
                dA = jnp.exp(A * dt_t)[..., None, None]
                h = dA * h + B_t[..., :, None] * x_t[..., None, :]
                y_t = jnp.einsum('bhnp,bhn->bhp', h, C_t) + D_param[None, :, None] * x_t
                return (h, y_t)
            _, ys = jax.lax.scan(step, h0, (jnp.moveaxis(x_ssm, 1, 0), jnp.moveaxis(B, 1, 0), jnp.moveaxis(C, 1, 0), jnp.moveaxis(dt, 1, 0)))
            y = jnp.moveaxis(ys, 0, 1).reshape(b, s, D_INNER)
            y = _rms(y, inner_norm_w)
            y = y * jax.nn.silu(z)
            out = y @ out_proj_w.T
            return x + out * RES_MULT
        return _forward(x, norm_w, in_proj_w, conv_w, conv_b, dt_bias, A_log, D_param, inner_norm_w, out_proj_w, conv_state, ssm_state)

    def _L0_attn_b_ref(x, W_key, W_value, W_output, W_shift, gate, time_decay, time_first, ln_gamma, ln_beta):
        import jax, jax.numpy as jnp
        import numpy as np
        D_ATTN = 256
        D_STATE = 64
        SHIFT_FRAC = 0.5
        LN_EPS = 1e-05

        def _reference_tuple_inner(x, W_key, W_value, W_output, W_shift, gate, time_decay, time_first, ln_gamma, ln_beta):
            B, T, D = x.shape
            shift_len = max(1, int(T * SHIFT_FRAC))
            x_cat = jnp.roll(x, -shift_len, axis=1)
            g = jax.nn.sigmoid(gate)
            x_shift = jnp.einsum('btd,ed->bte', x_cat, W_shift) * g + x * (1.0 - g)
            mu = jnp.mean(x_shift, axis=-1, keepdims=True)
            var = jnp.var(x_shift, axis=-1, keepdims=True)
            x_norm = (x_shift - mu) * jax.lax.rsqrt(var + LN_EPS) * ln_gamma + ln_beta
            k = jnp.einsum('btd,sd->bts', x_norm, W_key)
            v = jnp.einsum('btd,sd->bts', x_norm, W_value)
            w = jnp.exp(time_decay)
            u = jnp.exp(time_first)
            wkv = jnp.exp(-u * jax.nn.sigmoid(k)) * v

            def step(state, wkv_t):
                state = state * w + wkv_t
                return (state, state)
            init = jnp.zeros((B, k.shape[-1]), x.dtype)
            last_state, states = jax.lax.scan(step, init, jnp.swapaxes(wkv, 0, 1))
            states = jnp.swapaxes(states, 0, 1)
            output = jnp.einsum('bts,ds->btd', states, W_output)
            return (output, jax.lax.stop_gradient(last_state))
        return _reference_tuple_inner(x, W_key, W_value, W_output, W_shift, gate, time_decay, time_first, ln_gamma, ln_beta)[0]

    def _L0_ffn_ref(x, w_router, we1, we3, we2, ws1, ws3, ws2):
        import jax, jax.numpy as jnp
        import numpy as np
        TOP_K = 4
        B, S, D = x.shape
        T = B * S
        E = w_router.shape[1]
        xt = x.reshape(T, D)
        probs = jax.nn.softmax(xt @ w_router, axis=-1)
        top_w, top_i = jax.lax.top_k(probs, TOP_K)
        top_w = top_w / jnp.sum(top_w, axis=-1, keepdims=True)
        cw = jnp.zeros((T, E), xt.dtype).at[jnp.arange(T)[:, None], top_i].add(top_w)
        g = jax.nn.silu(jnp.einsum('td,edh->teh', xt, we1)) * jnp.einsum('td,edh->teh', xt, we3)
        g = g * cw[:, :, None]
        moe_out = jnp.einsum('teh,ehd->td', g, we2)
        shared = jax.nn.silu(xt @ ws1) * (xt @ ws3) @ ws2
        k = TOP_K
        out = shared / (k + 1) + moe_out * (k / (k + 1))
        return out.reshape(B, S, D)

    def _L1_attn_a_ref(x, slope_rate, W_qkvu, W_out):
        import jax, jax.numpy as jnp
        import numpy as np
        BLOCK = 32
        EPS = 1e-06

        def _silu(x):
            return x * jax.nn.sigmoid(x)
        b, n, embed_dim = x.shape
        h = slope_rate.shape[0]
        hidden_dim = W_qkvu.shape[0] // 4
        d = hidden_dim // h
        NB = n // BLOCK
        qkvu = x @ W_qkvu.T
        q, k, v, u = jnp.split(qkvu, 4, axis=-1)

        def to_heads(t):
            return t.reshape(b, n, h, d).transpose(0, 2, 1, 3)
        q = _silu(to_heads(q))
        k = _silu(to_heads(k))
        v = to_heads(v)
        s = slope_rate
        arr = jnp.arange(1, BLOCK + 1, dtype=x.dtype)
        q_decay = jnp.exp(-s * arr[:, None])
        k_decay = jnp.exp(-s * (BLOCK - arr[:, None]))
        idx = arr[:, None] - arr[None, :]
        diag_decay = jnp.exp(jnp.where(idx >= 0, -s * idx, -jnp.inf))
        block_decay = jnp.exp(-s * BLOCK)

        def blk(t):
            return t.reshape(b, h, NB, BLOCK, d).transpose(2, 0, 1, 3, 4)
        qb, kb, vb = (blk(q), blk(k), blk(v))

        def step(kv, inp):
            qi, ki, vi = inp
            qkv_none_diag = jnp.einsum('bhmd,bhde->bhme', qi * q_decay, kv)
            qk = jnp.einsum('bhmd,bhsd->bhms', qi, ki) * diag_decay
            qkv_diag = jnp.einsum('bhms,bhse->bhme', qk, vi)
            kv_new = block_decay * kv + jnp.einsum('bhsd,bhse->bhde', ki * k_decay, vi)
            return (kv_new, qkv_none_diag + qkv_diag)
        kv0 = jnp.zeros((b, h, d, d), dtype=jnp.float32)
        _, outs = jax.lax.scan(step, kv0, (qb, kb, vb))
        o = outs.transpose(1, 2, 0, 3, 4).reshape(b, h, n, d)
        o = o.transpose(0, 2, 1, 3).reshape(b, n, hidden_dim)
        o = o * jax.lax.rsqrt(jnp.mean(o * o, axis=-1, keepdims=True) + EPS)
        o = u * o
        return o @ W_out.T

    def _L1_attn_b_ref(x):
        import jax, jax.numpy as jnp
        import numpy as np
        D_MODEL = 256
        NUM_HEADS = 16
        DILATION = 2
        SEG = 64
        HEAD_DIM = D_MODEL // NUM_HEADS

        def _dilated_attention(x):
            B, N, D = x.shape
            w, r, H, hd = (SEG, DILATION, NUM_HEADS, HEAD_DIM)
            pad = -N % w
            x = jnp.pad(x, ((0, 0), (0, pad), (0, 0)))
            Np = N + pad
            nseg = Np // w
            s = w // r
            xs = x.reshape(B, nseg, w, H, hd).transpose(0, 1, 3, 2, 4)
            offsets = jnp.arange(H) % r
            idx = offsets[:, None] + jnp.arange(s)[None, :] * r
            g = jnp.take_along_axis(xs, idx[None, None, :, :, None], axis=3)
            scale = jnp.asarray(hd, x.dtype) ** (-0.5)
            scores = jnp.einsum('bnhqd,bnhkd->bnhqk', g, g) * scale
            attn = jax.nn.softmax(scores, axis=-1)
            out = jnp.einsum('bnhqk,bnhkd->bnhqd', attn, g)
            out_full = jnp.zeros((B, nseg, H, w, hd), dtype=x.dtype)
            out_full = out_full.at[:, :, jnp.arange(H)[:, None], idx, :].set(out)
            out_full = out_full.transpose(0, 1, 3, 2, 4).reshape(B, Np, D)
            return out_full[:, :N, :]
        return _dilated_attention(x)

    def _L1_ffn_ref(x, Wg1, Wg2, Wup, bup, Wdown, bdown):
        import jax, jax.numpy as jnp
        import numpy as np
        D = 256
        H_TOTAL = 1024
        E = 8
        K = 2
        HE = H_TOTAL // E
        B, S = (2, 256)
        Bd, Sd, Dd = x.shape
        T = Bd * Sd
        xt = x.reshape(T, Dd)
        logits = jnp.tanh(xt @ Wg1.T) @ Wg2.T
        _, top_idx = jax.lax.top_k(logits, K)
        top_logits = jnp.take_along_axis(logits, top_idx, axis=1)
        top_scores = jax.nn.softmax(top_logits.astype(jnp.float32), axis=1).astype(logits.dtype)
        rows = jnp.arange(T)[:, None]
        scores = jnp.zeros_like(logits).at[rows, top_idx].set(top_scores)
        up = jnp.einsum('td,ehd->teh', xt, Wup) + bup
        h = jax.nn.silu(up)
        down = jnp.einsum('teh,eoh->teo', h, Wdown) + bdown
        out = jnp.einsum('te,teo->to', scores, down)
        return out.reshape(Bd, Sd, Dd)
    x = L0_attn_a_x
    x = x + _L0_attn_a_ref(_layernorm(x, axis=-1), L0_attn_a_norm_w, L0_attn_a_in_proj_w, L0_attn_a_conv_w, L0_attn_a_conv_b, L0_attn_a_dt_bias, L0_attn_a_A_log, L0_attn_a_D_param, L0_attn_a_inner_norm_w, L0_attn_a_out_proj_w, L0_attn_a_conv_state, L0_attn_a_ssm_state)
    x = x + _L0_ffn_ref(_layernorm(x, axis=-1), L0_ffn_w_router, L0_ffn_we1, L0_ffn_we3, L0_ffn_we2, L0_ffn_ws1, L0_ffn_ws3, L0_ffn_ws2)
    x = x + _L0_attn_b_ref(_layernorm(x, axis=-1), L0_attn_b_W_key, L0_attn_b_W_value, L0_attn_b_W_output, L0_attn_b_W_shift, L0_attn_b_gate, L0_attn_b_time_decay, L0_attn_b_time_first, L0_attn_b_ln_gamma, L0_attn_b_ln_beta)
    x = x + _L0_ffn_ref(_layernorm(x, axis=-1), L0_ffn_w_router, L0_ffn_we1, L0_ffn_we3, L0_ffn_we2, L0_ffn_ws1, L0_ffn_ws3, L0_ffn_ws2)
    x = x + _L1_attn_a_ref(_layernorm(x, axis=-1), L1_attn_a_slope_rate, L1_attn_a_W_qkvu, L1_attn_a_W_out)
    x = x + _L1_ffn_ref(_layernorm(x, axis=-1), L1_ffn_Wg1, L1_ffn_Wg2, L1_ffn_Wup, L1_ffn_bup, L1_ffn_Wdown, L1_ffn_bdown)
    x = x + _L1_attn_b_ref(_layernorm(x, axis=-1))
    x = x + _L1_ffn_ref(_layernorm(x, axis=-1), L1_ffn_Wg1, L1_ffn_Wg2, L1_ffn_Wup, L1_ffn_bup, L1_ffn_Wdown, L1_ffn_bdown)
    return x

_drawn_inputs = setup_inputs


def setup_inputs(seed=0):
    import zlib

    import numpy as np

    out = dict(_drawn_inputs(seed))
    spreads = {'L0_attn_a_norm_w': (1.0, 0.2),
     'L0_attn_a_inner_norm_w': (1.0, 0.2),
     'L0_attn_a_conv_state': (0.0, 2.0),
     'L0_attn_a_ssm_state': (0.0, 0.272),
     'L0_attn_b_gate': (1.0, 0.2),
     'L0_attn_b_ln_gamma': (1.0, 0.2),
     'L0_attn_b_ln_beta': (0.0, 0.1)}
    factors = {'L0_attn_a_dt_bias': 4.334,
     'L0_attn_a_A_log': 3.395,
     'L1_ffn_bup': 8.0,
     'L0_attn_a_D_param': 2.7}
    for name, (base, spread) in spreads.items():
        noise = np.random.default_rng([zlib.crc32(name.encode()), seed]).standard_normal(out[name].shape)
        drawn = base * np.exp(spread * noise) if base else spread * noise
        out[name] = jnp.asarray(drawn.astype(out[name].dtype))
    for name, factor in factors.items():
        out[name] = (out[name] * factor).astype(out[name].dtype)
    return out
```

```python
from contextlib import ExitStack

import concourse.bass as bass
from concourse import mybir

FP32 = mybir.dt.float32
BF16 = mybir.dt.bfloat16
ALU = mybir.AluOpType
ACT = mybir.ActivationFunctionType
AX = mybir.AxisListType

P = 128
D = 256
KD = D // P
T = 1024
NT = T // P
NB = 4
LN_EPS = 1e-5
NEG = -1e30

DI = 3072
NH = 48
HD = 64
NS = 128
GH = 8
NG = NH // GH
GW = GH * HD
GC = GW // P
TAPS = 4
NPC = TAPS + 1 + (TAPS - 1) + 1


LH = 16
LD = 16
LQ = LH * 32
TINY = -3e38
TAKEN = 3e38


class Experts:

    def __init__(self, n, gated, routed, shared, top, norm, before):
        self.n, self.gated, self.routed, self.shared, self.top, self.norm = n, gated, routed, shared, top, norm
        self.count = routed + shared
        self.pairs = self.count // 2
        self.s0 = before.s0 + 4 * before.pairs if before else 0
        self.p0 = before.p0 + before.pairs if before else 0
        self.width = 256 * (2 if gated else 1) + (0 if gated else 1)


F2 = Experts(0, True, 16, 4, 4, 1, None)
F4 = Experts(1, True, 16, 4, 4, 4, F2)
F6 = Experts(2, False, 8, 0, 2, 6, F4)
F8 = Experts(3, False, 8, 0, 2, 8, F6)


class Chain:

    def __init__(self, eng, sem):
        self.eng, self.sem, self.base, self.n = eng, sem, 0, 0

    def link(self, ins):
        self.n += 1
        ins.then_inc(self.sem, 1)
        self.eng.wait_ge(self.sem, self.base + self.n)

    def enter(self, i, per):
        self.start, self.per = self.n, per
        self.base, self.n = i * per + self.n, 0

    def leave(self, times):
        assert self.n == self.per, self.n
        self.base, self.n = 0, self.start + self.per * times


def mixer_program(nc, x, consts, rows, cols, wx, wz, wbcdt, wout, chan, h0, small, w3, wo3, t3,
                  wu2, wd2, wu6, wd6, wg6, bd6, w5, wo5, out):
    ctx = ExitStack()
    with ctx:
        def sb(name, shape, dt=FP32):
            return ctx.enter_context(nc.sbuf_tensor(name, shape, dt))

        def sem(name):
            return ctx.enter_context(nc.semaphore(name))

        BANKS = ctx.enter_context(nc.psum_tensor("BANKS", [P, 8, 512], FP32))
        PS = [BANKS[:, n, :] for n in range(8)]

        X = sb("X", [P, NT, D])
        XN = sb("XN", [P, NT, D + 16])
        XT = sb("XT", [P, KD, T])
        K = sb("K", [P, 640])
        ident, tri, dist, blk = K[:, 0:128], K[:, 128:256], K[:, 256:512], K[:, 512:640]
        identb = sb("identb", [P, P], BF16)
        causalb = sb("causalb", [P, 4 * P], BF16)
        ROW = sb("ROW", [P, 3 * NH])
        COL = sb("COL", [P, 3, KD])
        bn = sb("bn", [P, NT, 6])
        mv = sb("mv", [P, NT, 2])
        rstd = sb("rstd", [P, NT])
        rms = sb("rms", [P, NT])
        half = sb("half", [P, NT])

        WB = sb("WB", [P, KD, 2 * NS + NH])
        BT = sb("BT", [P, T])
        CT = sb("CT", [P, T])
        BN = sb("BN", [P, NB, NS])
        GT = sb("GT", [P, NT, P])
        ones = sb("ones", [P, P])
        dtr = sb("dtr", [P, NT, NH])
        dta = sb("dta", [P, NT, NH])
        dA = sb("dA", [P, NT, NH])
        ncum = sb("ncum", [P, NT, NH])
        ecum = sb("ecum", [P, NT, NH])
        eend = sb("eend", [P, NT, NH])
        eA = sb("eA", [P, NH])
        GRP = sb("GRP", [P, 4, NT, GH])
        Dg = sb("Dg", [P, GH])
        WX = sb("WX", [P, KD, GW])
        WZ = sb("WZ", [P, KD, GW])
        WOr = sb("WOr", [P, GC, D])
        WO = sb("WO", [P, GC, D])
        CH = sb("CH", [P, GC, NPC])
        H0 = sb("H0", [P, GW])
        H1 = sb("H1", [P, GW])
        XP = sb("XP", [P, 2, NB, D + TAPS - 1])
        CVTH = sb("CVTH", [P, 4, NB, D])
        CV, TH = CVTH[:, 0:2, :, :], CVTH[:, 2:4, :, :]
        XTOK = sb("XTOK", [P, NT, GW])
        E = sb("E", [P, 2, GH, P])
        M = sb("M", [P, 2, GH, P])
        SZ = sb("SZ", [P, 2, GW])
        Y0 = sb("Y0", [P, 2, GW])
        Y1 = sb("Y1", [P, 2, GW])
        G = sb("G", [P, 2, GW])
        XD = sb("XD", [P, 2, GW])
        XS = sb("XS", [P, GW])
        GTR = sb("GTR", [P, 2, GW])
        OUT = sb("OUT", [P, NT, D])
        SQ = sb("SQ", [P, NT])
        SS = sb("SS", [P, NT])
        sqj = sb("sqj", [P, GW])

        SM = sb("SM", [P, KD, 24])
        WG = sb("WG", [8, 8])
        BD = sb("BD", [8, D])
        WU = [sb(f"WU{n}", [P, 512]) for n in range(2)]
        WD = [sb(f"WD{n}", [P, D]) for n in range(2)]
        FT = sb("FT", [P, 2, 512])
        FG = sb("FG", [P, 2, 512])
        LG = sb("LG", [P, NT, 20])
        LR = sb("LR", [P, NT, 20])
        MX = sb("MX", [P, NT, 8])
        SUM = sb("SUM", [P, NT])
        CW = sb("CW", [P, 20, NT])
        CWP = sb("CWP", [P, 2, NT])
        TT = sb("TT", [8, T])
        SCT = TT
        W3 = sb("W3", [P, KD, D + P])
        WO3 = sb("WO3", [64, D])
        T3 = sb("T3", [64, 2])
        GATE = sb("GATE", [P, 2, D])
        KS, WKV, ST = BT[0:64, :], CT[0:64, :], GT[0:64, :, :].rearrange("p t s -> p (t s)")
        W5 = XTOK[:, :, :].rearrange("p t n -> p (t n)")[:, 0:KD * (2 * LQ + 512)].rearrange("p (k n) -> p k n", k=KD)
        WO5 = XS[:, :].rearrange("p (k n) -> p k n", k=KD)
        DEC = CVTH[:, :, :, :].rearrange("p a b t -> p (a b) t")
        DMASK = sb("DMASK", [P, 2 * P])
        SLOPE = sb("SLOPE", [P, LH])
        XB = XD[:, 0, :].rearrange("p (k t) -> p k t", k=KD)
        QT = E[:, 0, :, :].rearrange("p (g a) t -> p g (a t)", g=4)
        KT = E[:, 1, :, :].rearrange("p (g a) t -> p g (a t)", g=4)
        UO, UOT = Y1[:, 0, :], G[:, 0, :]
        sso = sb("sso", [P, 2])
        tiny = sb("tiny", [P, 2])
        blockb = sb("blockb", [P, 4 * P], BF16)
        XA = sb("XA", [P, NT, 8, LD + 1])
        MXS = sb("MXS", [P, 2, 8])
        RS = sb("RS", [P, 2, 8])
        AV = sb("AV", [P, 2, 8, LD])

        consts_loaded, x_loaded, rows_loaded, cols_loaded = sem("consts_loaded"), sem("x_loaded"), sem("rows_loaded"), sem("cols_loaded")
        wb_loaded, wx_loaded, chan_loaded = sem("wb_loaded"), sem("wx_loaded"), sem("chan_loaded")
        wz_loaded, wo_loaded, h0_loaded = sem("wz_loaded"), sem("wo_loaded"), sem("h0_loaded")
        out_stored = sem("out_stored")
        dve_self, act_self, pool_self = sem("dve_self"), sem("act_self"), sem("pool_self")
        dve_tap = sem("dve_tap")
        half_ready = sem("half_ready")
        stats_ready, rstd_ready, xn_ready, xt_in_psum, xt_ready = (
            sem(n) for n in ("stats_ready", "rstd_ready", "xn_ready", "xt_in_psum", "xt_ready"))
        masks_ready = sem("masks_ready")
        bc_in_psum, bc_ready, bdt_in_psum, b_ready, dt_ready = (
            sem(n) for n in ("bc_in_psum", "bc_ready", "bdt_in_psum", "b_ready", "dt_ready"))
        gt_in_psum, gt_ready, softplus_step, da_ready, cum_in_psum, cum_ready, ea_ready = (
            sem(n) for n in ("gt_in_psum", "gt_ready", "softplus_step", "da_ready", "cum_in_psum", "cum_ready", "ea_ready"))
        group_ready, wo_ready = sem("group_ready"), sem("wo_ready")
        up_in_psum, xp_ready, conv_begun, conv_done, tanh_done, xc_ready, xc_in_psum, xtok_ready = (
            sem(n) for n in ("up_in_psum", "xp_ready", "conv_begun", "conv_done", "tanh_done",
                             "xc_ready", "xc_in_psum", "xtok_ready"))
        cumsum_in_psum, decay_ready, mix_ready, xs_ready, xd_ready = (
            sem(n) for n in ("cumsum_in_psum", "decay_ready", "mix_ready", "xs_ready", "xd_ready"))
        z_in_psum, y_in_psum, i_in_psum, s_in_psum = (
            sem(n) for n in ("z_in_psum", "y_in_psum", "i_in_psum", "s_in_psum"))
        ztanh_ready, zsilu_ready, y0_ready, y1_ready, h1_ready, y_ready, gated_ready = (
            sem(n) for n in ("ztanh_ready", "zsilu_ready", "y0_ready", "y1_ready", "h1_ready", "y_ready", "gated_ready"))
        g_in_psum, gtr_ready, o_in_psum, o_added, squares_ready, squares_added = (
            sem(n) for n in ("g_in_psum", "gtr_ready", "o_in_psum", "o_added", "squares_ready", "squares_added"))
        ss_ready, rms_ready = sem("ss_ready"), sem("rms_ready")
        layer_done = sem("layer_done")
        small_loaded, wg_loaded, bd_loaded = sem("small_loaded"), sem("wg_loaded"), sem("bd_loaded")
        wu_loaded = [sem("wu0_loaded"), sem("wu1_loaded")]
        wd_loaded = [sem("wd0_loaded"), sem("wd1_loaded")]
        hidden_in_psum, act_ready, gate_ready, down_in_psum, down_added = (
            sem(n) for n in ("hidden_in_psum", "act_ready", "gate_ready", "down_in_psum", "down_added"))
        hop_in_psum, hop_ready, logits_in_psum, logits_ready, weights_ready = (
            sem(n) for n in ("hop_in_psum", "hop_ready", "logits_in_psum", "logits_ready", "weights_ready"))
        scores_in_psum, scores_ready, bias_in_psum, bias_added = (
            sem(n) for n in ("scores_in_psum", "scores_ready", "bias_in_psum", "bias_added"))
        w3_loaded, wo3_loaded, t3_loaded, gate_loaded = sem("w3_loaded"), sem("wo3_loaded"), sem("t3_loaded"), sem("gate_loaded")
        gate_tanh, gate_set, kept_ready, shift_in_psum = sem("gate_tanh"), sem("gate_set"), sem("kept_ready"), sem("shift_in_psum")
        kv_in_psum, time_ready, kexp_ready, wkv_ready, states_ready, out3_in_psum = (
            sem(n) for n in ("kv_in_psum", "time_ready", "kexp_ready", "wkv_ready", "states_ready", "out3_in_psum"))
        w5_loaded, wo5_loaded, slope_loaded, permuted = sem("w5_loaded"), sem("wo5_loaded"), sem("slope_loaded"), sem("permuted")
        dec_begun, dec_exp, dec_ready = sem("dec_begun"), sem("dec_exp"), sem("dec_ready")
        xb_ready, qk_in_psum, qktanh_ready, qk_ready, vu_in_psum, vu_ready = (
            sem(n) for n in ("xb_ready", "qk_in_psum", "qktanh_ready", "qk_ready", "vu_in_psum", "vu_ready"))
        sc_in_psum, p_ready, oss_ready, oeps_ready, or_ready, uo_ready, uot_in_psum, uot_ready, out5_in_psum, x5_ready = (
            sem(n) for n in ("sc_in_psum", "p_ready", "oss_ready", "oeps_ready", "or_ready", "uo_ready", "uot_in_psum",
                             "uot_ready", "out5_in_psum", "x5_ready"))
        silu_ready, pair_ready, biased_ready, pv_done = sem("silu_ready"), sem("pair_ready"), sem("biased_ready"), sem("pv_done")
        max_ready, recip_ready, av_ready = sem("max_ready"), sem("recip_ready"), sem("av_ready")
        xb7_ready, xa_ready, s7_in_psum, s7_ready, e7_ready, et7_ready, av_in_psum, x7_ready = (
            sem(n) for n in ("xb7_ready", "xa_ready", "s7_in_psum", "s7_ready", "e7_ready", "et7_ready", "av_in_psum", "x7_ready"))

        block = ctx.enter_context(nc.Block())

        @block.sync
        def _(sp):
            sp.dma_start(K[:, :], consts).then_inc(consts_loaded, 16)
            sp.dma_start(X[:, :, :], x.rearrange("(t p) d -> p t d", p=P)).then_inc(x_loaded, 16)
            sp.dma_start(WB[:, :, :], wbcdt).then_inc(wb_loaded, 16)
            sp.dma_start(COL[:, :, :], cols).then_inc(cols_loaded, 16)
            sp.dma_start(ROW[:, :], rows[0:3 * NH].partition_broadcast(P)).then_inc(rows_loaded, 16)

            def load_conv(g):
                sp.dma_start(WX[:, :, :], wx[g]).then_inc(wx_loaded, 16)
                sp.dma_start(CH[:, :, :], chan[g]).then_inc(chan_loaded, 16)

            def load_heads(g):
                sp.dma_start(WZ[:, :, :], wz[g]).then_inc(wz_loaded, 16)
                sp.dma_start(WOr[:, :, :], wout[g]).then_inc(wo_loaded, 16)
                sp.dma_start(H0[:, :], h0[g]).then_inc(h0_loaded, 16)

            load_conv(0)
            load_heads(0)
            with sp.Fori(1, NG) as g:
                sp.wait_ge(xc_ready, g * GC)
                sp.wait_ge(wo_ready, g)
                load_conv(g)
                sp.wait_ge(o_added, g * NT)
                load_heads(g)
            sp.dma_start(SM[:, :, :], small).then_inc(small_loaded, 16)
            sp.dma_start(WG[:, :], wg6).then_inc(wg_loaded, 16)
            sp.dma_start(BD[:, :], bd6).then_inc(bd_loaded, 16)
            sp.dma_start(W3[:, :, :], w3).then_inc(w3_loaded, 16)
            sp.dma_start(WO3[:, :], wo3).then_inc(wo3_loaded, 16)
            sp.dma_start(T3[:, :], t3).then_inc(t3_loaded, 16)
            sp.dma_start(GATE[:, 0, :], rows[3 * NH:3 * NH + D].partition_broadcast(P)).then_inc(gate_loaded, 16)
            sp.dma_start(SLOPE[:, :], rows[3 * NH + D:3 * NH + D + LH].partition_broadcast(P)).then_inc(slope_loaded, 16)

            def load_experts(f, wu, wd):
                def up(e, slot):
                    sp.dma_start(WU[slot][:, 0:f.width], wu[e]).then_inc(wu_loaded[slot], 16)

                def down(e, slot):
                    sp.dma_start(WD[slot][:, :], wd[e]).then_inc(wd_loaded[slot], 16)

                if f.s0:
                    sp.wait_ge(down_in_psum, f.s0)
                    sp.wait_ge(act_ready, f.s0)
                for slot in range(2):
                    up(slot, slot)
                    down(slot, slot)
                with sp.Fori(0, f.pairs - 1) as i:
                    for slot in range(2):
                        sp.wait_ge(hidden_in_psum, f.s0 + 4 * i + 2 * slot + 2)
                        if not f.gated:
                            sp.wait_ge(act_ready, f.s0 + 4 * i + 2 * slot + 2)
                        up(2 * i + 2 + slot, slot)
                        sp.wait_ge(down_in_psum, f.s0 + 4 * i + 2 * slot + 2)
                        down(2 * i + 2 + slot, slot)

            load_experts(F2, wu2, wd2)
            load_experts(F4, wu2, wd2)
            sp.dma_start(W5, w5).then_inc(w5_loaded, 16)
            sp.dma_start(WO5, wo5).then_inc(wo5_loaded, 16)
            sp.wait_ge(layer_done, 4)
            for seg in range(4):
                for par in range(2):
                    r0 = 64 * (seg % 2) + par
                    sp.dma_start(OUT[32 * seg:32 * seg + 32, par::2, :],
                                 X[r0:r0 + 63:2, seg // 2::2, :]).then_inc(permuted, 16)
            load_experts(F6, wu6, wd6)
            load_experts(F8, wu6, wd6)
            sp.wait_ge(layer_done, 8)
            rows_of = out.rearrange("(b s j a) d -> b a (s j) d", b=NB, s=4, a=2)
            for t in range(NT):
                sp.dma_start(rows_of[t // 2, t % 2], X[:, t, :]).then_inc(out_stored, 16)
            sp.wait_ge(out_stored, 16 * NT)

        @block.gpsimd
        def _(pool):
            chain = Chain(pool, pool_self)

            def norm_scales(layer):
                for q in range(2):
                    s = slice(4 * q, 4 * q + 4)
                    pool.wait_ge(stats_ready, 2 * layer + q + 1)
                    chain.link(pool.tensor_scalar(rstd[:, s], mv[:, s, 1], LN_EPS, None, ALU.add))
                    ins = pool.tensor_tensor(rstd[:, s], rstd[:, s], half[:, s], op=ALU.pow)
                    if layer:
                        ins.then_inc(rstd_ready, 1)
                    else:
                        chain.link(ins)
                        chain.link(pool.tensor_tensor(rms[:, s], rstd[:, s], rstd[:, s], op=ALU.mult))
                        chain.link(pool.tensor_tensor(rms[:, s], rms[:, s], mv[:, s, 1], op=ALU.mult))
                        chain.link(pool.tensor_scalar(rms[:, s], rms[:, s], LN_EPS, None, ALU.add))
                        pool.tensor_tensor(rms[:, s], rms[:, s], half[:, s], op=ALU.pow).then_inc(rstd_ready, 1)

            chain.link(pool.memset(half[:, :], -0.5))
            pool.memset(tiny[:, :], 1e-6)
            pool.memset(XA[:, :, :, LD:LD + 1], 1.0)
            pool.memset(XN[:, :, D:], 0.0)
            pool.memset(ones[:, :], 1.0).then_inc(masks_ready, 1)
            norm_scales(0)

            pool.wait_ge(rows_loaded, 16)
            with pool.Fori(0, NG) as g:
                pool.wait_ge(chan_loaded, (g + 1) * 16)
                pool.wait_ge(wo_loaded, (g + 1) * 16)
                pool.tensor_tensor(WO[:, :, :], WOr[:, :, :],
                                   CH[:, :, 2 * TAPS:2 * TAPS + 1].to_broadcast([P, GC, D]), op=ALU.mult).then_inc(wo_ready, 1)
                pool.wait_ge(group_ready, g + 1)
                for c in range(NT):
                    xt = XTOK[:, c, :].rearrange("p (h d) -> p h d", h=GH)
                    if c == 0:
                        pool.wait_ge(xtok_ready, (g + 1) * GC)
                    if c >= 2:
                        pool.wait_ge(y0_ready, g * NT + c - 1)
                    pool.tensor_tensor(XD[:, c % 2, :].rearrange("p (h d) -> p h d", h=GH), xt,
                                       Dg[:, :].unsqueeze(2).to_broadcast([P, GH, HD]), op=ALU.mult).then_inc(xd_ready, 1)
                    if c % 2 == 0:
                        pool.wait_ge(decay_ready, g * NT + c + 1)
                        if c:
                            pool.wait_ge(s_in_psum, g * NB + c // 2)
                        pool.tensor_tensor(XS[:, :].rearrange("p (h d) -> p h d", h=GH), xt,
                                           E[:, c % 2, :, P - 1:P].to_broadcast([P, GH, HD]), op=ALU.mult).then_inc(xs_ready, 1)
                    pool.wait_ge(y0_ready, g * NT + c + 1)
                    pool.wait_ge(y1_ready, g * NT + c + 1)
                    pool.tensor_tensor(Y1[:, c % 2, :], Y0[:, c % 2, :], Y1[:, c % 2, :], op=ALU.add).then_inc(y_ready, 1)
                    pool.wait_ge(zsilu_ready, g * NT + c + 1)
                    pool.wait_ge(y_ready, g * NT + c + 1)
                    if c >= 2:
                        pool.wait_ge(g_in_psum, g * NT + c - 1)
                    pool.tensor_tensor(G[:, c % 2, :], Y1[:, c % 2, :], SZ[:, c % 2, :], op=ALU.mult).then_inc(gated_ready, 1)
            pool.wait_ge(ss_ready, 1)
            chain.link(pool.tensor_scalar(SS[:, :], SS[:, :], 1.0 / DI, LN_EPS, ALU.mult, ALU.add))
            pool.tensor_tensor(SS[:, :], SS[:, :], half[:, :], op=ALU.pow).then_inc(rms_ready, 1)

            norm_scales(1)
            norm_scales(2)
            pool.wait_ge(gate_set, 1)
            for t in range(NT):
                pool.wait_ge(xn_ready, NT * 2 + t + 1)
                pool.tensor_tensor(OUT[:, t, :], XN[:, t, 0:D], GATE[:, 1, :], op=ALU.mult).then_inc(kept_ready, 1)
            norm_scales(3)
            for f in range(4, 9):
                norm_scales(f)
                if f == 5:
                    with pool.Fori(0, NB) as b:
                        pool.wait_ge(oss_ready, b + 1)
                        pool.tensor_tensor(sso[:, :], sso[:, :], tiny[:, :], op=ALU.add).then_inc(oeps_ready, 1)
                        pool.wait_ge(oeps_ready, b + 1)
                        pool.tensor_tensor(sso[:, :], sso[:, :], half[:, 0:2], op=ALU.pow).then_inc(or_ready, 1)
                if f == 7:
                    heads = XN[:, :, 0:D].rearrange("p t (h a d) -> p t h a d", a=2, d=LD)
                    for t in range(NT):
                        pool.wait_ge(xn_ready, NT * 7 + t + 1)
                        pool.tensor_copy(XA[:, t, :, 0:LD], heads[:, t, :, t % 2, :]).then_inc(xa_ready, 1)

        @block.scalar
        def _(act):
            chain = Chain(act, act_self)

            def xt_out(layer, scale=None, bias=None):
                for q in range(NT // 2):
                    act.wait_ge(xt_in_psum, 4 * layer + q + 1)
                    for k in range(KD):
                        ins = act.activation(XT[:, k, q * 256:q * 256 + 256], PS[6 + q % 2][:, k * 256:k * 256 + 256],
                                             ACT.Identity, bias=bias(k) if bias else 0.0, scale=scale(k) if scale else 1.0)
                    ins.then_inc(xt_ready, 1)

            act.wait_ge(cols_loaded, 16)
            xt_out(0, scale=lambda k: COL[:, 0, k:k + 1])

            for n, to in enumerate((BT, BT, CT, CT)):
                act.wait_ge(bc_in_psum, n + 1)
                act.copy(to[:, (n % 2) * 512:(n % 2) * 512 + 512], PS[n][:, :]).then_inc(bc_ready, 1)
            for q in range(2):
                act.wait_ge(gt_in_psum, q + 1)
                act.copy(GT[:, 4 * q:4 * q + 4, :].rearrange("p t s -> p (t s)"), PS[2 + q][:, :]).then_inc(gt_ready, 1)
            act.wait_ge(rows_loaded, 16)
            act.activation(eA[:, :], ROW[:, NH:2 * NH], ACT.Exp).then_inc(ea_ready, 1)
            act.wait_ge(softplus_step, 1)
            chain.link(act.activation(dta[:, :, :], dta[:, :, :], ACT.Exp, scale=-1.0))
            act.activation(dta[:, :, :], dta[:, :, :], ACT.Ln, bias=1.0).then_inc(softplus_step, 1)
            act.wait_ge(cum_in_psum, 2)
            act.activation(ncum[:, :, :].rearrange("p t h -> p (t h)"), PS[0][:, 0:NT * NH], ACT.Copy, scale=-1.0).then_inc(cum_ready, 1)
            act.activation(ecum[:, :, :].rearrange("p t h -> p (t h)"), PS[0][:, 0:NT * NH], ACT.Exp).then_inc(cum_ready, 1)
            act.activation(eend[:, :, :].rearrange("p t h -> p (t h)"), PS[1][:, 0:NT * NH], ACT.Exp).then_inc(cum_ready, 1)

            with act.Fori(0, NG) as g:
                act.wait_ge(chan_loaded, (g + 1) * 16)

                def tokens_out(j):
                    for q in range(2):
                        act.wait_ge(xc_in_psum, g * 2 * GC + 2 * j + q + 1)
                        ins = act.activation(XTOK[:, 4 * q:4 * q + 4, j * P:j * P + P],
                                             PS[4 + q][:, :].rearrange("p (t c) -> p t c", t=4), ACT.Copy, scale=0.5)
                    ins.then_inc(xtok_ready, 1)

                for j in range(GC + 2):
                    if j < GC:
                        act.wait_ge(up_in_psum, g * GC + j + 1)
                        if j >= 2:
                            act.wait_ge(conv_done, g * GC + j - 1)
                        act.copy(XP[:, j % 2, :, 0:TAPS - 1],
                                 CH[:, j, TAPS + 1:2 * TAPS].unsqueeze(1).to_broadcast([P, NB, TAPS - 1]))
                        for q in range(2):
                            ins = act.copy(XP[:, j % 2, 2 * q:2 * q + 2, TAPS - 1:],
                                           PS[2 * (j % 2) + q][:, :].rearrange("p (b t) -> p b t", b=2))
                        ins.then_inc(xp_ready, 1)
                        act.wait_ge(xp_ready, g * GC + j + 1)
                        if j >= 2:
                            act.wait_ge(xc_ready, g * GC + j - 1)
                        act.activation(CV[:, j % 2, :, :], XP[:, j % 2, :, TAPS - 1:], ACT.Identity,
                                       scale=CH[:, j, TAPS - 1:TAPS], bias=CH[:, j, TAPS:TAPS + 1]).then_inc(conv_begun, 1)
                    if j >= 1 and j - 1 < GC:
                        act.wait_ge(conv_done, g * GC + j)
                        if j >= 3:
                            act.wait_ge(xc_in_psum, g * 2 * GC + 2 * (j - 2))
                        act.activation(TH[:, (j - 1) % 2, :, :], CV[:, (j - 1) % 2, :, :], ACT.Tanh, scale=0.5).then_inc(tanh_done, 1)
                    if j >= 2:
                        tokens_out(j - 2)

                act.wait_ge(group_ready, g + 1)

                def gated_out(c):
                    act.wait_ge(g_in_psum, g * NT + c + 1)
                    if c >= 2:
                        act.wait_ge(o_in_psum, g * NT + c - 1)
                    act.copy(GTR[:, c % 2, :], PS[6][:, :]).then_inc(gtr_ready, 1)

                for c in range(NT):
                    act.wait_ge(cumsum_in_psum, g * NT + c + 1)
                    if c >= 2:
                        act.wait_ge(mix_ready, g * NT + c - 1)
                        act.wait_ge(xs_ready, g * NB + c // 2)
                    for h in range(GH):
                        ins = act.activation(E[:, c % 2, h, :], PS[h // 4][:, (h % 4) * P:(h % 4) * P + P], ACT.Exp,
                                             bias=GRP[:, 1, c, h:h + 1])
                    ins.then_inc(decay_ready, 1)
                    act.wait_ge(z_in_psum, g * NT + c + 1)
                    if c >= 2:
                        act.wait_ge(gated_ready, g * NT + c - 1)
                    act.activation(SZ[:, c % 2, :], PS[4][:, :], ACT.Tanh, scale=0.5).then_inc(ztanh_ready, 1)
                    if c >= 1:
                        gated_out(c - 1)
                    act.wait_ge(y_ready, g * NT + c + 1)
                    act.activation(sqj[:, :], Y1[:, c % 2, :], ACT.Square, accum_out=SQ[:, c:c + 1]).then_inc(squares_ready, 1)
                gated_out(NT - 1)

            def experts(f):
                if not f.gated:
                    for q in range(2):
                        act.wait_ge(hop_in_psum, 2 * (f.n - 2) + q + 1)
                        act.activation(TT[:, q * 512:q * 512 + 512], PS[4 + q][0:8, :], ACT.Tanh).then_inc(hop_ready, 1)
                act.wait_ge(logits_ready, 2 * f.n + 1)
                act.activation(LR[:, :, 0:f.routed], LR[:, :, 0:f.routed], ACT.Exp).then_inc(logits_ready, 1)
                if not f.gated:
                    for q in range(2):
                        act.wait_ge(scores_in_psum, 2 * (f.n - 2) + q + 1)
                        act.copy(SCT[:, q * 512:q * 512 + 512], PS[6 + q][0:8, :]).then_inc(scores_ready, 1)

                def hidden(s, r):
                    act.wait_ge(hidden_in_psum, s + 1)
                    if s is not f.s0 and not (isinstance(s, int) and s < f.s0 + 2):
                        act.wait_ge(gate_ready, s - 1)
                    if f.gated:
                        act.activation(FT[:, r % 2, :], PS[2 * (r % 2)][:, :], ACT.Tanh, scale=0.5).then_inc(act_ready, 1)
                    else:
                        if not (isinstance(s, int) and s < f.s0 + 2):
                            act.wait_ge(down_in_psum, s - 1)
                        act.activation(FG[:, r % 2, :], PS[2 * (r % 2)][:, :], ACT.Identity,
                                       bias=WU[r // 2][:, 256:257]).then_inc(biased_ready, 1)
                        act.wait_ge(biased_ready, s - F6.s0 + 1)
                        act.activation(FT[:, r % 2, :], FG[:, r % 2, :], ACT.Tanh, scale=0.5).then_inc(act_ready, 1)

                hidden(f.s0, 0)
                hidden(f.s0 + 1, 1)
                with act.Fori(0, f.pairs - 1) as i:
                    for r in (2, 3, 4, 5):
                        hidden(f.s0 + 4 * i + r, r % 4)
                for r in (2, 3):
                    hidden(f.s0 + 4 * (f.pairs - 1) + r, r)

            xt_out(1)
            experts(F2)
            act.wait_ge(gate_loaded, 16)
            act.activation(GATE[:, 0, :], GATE[:, 0, :], ACT.Tanh, scale=0.5).then_inc(gate_tanh, 1)
            act.wait_ge(t3_loaded, 16)
            act.activation(T3[:, :], T3[:, :], ACT.Exp).then_inc(gate_tanh, 1)
            xt_out(2)
            xt_out(3, scale=lambda k: COL[:, 1, k:k + 1], bias=lambda k: COL[:, 2, k:k + 1])
            act.wait_ge(time_ready, 1)
            for q in range(2):
                s = slice(q * 512, q * 512 + 512)
                act.wait_ge(kv_in_psum, q + 1)
                act.activation(KS[:, s], PS[q][0:64, :], ACT.Tanh, scale=0.5).then_inc(kexp_ready, 1)
                act.wait_ge(kexp_ready, 2 * q + 1)
                act.activation(KS[:, s], KS[:, s], ACT.Exp, scale=T3[:, 1:2], bias=T3[:, 1:2]).then_inc(kexp_ready, 1)
            xt_out(4)
            experts(F4)
            act.wait_ge(dec_begun, 1)
            act.activation(DEC, DEC, ACT.Exp).then_inc(dec_exp, 1)
            xt_out(5)
            act.wait_ge(xt_ready, 4 * 6)
            with act.Fori(0, NB) as b:
                act.copy(XB, XT[:, :, bass.ds(b * D, D)]).then_inc(xb_ready, 1)
                for n in range(4):
                    act.wait_ge(qk_in_psum, 4 * b + n + 1)
                    act.activation((QT if n < 2 else KT)[:, 2 * (n % 2):2 * (n % 2) + 2, :],
                                   PS[n][:, :].rearrange("p (g t) -> p g t", g=2), ACT.Tanh, scale=0.5).then_inc(qktanh_ready, 1)
                for c in range(2):
                    act.wait_ge(vu_in_psum, 2 * b + c + 1)
                    act.copy(Y0[:, c, :], PS[4 + c][:, :]).then_inc(vu_ready, 1)
                act.wait_ge(pv_done, 4 * b + 4)
                for c in range(2):
                    ins = act.activation(sqj[:, c * D:c * D + D], PS[6][:, c * D:c * D + D], ACT.Square, scale=1.0 / 16, accum_out=sso[:, c:c + 1])
                ins.then_inc(oss_ready, 1)
                act.wait_ge(uot_in_psum, b + 1)
                act.copy(UOT, PS[7][:, :]).then_inc(uot_ready, 1)
            xt_out(6)
            experts(F6)
            xt_out(7)
            act.wait_ge(xt_ready, 4 * 8)
            with act.Fori(0, NB) as b:
                act.copy(XB, XT[:, :, bass.ds(b * D, D)]).then_inc(xb7_ready, 1)
                for c in range(2):
                    act.wait_ge(s7_ready, 2 * b + c + 1)
                    act.activation(E[:, c, :, :], E[:, c, :, :], ACT.Exp, scale=0.25).then_inc(e7_ready, 1)
            xt_out(8)
            experts(F8)

        @block.vector
        def _(dve):
            chain = Chain(dve, dve_self)

            def layer_norm(layer, src=X):
                for q in range(2):
                    for t in range(4 * q, 4 * q + 4):
                        ins = dve.bn_stats(bn[:, t, :], src[:, t, :])
                    chain.link(ins)
                    for t in range(4 * q, 4 * q + 4):
                        ins = dve.bn_aggr(mv[:, t, :], bn[:, t, :])
                    ins.then_inc(stats_ready, 1)
                for t in range(NT):
                    if t % 4 == 0:
                        dve.wait_ge(rstd_ready, 2 * layer + t // 4 + 1)
                    ins = dve.tensor_scalar(XN[:, t, 0:D], src[:, t, :], mv[:, t, 0:1], rstd[:, t:t + 1], ALU.subtract, ALU.mult)
                    if layer:
                        ins.then_inc(xn_ready, 1)
                    else:
                        chain.link(ins)
                        dve.tensor_tensor(X[:, t, :], X[:, t, :], XN[:, t, 0:D], op=ALU.add)
                        chain.link(dve.tensor_scalar(XN[:, t, 0:D], XN[:, t, 0:D], rms[:, t:t + 1], None, ALU.mult))
                        dve.sem_inc(xn_ready, 1)

            dve.wait_ge(consts_loaded, 16)
            dve.tensor_copy(identb[:, :], ident)
            for n in range(4):
                ins = dve.tensor_scalar(causalb[:, n * P:n * P + P], tri, 1.0, -NEG, ALU.subtract, ALU.mult)
            ins.then_inc(masks_ready, 1)
            dve.wait_ge(x_loaded, 16)
            layer_norm(0)

            for q in range(4):
                dve.wait_ge(bdt_in_psum, q + 1)
                b = PS[4 + q][:, :].rearrange("p (t n) -> p t n", t=2)
                dve.tensor_copy(BN[:, q, :], b[:, 0, 0:NS]).then_inc(b_ready, 1)
                if q == 0:
                    dve.wait_ge(rows_loaded, 16)
                ins = dve.tensor_tensor(dtr[:, 2 * q:2 * q + 2, :], b[:, :, NS:NS + NH],
                                        ROW[:, 0:NH].unsqueeze(1).to_broadcast([P, 2, NH]), op=ALU.add)
            chain.link(ins)
            chain.link(dve.scalar_tensor_tensor(dta[:, :, :], dtr[:, :, :], -1.0, dtr[:, :, :], ALU.mult, ALU.max))
            dve.sem_inc(softplus_step, 1)
            dve.wait_ge(softplus_step, 2)
            chain.link(dve.scalar_tensor_tensor(dtr[:, :, :], dtr[:, :, :], 0.0, dta[:, :, :], ALU.max, ALU.add))
            dve.wait_ge(ea_ready, 1)
            dve.scalar_tensor_tensor(dA[:, :, :], dtr[:, :, :], -1.0, eA[:, :].unsqueeze(1).to_broadcast([P, NT, NH]),
                                     ALU.mult, ALU.mult).then_inc(da_ready, 1)
            dve.memset(OUT[:, :, :], 0.0)
            chain.link(dve.memset(SS[:, :], 0.0))
            dve.wait_ge(da_ready, 1)
            dve.wait_ge(cum_ready, 3)

            with dve.Fori(0, NG) as g:
                dve.tensor_copy(Dg[:, :], ROW[:, bass.ds(2 * NH + g * GH, GH)])
                for n, src in enumerate((dA, ncum, ecum, eend)):
                    ins = dve.tensor_copy(GRP[:, n, :, :], src[:, :, bass.ds(g * GH, GH)])
                ins.then_inc(group_ready, 1)
                dve.wait_ge(group_ready, g + 1)
                for j in range(GC):
                    dve.wait_ge(conv_begun, g * GC + j + 1)
                    for tap in range(TAPS - 1):
                        if tap:
                            dve.wait_ge(dve_tap, g * GC * (TAPS - 2) + j * (TAPS - 2) + tap)
                        ins = dve.scalar_tensor_tensor(CV[:, j % 2, :, :], XP[:, j % 2, :, tap:tap + D], CH[:, j, tap:tap + 1],
                                                       CV[:, j % 2, :, :], ALU.mult, ALU.add)
                        ins.then_inc(conv_done if tap == TAPS - 2 else dve_tap, 1)
                    dve.wait_ge(tanh_done, g * GC + j + 1)
                    dve.scalar_tensor_tensor(TH[:, j % 2, :, :], TH[:, j % 2, :, :], 1.0, CV[:, j % 2, :, :],
                                             ALU.add, ALU.mult).then_inc(xc_ready, 1)

                def add_out(c):
                    dve.wait_ge(o_in_psum, g * NT + c + 1)
                    dve.tensor_tensor(OUT[:, c, :], PS[7][:, 0:D], OUT[:, c, :], op=ALU.add).then_inc(o_added, 1)

                dve.wait_ge(h0_loaded, (g + 1) * 16)
                for c in range(NT):
                    n = g * NT + c
                    dve.wait_ge(ztanh_ready, n + 1)
                    dve.scalar_tensor_tensor(SZ[:, c % 2, :], SZ[:, c % 2, :], 1.0, PS[4][:, :],
                                             ALU.add, ALU.mult).then_inc(zsilu_ready, 1)
                    dve.wait_ge(decay_ready, n + 1)
                    if c >= 2:
                        dve.wait_ge(y_in_psum, n - 1)
                    dve.tensor_tensor(M[:, c % 2, :, :], E[:, c % 2, :, :],
                                      GT[:, c, :].unsqueeze(1).to_broadcast([P, GH, P]), op=ALU.mult).then_inc(mix_ready, 1)
                    if c % 2 == 0:
                        if c:
                            dve.wait_ge(i_in_psum, n)
                        dve.tensor_tensor(H1[:, :].rearrange("p (h d) -> p h d", h=GH), H0[:, :].rearrange("p (h d) -> p h d", h=GH),
                                          GRP[:, 3, c, :].unsqueeze(2).to_broadcast([P, GH, HD]), op=ALU.mult)
                    if c >= 1:
                        add_out(c - 1)
                    dve.wait_ge(y_in_psum, n + 1)
                    dve.wait_ge(xd_ready, n + 1)
                    if c >= 2:
                        dve.wait_ge(y_ready, n - 1)
                    dve.tensor_tensor(Y0[:, c % 2, :], PS[2][:, :], XD[:, c % 2, :], op=ALU.add).then_inc(y0_ready, 1)
                    if c % 2 == 0:
                        dve.wait_ge(s_in_psum, g * NB + c // 2 + 1)
                        dve.wait_ge(y0_ready, n + 1)
                        dve.tensor_tensor(H1[:, :], PS[5][:, :], H1[:, :], op=ALU.add).then_inc(h1_ready, 1)
                    dve.wait_ge(i_in_psum, n + 1)
                    if c >= 2:
                        dve.wait_ge(squares_ready, n - 1)
                        dve.wait_ge(gated_ready, n - 1)
                    dve.tensor_tensor(Y1[:, c % 2, :].rearrange("p (h d) -> p h d", h=GH), PS[3][:, :].rearrange("p (h d) -> p h d", h=GH),
                                      GRP[:, 2, c, :].unsqueeze(2).to_broadcast([P, GH, HD]), op=ALU.mult).then_inc(y1_ready, 1)
                add_out(NT - 1)
                dve.wait_ge(squares_ready, (g + 1) * NT)
                dve.tensor_tensor(SS[:, :], SQ[:, :], SS[:, :], op=ALU.add).then_inc(squares_added, 1)
                dve.wait_ge(squares_added, g + 1)
            dve.sem_inc(ss_ready, 1)
            dve.wait_ge(rms_ready, 1)
            chain.link(dve.tensor_scalar(SS[:, :], SS[:, :], 0.5, None, ALU.mult))
            for t in range(NT):
                ins = dve.scalar_tensor_tensor(X[:, t, :], OUT[:, t, :], SS[:, t:t + 1], X[:, t, :], ALU.mult, ALU.add)
            ins.then_inc(layer_done, 1)

            def route(f):
                n, w, k = f.routed, f.routed + 8 - f.top, f.top
                chain.link(dve.memset(LG[:, :, n:w], TINY))
                dve.wait_ge(logits_in_psum, f.n + 1)
                chain.link(dve.tensor_copy(LG[:, :, 0:n], PS[4][:, 0:NT * n].rearrange("p (t e) -> p t e", t=NT)))
                for t in range(NT):
                    ins = dve.max(MX[:, t, :], LG[:, t, 0:n])
                chain.link(ins)
                dve.tensor_tensor(LR[:, :, 0:n], LG[:, :, 0:n], MX[:, :, 0:1].to_broadcast([P, NT, n]),
                                  op=ALU.subtract).then_inc(logits_ready, 1)
                chain.link(dve.memset(MX[:, :, k:8], TINY))
                for t in range(NT):
                    ins = dve.match_replace(LG[:, t, 0:w], MX[:, t, :], LG[:, t, 0:w], TAKEN)
                chain.link(ins)
                chain.link(dve.tensor_scalar(LG[:, :, 0:n], LG[:, :, 0:n], TAKEN, None, ALU.is_equal))
                dve.wait_ge(logits_ready, 2 * f.n + 2)
                chain.link(dve.tensor_tensor(LR[:, :, 0:n], LR[:, :, 0:n], LG[:, :, 0:n], op=ALU.mult))
                chain.link(dve.tensor_reduce(SUM[:, :], LR[:, :, 0:n], AX.X, ALU.add))
                chain.link(dve.reciprocal(SUM[:, :], SUM[:, :]))
                ins = dve.tensor_tensor(LR[:, :, 0:n], LR[:, :, 0:n], SUM[:, :].unsqueeze(2).to_broadcast([P, NT, n]), op=ALU.mult)
                if not f.gated:
                    ins.then_inc(weights_ready, 1)
                    dve.wait_ge(weights_ready, f.n - 1)
                else:
                    chain.link(ins)
                share = k / (k + 1) if f.shared else 1.0
                ins = dve.tensor_scalar(CW[:, 0:n, :], LR[:, :, 0:n].rearrange("p t e -> p e t"), 0.5 * share, None, ALU.mult)
                if f.shared:
                    chain.link(ins)
                    ins = dve.memset(CW[:, n:n + f.shared, :], 0.5 / (k + 1))
                chain.link(ins)

            def experts(f):
                route(f)
                if not f.gated:
                    for q in range(4):
                        dve.wait_ge(bias_in_psum, 4 * (f.n - 2) + q + 1)
                        ins = dve.tensor_tensor(X[:, 2 * q:2 * q + 2, :].rearrange("p t d -> p (t d)"), PS[4 + q % 2][:, :],
                                                X[:, 2 * q:2 * q + 2, :].rearrange("p t d -> p (t d)"), op=ALU.add)
                        ins.then_inc(bias_added, 1)
                    dve.wait_ge(bias_added, 4 * (f.n - 1))

                def gate(s, r):
                    dve.wait_ge(act_ready, s + 1)
                    if not (isinstance(s, int) and s < f.s0 + 2):
                        dve.wait_ge(down_in_psum, s - 1)
                    if f.gated:
                        dve.scalar_tensor_tensor(FT[:, r % 2, :], FT[:, r % 2, :], 1.0, PS[2 * (r % 2)][:, :],
                                                 ALU.add, ALU.mult).then_inc(silu_ready, 1)
                        dve.wait_ge(silu_ready, s + 1)
                        dve.tensor_tensor(FG[:, r % 2, :], PS[2 * (r % 2) + 1][:, :], FT[:, r % 2, :], op=ALU.mult).then_inc(gate_ready, 1)
                    else:
                        dve.scalar_tensor_tensor(FG[:, r % 2, :], FT[:, r % 2, :], 1.0, FG[:, r % 2, :],
                                                 ALU.add, ALU.mult).then_inc(gate_ready, 1)

                def add(s, r):
                    dve.wait_ge(down_in_psum, s + 1)
                    if not (isinstance(s, int) and s < f.s0 + 2):
                        dve.wait_ge(down_added, s - 1)
                    for t in range(4):
                        tile = 4 * (r % 2) + t
                        ins = dve.scalar_tensor_tensor(X[:, tile, :], PS[4 + 2 * (r % 2) + t // 2][:, (t % 2) * D:(t % 2) * D + D],
                                                       CWP[:, r // 2, tile:tile + 1], X[:, tile, :], ALU.mult, ALU.add)
                    ins.then_inc(down_added, 1)

                def pair_weights(i):
                    dve.tensor_copy(CWP[:, :, :], CW[:, bass.ds(2 * i, 2), :]).then_inc(pair_ready, 1)
                    dve.wait_ge(pair_ready, f.p0 + i + 1)

                gate(f.s0, 0)
                gate(f.s0 + 1, 1)
                pair_weights(0)
                add(f.s0, 0)
                gate(f.s0 + 2, 2)
                add(f.s0 + 1, 1)
                gate(f.s0 + 3, 3)
                add(f.s0 + 2, 2)
                with dve.Fori(1, f.pairs) as i:
                    s = f.s0 + 4 * i
                    gate(s, 0)
                    add(s - 1, 3)
                    dve.wait_ge(down_added, s)
                    pair_weights(i)
                    for r in range(1, 4):
                        gate(s + r, r)
                        add(s + r - 1, r - 1)
                add(f.s0 + 4 * f.pairs - 1, 3)
                dve.wait_ge(down_added, f.s0 + 4 * f.pairs)
                dve.sem_inc(layer_done, 1)

            dve.wait_ge(layer_done, 1)
            layer_norm(1)
            experts(F2)
            dve.wait_ge(gate_tanh, 2)
            chain.link(dve.tensor_scalar(GATE[:, 0, :], GATE[:, 0, :], 0.5, 0.5, ALU.mult, ALU.add))
            dve.tensor_scalar(GATE[:, 1, :], GATE[:, 0, :], -1.0, 1.0, ALU.mult, ALU.add).then_inc(gate_set, 1)
            dve.tensor_scalar(T3[:, 1:2], T3[:, 1:2], -0.5, None, ALU.mult).then_inc(time_ready, 1)
            layer_norm(2)
            for q in range(4):
                dve.wait_ge(shift_in_psum, q + 1)
                if q == 0:
                    dve.wait_ge(gate_set, 1)
                dve.wait_ge(kept_ready, 2 * q + 2)
                chain.link(dve.tensor_tensor(SZ[:, q % 2, :].rearrange("p (t d) -> p t d", t=2), PS[q][:, :].rearrange("p (t d) -> p t d", t=2),
                                             GATE[:, 0, :].unsqueeze(1).to_broadcast([P, 2, D]), op=ALU.mult))
                ins = dve.tensor_tensor(OUT[:, 2 * q:2 * q + 2, :].rearrange("p t d -> p (t d)"), SZ[:, q % 2, :],
                                        OUT[:, 2 * q:2 * q + 2, :].rearrange("p t d -> p (t d)"), op=ALU.add)
            chain.link(ins)
            layer_norm(3, OUT)
            for q in range(2):
                s = slice(q * 512, q * 512 + 512)
                dve.wait_ge(kexp_ready, 2 * q + 2)
                ins = dve.tensor_tensor(WKV[:, s], PS[2 + q][0:64, :], KS[:, s], op=ALU.mult)
                chain.link(ins)
                for b in range(2 * q, 2 * q + 2):
                    dve.tensor_tensor_scan(ST[:, b * D:b * D + D], T3[:, 0:1].to_broadcast([64, D]), WKV[:, b * D:b * D + D],
                                           0.0, ALU.mult, ALU.add).then_inc(states_ready, 1)
            for q in range(4):
                dve.wait_ge(out3_in_psum, q + 1)
                ins = dve.tensor_tensor(X[:, 2 * q:2 * q + 2, :].rearrange("p t d -> p (t d)"), PS[4 + q][:, :],
                                        X[:, 2 * q:2 * q + 2, :].rearrange("p t d -> p (t d)"), op=ALU.add)
            ins.then_inc(layer_done, 1)
            dve.wait_ge(layer_done, 3)
            layer_norm(4)
            experts(F4)
            dve.wait_ge(slope_loaded, 16)
            chain.link(dve.tensor_scalar(SLOPE[:, :], SLOPE[:, :], -1.0, None, ALU.mult))
            chain.link(dve.tensor_scalar(DMASK[:, :], dist, 0.0, NEG, ALU.is_lt, ALU.mult))
            for h in range(LH):
                ins = dve.scalar_tensor_tensor(DEC[:, h, :], dist, SLOPE[:, h:h + 1], DMASK[:, :], ALU.mult, ALU.add)
            ins.then_inc(dec_begun, 1)
            dve.wait_ge(dec_exp, 1)
            dve.tensor_scalar(DEC, DEC, 0.25, None, ALU.mult).then_inc(dec_ready, 1)
            dve.wait_ge(layer_done, 4)
            layer_norm(5)
            dve.wait_ge(permuted, 16 * 8)
            dve.wait_ge(dec_ready, 1)
            with dve.Fori(0, NB) as b:
                for n in range(4):
                    dve.wait_ge(qktanh_ready, 4 * b + n + 1)
                    v = (QT if n < 2 else KT)[:, 2 * (n % 2):2 * (n % 2) + 2, :]
                    dve.scalar_tensor_tensor(v, v, 1.0, PS[n][:, :].rearrange("p (g t) -> p g t", g=2),
                                             ALU.add, ALU.mult).then_inc(qk_ready, 1)
                for g in range(4):
                    dve.wait_ge(sc_in_psum, 4 * b + g + 1)
                    if g >= 2:
                        dve.wait_ge(pv_done, 4 * b + g - 1)
                    p0 = M[:, g % 2, :, :].rearrange("p (h a) t -> p h (a t)", h=4)
                    dve.tensor_tensor(p0, BANKS[:, 0:4, 0:D], DEC[:, 4 * g:4 * g + 4, :], op=ALU.mult)
                    dve.tensor_tensor(SZ[:, g % 2, :].rearrange("p (h t) -> p h t", h=4), BANKS[:, 0:4, D:D + P],
                                      DEC[:, 4 * g:4 * g + 4, 0:P], op=ALU.mult).then_inc(p_ready, 1)
                dve.wait_ge(or_ready, b + 1)
                dve.wait_ge(pv_done, 4 * b + 4)
                for c in range(2):
                    ins = dve.scalar_tensor_tensor(UO[:, c * D:c * D + D], PS[6][:, c * D:c * D + D], sso[:, c:c + 1],
                                                   Y0[:, c, D:2 * D], ALU.mult, ALU.mult)
                ins.then_inc(uo_ready, 1)
                dve.wait_ge(out5_in_psum, b + 1)
                dve.tensor_tensor(X[:, bass.ds(2 * b, 2), :], PS[4][:, :].rearrange("p (t d) -> p t d", t=2),
                                  OUT[:, bass.ds(2 * b, 2), :], op=ALU.add).then_inc(x5_ready, 1)
            dve.wait_ge(x5_ready, NB)
            dve.sem_inc(layer_done, 1)
            layer_norm(6)
            experts(F6)
            dve.tensor_scalar(blockb[:, 0:P], blk, 1.0, -NEG, ALU.subtract, ALU.mult)
            for n in range(1, 4):
                ins = dve.tensor_scalar(blockb[:, n * P:n * P + P], blk, 1.0, -NEG, ALU.subtract, ALU.mult)
            ins.then_inc(masks_ready, 1)
            layer_norm(7)
            heads = X[:, :, :].rearrange("p t (h a d) -> p t h a d", a=2, d=LD)
            with dve.Fori(0, NB) as b:
                for c in range(2):
                    n = 2 * b + c
                    dve.wait_ge(s7_in_psum, n + 1)
                    sc = BANKS[:, 4 * c:4 * c + 4, 0:D].rearrange("p j (k t) -> p j k t", k=KD)
                    dve.tensor_reduce(MXS[:, c, :].rearrange("p (j k) -> p j k", k=KD), sc, AX.X, ALU.max).then_inc(max_ready, 1)
                    dve.wait_ge(max_ready, n + 1)
                    dve.tensor_tensor(E[:, c, :, :].rearrange("p (j k) t -> p j k t", k=KD), sc,
                                      MXS[:, c, :].rearrange("p (j k) -> p j k", k=KD).unsqueeze(3).to_broadcast([P, 4, KD, P]),
                                      op=ALU.subtract).then_inc(s7_ready, 1)
                for c in range(2):
                    n = 2 * b + c
                    dve.wait_ge(e7_ready, n + 1)
                    dve.transpose(M[:, c, :, :].rearrange("p h k -> p (h k)"), E[:, c, :, :].rearrange("p h k -> p (h k)")).then_inc(et7_ready, 1)
                for c in range(2):
                    n = 2 * b + c
                    dve.wait_ge(av_in_psum, n + 1)
                    av = PS[4 * c][:, D:D + 8 * (LD + 1)].rearrange("p (h d) -> p h d", h=8)
                    dve.reciprocal(RS[:, c, :], av[:, :, LD]).then_inc(recip_ready, 1)
                    dve.wait_ge(recip_ready, n + 1)
                    dve.tensor_tensor(AV[:, c, :, :], av[:, :, 0:LD], RS[:, c, :].unsqueeze(2).to_broadcast([P, 8, LD]),
                                      op=ALU.mult).then_inc(av_ready, 1)
                    dve.wait_ge(av_ready, n + 1)
                    xh = heads[:, bass.ds(n, 1), :, c, :].rearrange("p a h d -> p (a h) d")
                    ins = dve.tensor_tensor(xh, xh, AV[:, c, :, :], op=ALU.add)
                    ins.then_inc(x7_ready, 1)
            dve.wait_ge(x7_ready, NT)
            dve.sem_inc(layer_done, 1)
            layer_norm(8)
            experts(F8)

        @block.tensor
        def _(pe):
            def transpose_xn(layer, odd_from=0):
                for q in range(NT // 2):
                    if q >= 2:
                        pe.wait_ge(xt_ready, 4 * layer + q - 1)
                    for t in range(2 * q, 2 * q + 2):
                        pe.wait_ge(xn_ready, NT * layer + t + 1)
                        for k in range(KD):
                            ins = pe.transpose(PS[6 + q % 2][:, k * 256 + (t % 2) * P:k * 256 + (t % 2) * P + P],
                                               XN[:, t, k * P + (t % 2) * odd_from:k * P + (t % 2) * odd_from + P], ident)
                    ins.then_inc(xt_in_psum, 1)

            pe.wait_ge(consts_loaded, 16)
            transpose_xn(0)
            pe.wait_ge(xt_ready, 4)
            pe.wait_ge(wb_loaded, 16)
            for n in range(4):
                for k in range(KD):
                    ins = pe.matmul(PS[n][:, :], WB[:, k, (n // 2) * (NS + NH):(n // 2) * (NS + NH) + NS],
                                    XT[:, k, (n % 2) * 512:(n % 2) * 512 + 512], start=k == 0, stop=k == KD - 1)
                ins.then_inc(bc_in_psum, 1)
            for q in range(4):
                for t in range(2 * q, 2 * q + 2):
                    for k in range(KD):
                        ins = pe.matmul(PS[4 + q][:, (t % 2) * 256:(t % 2) * 256 + NS + NH], XT[:, k, t * P:t * P + P],
                                        WB[:, k, 0:NS + NH], start=k == 0, stop=k == KD - 1)
                ins.then_inc(bdt_in_psum, 1)
            pe.wait_ge(bc_ready, 4)
            for q in range(2):
                for t in range(4 * q, 4 * q + 4):
                    ins = pe.matmul(PS[2 + q][:, (t % 4) * P:(t % 4) * P + P], BT[:, t * P:t * P + P],
                                    CT[:, t * P:t * P + P], start=True, stop=True)
                ins.then_inc(gt_in_psum, 1)
            pe.wait_ge(da_ready, 1)
            pe.wait_ge(masks_ready, 2)
            for n, lower in enumerate((tri, ones[:, :])):
                pe.matmul(PS[n][:, 0:NT * NH], lower, dA[:, :, :].rearrange("p t h -> p (t h)"),
                          start=True, stop=True).then_inc(cum_in_psum, 1)
            pe.wait_ge(gt_ready, 2)
            pe.wait_ge(b_ready, 4)
            pe.wait_ge(cum_ready, 3)

            with pe.Fori(0, NG) as g:
                def up(j):
                    if j >= 2:
                        pe.wait_ge(xp_ready, g * GC + j - 1)
                    for q in range(2):
                        for k in range(KD):
                            ins = pe.matmul(PS[2 * (j % 2) + q][:, :], WX[:, k, j * P:j * P + P],
                                            XT[:, k, q * 512:q * 512 + 512], start=k == 0, stop=k == KD - 1)
                    ins.then_inc(up_in_psum, 1)

                pe.wait_ge(wx_loaded, (g + 1) * 16)
                for j in range(GC + 1):
                    if j < GC:
                        up(j)
                    if j >= 1:
                        pe.wait_ge(xc_ready, g * GC + j)
                        if j >= 2:
                            pe.wait_ge(xtok_ready, g * GC + j - 1)
                        for q in range(2):
                            for t in range(4 * q, 4 * q + 4):
                                ins = pe.transpose(PS[4 + q][:, (t % 4) * P:(t % 4) * P + P],
                                                   TH[:, (j - 1) % 2, t // 2, (t % 2) * P:(t % 2) * P + P], ident)
                            ins.then_inc(xc_in_psum, 1)

                def cumulate(c):
                    if c:
                        pe.wait_ge(decay_ready, g * NT + c)
                    else:
                        pe.wait_ge(xp_ready, (g + 1) * GC)
                    for q in range(2):
                        pe.matmul(PS[q][:, :], identb[:, :], causalb[:, :], start=True, stop=False, skip_group_check=True)
                        for h in range(4 * q, 4 * q + 4):
                            ins = pe.matmul(PS[q][:, (h % 4) * P:(h % 4) * P + P], GRP[:, 0, c, h:h + 1].to_broadcast([P, P]),
                                            tri, start=False, stop=h % 4 == 3, skip_group_check=True)
                    ins.then_inc(cumsum_in_psum, 1)

                def project_out(c):
                    pe.wait_ge(gated_ready, g * NT + c + 1)
                    if c:
                        pe.wait_ge(gtr_ready, g * NT + c)
                    for k in range(GC):
                        ins = pe.transpose(PS[6][:, k * P:k * P + P], G[:, c % 2, k * P:k * P + P], ident)
                    ins.then_inc(g_in_psum, 1)
                    pe.wait_ge(gtr_ready, g * NT + c + 1)
                    if c:
                        pe.wait_ge(o_added, g * NT + c)
                    for k in range(GC):
                        ins = pe.matmul(PS[7][:, 0:D], GTR[:, c % 2, k * P:k * P + P], WO[:, k, :], start=k == 0, stop=k == GC - 1)
                    ins.then_inc(o_in_psum, 1)

                pe.wait_ge(group_ready, g + 1)
                cumulate(0)
                pe.wait_ge(xtok_ready, (g + 1) * GC)
                pe.wait_ge(wz_loaded, (g + 1) * 16)
                pe.wait_ge(h0_loaded, (g + 1) * 16)
                for c in range(NT):
                    n = g * NT + c
                    if c:
                        pe.wait_ge(zsilu_ready, n)
                    for k in range(KD):
                        ins = pe.matmul(PS[4][:, :], XT[:, k, c * P:c * P + P], WZ[:, k, :], start=k == 0, stop=k == KD - 1)
                    ins.then_inc(z_in_psum, 1)
                    if c == 1:
                        pe.wait_ge(wo_ready, g + 1)
                    if c:
                        project_out(c - 1)
                    pe.wait_ge(mix_ready, n + 1)
                    if c:
                        pe.wait_ge(y0_ready, n)
                    for h in range(GH):
                        ins = pe.matmul(PS[2][:, h * HD:h * HD + HD], M[:, c % 2, h, :], XTOK[:, c, h * HD:h * HD + HD],
                                        start=True, stop=True)
                    ins.then_inc(y_in_psum, 1)
                    if c % 2 == 0:
                        pe.wait_ge(xs_ready, g * NB + c // 2 + 1)
                        if c:
                            pe.wait_ge(h1_ready, g * NB + c // 2)
                        pe.matmul(PS[5][:, :], BN[:, c // 2, :], XS[:, :], start=True, stop=True).then_inc(s_in_psum, 1)
                    else:
                        pe.wait_ge(h1_ready, g * NB + c // 2 + 1)
                    if c:
                        pe.wait_ge(y1_ready, n)
                    pe.matmul(PS[3][:, :], CT[:, c * P:c * P + P], (H1 if c % 2 else H0)[:, :], start=True, stop=True).then_inc(i_in_psum, 1)
                    if c < NT - 1:
                        cumulate(c + 1)
                project_out(NT - 1)

            def experts(f):
                pe.wait_ge(xt_ready, 4 * (f.norm + 1))
                if f.n == 0:
                    pe.wait_ge(small_loaded, 16)
                if f.gated:
                    logits = [(XT[:, k, t * P:t * P + P], SM[:, k, 0:16]) for t in range(NT) for k in range(KD)]
                else:
                    if f.n == 2:
                        pe.wait_ge(wg_loaded, 16)
                        pe.wait_ge(bd_loaded, 16)
                    for q in range(2):
                        for k in range(KD):
                            ins = pe.matmul(PS[4 + q][0:8, :], SM[:, k, 16:24], XT[:, k, q * 512:q * 512 + 512], start=k == 0, stop=k == KD - 1)
                        ins.then_inc(hop_in_psum, 1)
                    pe.wait_ge(hop_ready, 2 * (f.n - 1))
                    logits = [(TT[:, t * P:t * P + P], WG[:, :]) for t in range(NT)]
                m = f.routed
                per = len(logits) // NT
                for n, (l, r) in enumerate(logits):
                    ins = pe.matmul(PS[4][:, n // per * m:n // per * m + m], l, r, start=n % per == 0, stop=n % per == per - 1)
                ins.then_inc(logits_in_psum, 1)

                def up(s, r, pair):
                    pe.wait_ge(wu_loaded[r // 2], 16 * (pair + 1))
                    if not (isinstance(s, int) and s < f.s0 + 2):
                        pe.wait_ge(gate_ready, s - 1)
                    for w in range(2 if f.gated else 1):
                        for k in range(KD):
                            ins = pe.matmul(PS[2 * (r % 2) + w][:, :], WU[r // 2][:, (2 * w + k) * P:(2 * w + k) * P + P],
                                            XT[:, k, (r % 2) * 512:(r % 2) * 512 + 512], start=k == 0, stop=k == KD - 1)
                    ins.then_inc(hidden_in_psum, 1)

                def down(s, r, pair):
                    pe.wait_ge(wd_loaded[r // 2], 16 * (pair + 1))
                    pe.wait_ge(gate_ready, s + 1)
                    if not (isinstance(s, int) and s < f.s0 + 2):
                        pe.wait_ge(down_added, s - 1)
                    for t in range(4):
                        ins = pe.matmul(PS[4 + 2 * (r % 2) + t // 2][:, (t % 2) * D:(t % 2) * D + D], FG[:, r % 2, t * P:t * P + P],
                                        WD[r // 2][:, :], start=True, stop=True)
                    ins.then_inc(down_in_psum, 1)

                if not f.gated:
                    pe.wait_ge(weights_ready, f.n - 1)
                    for t in range(NT):
                        ins = pe.transpose(PS[6 + t // 4][0:8, (t % 4) * P:(t % 4) * P + P], LR[:, t, 0:8], ident)
                        if t % 4 == 3:
                            ins.then_inc(scores_in_psum, 1)
                    pe.wait_ge(scores_ready, 2 * (f.n - 1))
                    for q in range(4):
                        if q >= 2:
                            pe.wait_ge(bias_added, 4 * (f.n - 2) + q - 1)
                        for t in range(2 * q, 2 * q + 2):
                            ins = pe.matmul(PS[4 + q % 2][:, (t % 2) * D:(t % 2) * D + D], SCT[:, t * P:t * P + P], BD[:, :], start=True, stop=True)
                        ins.then_inc(bias_in_psum, 1)
                    pe.wait_ge(bias_added, 4 * (f.n - 1))

                up(f.s0, 0, f.p0)
                for r in range(3):
                    up(f.s0 + r + 1, r + 1, f.p0)
                    down(f.s0 + r, r, f.p0)
                with pe.Fori(1, f.pairs) as i:
                    s, pair = f.s0 + 4 * i, f.p0 + i
                    up(s, 0, pair)
                    down(s - 1, 3, pair - 1)
                    for r in range(3):
                        up(s + r + 1, r + 1, pair)
                        down(s + r, r, pair)
                down(f.s0 + 4 * f.pairs - 1, 3, f.p0 + f.pairs - 1)

            transpose_xn(1)
            experts(F2)
            transpose_xn(2)
            pe.wait_ge(xt_ready, 4 * 3)
            pe.wait_ge(w3_loaded, 16)
            for q in range(4):
                for t in range(2 * q, 2 * q + 2):
                    for k in range(KD):
                        ins = pe.matmul(PS[q][:, (t % 2) * D:(t % 2) * D + D], XT[:, k, (t ^ 1) * P:(t ^ 1) * P + P],
                                        W3[:, k, 0:D], start=k == 0, stop=k == KD - 1)
                ins.then_inc(shift_in_psum, 1)
            transpose_xn(3)
            pe.wait_ge(xt_ready, 4 * 4)
            for q in range(2):
                for n in range(2):
                    for k in range(KD):
                        ins = pe.matmul(PS[2 * n + q][0:64, :], W3[:, k, D + 64 * n:D + 64 * n + 64],
                                        XT[:, k, q * 512:q * 512 + 512], start=k == 0, stop=k == KD - 1)
                ins.then_inc(kv_in_psum, 1)
            pe.wait_ge(wo3_loaded, 16)
            for q in range(4):
                pe.wait_ge(states_ready, q + 1)
                for t in range(2 * q, 2 * q + 2):
                    ins = pe.matmul(PS[4 + q][:, (t % 2) * D:(t % 2) * D + D], ST[:, t * P:t * P + P], WO3[:, :], start=True, stop=True)
                ins.then_inc(out3_in_psum, 1)
            transpose_xn(4)
            experts(F4)
            transpose_xn(5)
            pe.wait_ge(w5_loaded, 16)
            pe.wait_ge(wo5_loaded, 16)
            with pe.Fori(0, NB) as b:
                pe.wait_ge(xb_ready, b + 1)
                for n in range(4):
                    for g in range(2 * n, 2 * n + 2):
                        for k in range(KD):
                            ins = pe.matmul(PS[n][:, (g % 2) * D:(g % 2) * D + D], W5[:, k, g * P:g * P + P], XB[:, k, :],
                                            start=k == 0, stop=k == KD - 1)
                    ins.then_inc(qk_in_psum, 1)
                for c in range(2):
                    for k in range(KD):
                        ins = pe.matmul(PS[4 + c][:, :], XB[:, k, c * P:c * P + P], W5[:, k, 2 * LQ:], start=k == 0, stop=k == KD - 1)
                    ins.then_inc(vu_in_psum, 1)
                pe.wait_ge(qk_ready, 4 * b + 4)
                pe.wait_ge(vu_ready, 2 * b + 2)

                def values(g):
                    pe.wait_ge(p_ready, 4 * b + g + 1)
                    p0 = M[:, g % 2, :, :].rearrange("p (h a) t -> p h (a t)", h=4)
                    for j in range(4):
                        h = 4 * g + j
                        v = slice(h * LD, h * LD + LD)
                        pe.matmul(PS[6][:, h * LD:h * LD + LD], p0[:, j, 0:P], Y0[:, 0, v], start=True, stop=True)
                        o1 = PS[6][:, D + h * LD:D + h * LD + LD]
                        pe.matmul(o1, p0[:, j, P:2 * P], Y0[:, 0, v], start=True, stop=False)
                        ins = pe.matmul(o1, SZ[:, g % 2, j * P:j * P + P], Y0[:, 1, v], start=False, stop=True)
                    ins.then_inc(pv_done, 1)

                for g in range(4):
                    if g:
                        pe.wait_ge(p_ready, 4 * b + g)
                    for j in range(4):
                        rows_ = slice(32 * j, 32 * j + LD)
                        pe.matmul(PS[j][:, 0:D], KT[rows_, g, 0:P], QT[rows_, g, :], start=True, stop=True)
                        ins = pe.matmul(PS[j][:, D:D + P], KT[rows_, g, P:2 * P], QT[rows_, g, P:2 * P], start=True, stop=True)
                    ins.then_inc(sc_in_psum, 1)
                    if g:
                        values(g - 1)
                values(3)
                pe.wait_ge(uo_ready, b + 1)
                for k in range(KD):
                    for c in range(2):
                        ins = pe.transpose(PS[7][:, k * D + c * P:k * D + c * P + P], UO[:, c * D + k * P:c * D + k * P + P], ident)
                ins.then_inc(uot_in_psum, 1)
                pe.wait_ge(uot_ready, b + 1)
                uot = UOT.rearrange("p (k t a) -> p k t a", k=KD, a=2)
                for par in range(2):
                    for k in range(KD):
                        ins = pe.matmul(PS[4][:, par * D:par * D + D], uot[:, k, :, par], WO5[:, k, :], start=k == 0, stop=k == KD - 1)
                ins.then_inc(out5_in_psum, 1)
                pe.wait_ge(x5_ready, b + 1)
            transpose_xn(6)
            experts(F6)
            transpose_xn(7, odd_from=LD)
            pe.wait_ge(masks_ready, 3)
            pe.wait_ge(xa_ready, NT)
            with pe.Fori(0, NB) as b:
                pe.wait_ge(xb7_ready, b + 1)
                for c in range(2):
                    if c == 0:
                        pe.wait_ge(av_ready, 2 * b)
                    for j in range(4):
                        pe.matmul(PS[4 * c + j][:, 0:D], identb[:, :], blockb[:, 0:D], start=True, stop=False, skip_group_check=True)
                    for j in range(4):
                        for k in range(KD):
                            g = XB[32 * j:32 * j + LD, k, c * P:c * P + P]
                            ins = pe.matmul(PS[4 * c + j][:, k * P:k * P + P], g, g, start=False, stop=k == KD - 1, skip_group_check=True)
                    ins.then_inc(s7_in_psum, 1)
                for c in range(2):
                    pe.wait_ge(et7_ready, 2 * b + c + 1)
                    for h in range(8):
                        ins = pe.matmul(PS[4 * c][:, D + h * (LD + 1):D + (h + 1) * (LD + 1)], M[:, c, 2 * (h % 4) + h // 4, :],
                                        XA[:, bass.ds(2 * b + c, 1), h, :].rearrange("p a d -> p (a d)"), start=True, stop=True)
                    ins.then_inc(av_in_psum, 1)
            transpose_xn(8)
            experts(F8)


def kernel(**inputs):
    import numpy as np
    import concourse.bacc as bacc
    from concourse.bass_utils import run_bass_kernel_spmd

    a = {n: np.asarray(v) for n, v in inputs.items()}
    t = lambda m: np.ascontiguousarray(m.T)

    def blocks(m):
        return np.ascontiguousarray(m.reshape(KD, P, -1).transpose(1, 0, 2))

    def groups(m):
        return np.ascontiguousarray(m.reshape(KD, P, NG, GW).transpose(2, 1, 0, 3))

    win = t(a["L0_attn_a_in_proj_w"])
    idx = np.arange(P)
    consts = np.concatenate([
        np.eye(P), idx[:, None] <= idx[None, :], np.arange(2 * P)[None, :] - idx[:, None],
        idx[:, None] // 32 == idx[None, :] // 32], axis=1).astype(np.float32)
    b, c, dt = win[:, 2 * DI:2 * DI + NS], win[:, 2 * DI + NS:2 * DI + 2 * NS], win[:, 2 * DI + 2 * NS:]
    chan = np.concatenate([a["L0_attn_a_conv_w"], a["L0_attn_a_conv_b"][:, None], a["L0_attn_a_conv_state"][0],
                           a["L0_attn_a_inner_norm_w"][:, None]], axis=1)
    def rows_of(w):
        return w.reshape(-1, KD, P, P).transpose(0, 2, 1, 3).reshape(-1, P, KD * P)

    def experts_up(routed, shared):
        return np.concatenate([rows_of(a[routed]), rows_of(a[shared].reshape(D, 4, P).transpose(1, 0, 2))])

    qkvu = t(a["L1_attn_a_W_qkvu"])
    w5 = np.zeros((D, 2 * LQ + 512), qkvu.dtype)
    w5[:, 0:2 * LQ].reshape(D, 2 * LH, 32)[:, :, 0:LD] = qkvu[:, 0:512].reshape(D, 2 * LH, LD)
    w5[:, 2 * LQ:] = qkvu[:, 512:]
    col = lambda v: v.reshape(KD, P).T
    arrays = {
        "x": a["L0_attn_a_x"].reshape(T, D),
        "consts": consts,
        "rows": np.concatenate([a["L0_attn_a_dt_bias"], a["L0_attn_a_A_log"], a["L0_attn_a_D_param"], a["L0_attn_b_gate"],
                                a["L1_attn_a_slope_rate"].reshape(-1)]),
        "cols": np.stack([col(a["L0_attn_a_norm_w"]), col(a["L0_attn_b_ln_gamma"]), col(a["L0_attn_b_ln_beta"])], axis=1),
        "wx": groups(win[:, DI:2 * DI]),
        "wz": groups(win[:, 0:DI]),
        "wbcdt": blocks(np.concatenate([b, dt, c], axis=1)),
        "wout": t(a["L0_attn_a_out_proj_w"]).reshape(NG, GC, P, D).transpose(0, 2, 1, 3),
        "chan": chan.reshape(NG, GC, P, NPC).transpose(0, 2, 1, 3),
        "h0": a["L0_attn_a_ssm_state"][0].reshape(NG, GH, NS, HD).transpose(0, 2, 1, 3).reshape(NG, NS, GW),
        "small": np.concatenate([blocks(a["L0_ffn_w_router"]), blocks(t(a["L1_ffn_Wg1"]))], axis=2),
        "w3": np.concatenate([blocks(t(a[f"L0_attn_b_W_{n}"])) for n in ("shift", "key", "value")], axis=2),
        "wo3": t(a["L0_attn_b_W_output"]),
        "t3": np.stack([a["L0_attn_b_time_decay"], a["L0_attn_b_time_first"]], axis=1),
        "wu2": np.concatenate([experts_up("L0_ffn_we1", "L0_ffn_ws1"), experts_up("L0_ffn_we3", "L0_ffn_ws3")], axis=2),
        "wd2": np.concatenate([a["L0_ffn_we2"], a["L0_ffn_ws2"].reshape(4, P, D)]),
        "wu6": np.concatenate([rows_of(a["L1_ffn_Wup"].transpose(0, 2, 1)), a["L1_ffn_bup"][:, :, None]], axis=2),
        "wd6": a["L1_ffn_Wdown"].transpose(0, 2, 1),
        "wg6": t(a["L1_ffn_Wg2"]),
        "bd6": a["L1_ffn_bdown"],
        "w5": blocks(w5),
        "wo5": blocks(t(a["L1_attn_a_W_out"])),
    }
    nc = bacc.Bacc("TRN2", target_bir_lowering=False, num_devices=1)
    arrays = {f"in_{n}": np.ascontiguousarray(v) for n, v in arrays.items()}
    args = {n[3:]: nc.dram_tensor(n, v.shape, mybir.dt.from_np(v.dtype), kind="ExternalInput").ap() for n, v in arrays.items()}
    out = nc.dram_tensor("out_x", (T, D), FP32, kind="ExternalOutput").ap()
    mixer_program(nc, out=out, **args)
    r = run_bass_kernel_spmd(nc, [arrays], core_ids=[0])
    return r.results[0]["out_x"].reshape(4, 256, 256)
```

```python
from contextlib import ExitStack

import concourse.bass as bass
from concourse import mybir

FP32 = mybir.dt.float32
BF16 = mybir.dt.bfloat16
ALU = mybir.AluOpType
ACT = mybir.ActivationFunctionType
AX = mybir.AxisListType

P = 128
D = 256
KD = D // P
T = 1024
NT = T // P
NB = 4
LN_EPS = 1e-5
NEG = -1e30

DI = 3072
NH = 48
HD = 64
NS = 128
GH = 8
NG = NH // GH
GW = GH * HD
GC = GW // P
TAPS = 4
NPC = TAPS + 1 + (TAPS - 1)


LH = 16
LD = 16
LQ = LH * 32
TINY = -3e38
TAKEN = 3e38


class Experts:

    def __init__(self, n, gated, routed, shared, top, norm, before):
        self.n, self.gated, self.routed, self.shared, self.top, self.norm = n, gated, routed, shared, top, norm
        self.count = routed + shared
        self.pairs = self.count // 2
        self.s0 = before.s0 + 4 * before.pairs if before else 0
        self.p0 = before.p0 + before.pairs if before else 0
        self.width = 256 * (2 if gated else 1) + (0 if gated else 1)


F2 = Experts(0, True, 16, 4, 4, 1, None)
F4 = Experts(1, True, 16, 4, 4, 4, F2)
F6 = Experts(2, False, 8, 0, 2, 6, F4)
F8 = Experts(3, False, 8, 0, 2, 8, F6)


class Chain:

    def __init__(self, eng, sem):
        self.eng, self.sem, self.base, self.n = eng, sem, 0, 0

    def link(self, ins):
        self.n += 1
        ins.then_inc(self.sem, 1)
        self.eng.wait_ge(self.sem, self.base + self.n)

    def enter(self, i, per):
        self.start, self.per = self.n, per
        self.base, self.n = i * per + self.n, 0

    def leave(self, times):
        assert self.n == self.per, self.n
        self.base, self.n = 0, self.start + self.per * times


def mixer_program(nc, x, consts, rows, cols, wx, wz, wbcdt, wout, chan, inw, h0, small, w3, wo3, t3,
                  wu2, wd2, wu6, wd6, wg6, bd6, w5, wo5, out):
    ctx = ExitStack()
    with ctx:
        def sb(name, shape, dt=FP32):
            return ctx.enter_context(nc.sbuf_tensor(name, shape, dt))

        def sem(name):
            return ctx.enter_context(nc.semaphore(name))

        BANKS = ctx.enter_context(nc.psum_tensor("BANKS", [P, 8, 512], FP32))
        PS = [BANKS[:, n, :] for n in range(8)]

        X = sb("X", [P, NT, D])
        XN = sb("XN", [P, NT, D + 16])
        XT = sb("XT", [P, KD, T])
        K = sb("K", [P, 640])
        ident, tri, dist, blk = K[:, 0:128], K[:, 128:256], K[:, 256:512], K[:, 512:640]
        CMASK = sb("CMASK", [P, P])
        identb = sb("identb", [P, P], BF16)
        ROW = sb("ROW", [P, 3 * NH])
        COL = sb("COL", [P, 3, KD])
        bn = sb("bn", [P, NT, 6])
        mv = sb("mv", [P, NT, 2])
        rstd = sb("rstd", [P, NT])
        rms = sb("rms", [P, NT])
        half = sb("half", [P, NT])

        WB = sb("WB", [P, KD, 2 * NS + NH])
        CT = sb("CT", [P, T])
        BN = sb("BN", [P, NB, NS])
        GT = sb("GT", [P, NT, P])
        ones = sb("ones", [P, P])
        dA = sb("dA", [P, NT, NH])
        ncum = sb("ncum", [P, NT, NH])
        ecum = sb("ecum", [P, NT, NH])
        eend = sb("eend", [P, NT, NH])
        eA = sb("eA", [P, NH])
        GRP = sb("GRP", [P, 2, 3, NT, GH])
        Dg = sb("Dg", [P, 2, GH])
        WZ = sb("WZ", [P, 2, KD, GW])
        WO = sb("WO", [P, 2, GC, D])
        NW = sb("NW", [P, 2, GC])
        H0 = sb("H0", [P, 2, GW])
        XTOK = sb("XTOK", [P, 2, NT, GW])
        SQ = sb("SQ", [P, 2, NT])
        WX = sb("WX", [P, KD, GW])
        CH = sb("CH", [P, GC, NPC])
        XP = sb("XP", [P, 2, 2, D + TAPS - 1])
        CV = sb("CV", [P, 2, 2, D])
        TH = sb("TH", [P, 2, 2, D])
        RB = sb("RB", [P, 2, GH, P])
        E = sb("E", [P, 2, GH, P])
        M = sb("M", [P, 2, GH, P])
        SZ = sb("SZ", [P, 2, GW])
        Y0 = sb("Y0", [P, 2, GW])
        Y1 = sb("Y1", [P, 2, GW])
        G = sb("G", [P, 2, GW])
        XD = sb("XD", [P, 2, GW])
        GTR = sb("GTR", [P, 2, GW])
        XS = sb("XS", [P, GW])
        H1 = sb("H1", [P, GW])
        OUT = sb("OUT", [P, NT, D])
        SS = sb("SS", [P, NT])
        junk = sb("junk", [P, GW], BF16)
        BT = RB[:, :, :, :].rearrange("p a h t -> p (a h t)")
        dtr = XD[:, :, :].rearrange("p a n -> p (a n)")[:, 0:NT * NH].rearrange("p (t h) -> p t h", t=NT)
        dta = G[:, :, :].rearrange("p a n -> p (a n)")[:, 0:NT * NH].rearrange("p (t h) -> p t h", t=NT)
        CUMT = Y0[0:NH, :, :].rearrange("p a n -> p (a n)")

        SM = sb("SM", [P, KD, 24])
        WG = sb("WG", [8, 8])
        BD = sb("BD", [8, D])
        WU = [sb(f"WU{n}", [P, 512]) for n in range(2)]
        WD = [sb(f"WD{n}", [P, D]) for n in range(2)]
        FT = M[:, 0, :, :].rearrange("p (a h) t -> p a (h t)", a=2)
        FG = M[:, 1, :, :].rearrange("p (a h) t -> p a (h t)", a=2)
        LG = sb("LG", [P, NT, 20])
        LR = sb("LR", [P, NT, 20])
        MX = sb("MX", [P, NT, 8])
        SUM = sb("SUM", [P, NT])
        CW = sb("CW", [P, 20, NT])
        CWP = sb("CWP", [P, 2, NT])
        TT = SZ[0:8, :, :].rearrange("p a n -> p (a n)")
        SCT = TT
        W3 = sb("W3", [P, KD, D + P])
        WO3 = sb("WO3", [64, D])
        T3 = sb("T3", [64, 2])
        GATE = sb("GATE", [P, 2, D])
        KS, WKV, ST = BT[0:64, :], CT[0:64, :], GT[0:64, :, :].rearrange("p t s -> p (t s)")
        W5 = XTOK[:, 0, :, :].rearrange("p t n -> p (t n)")[:, 0:KD * (2 * LQ + 512)].rearrange("p (k n) -> p k n", k=KD)
        WO5 = XS[:, :].rearrange("p (k n) -> p k n", k=KD)
        DEC = XTOK[:, 1, :, :].rearrange("p t (a n) -> p (t a) n", a=2)
        DMASK = sb("DMASK", [P, 2 * P])
        SLOPE = sb("SLOPE", [P, LH])
        XB = XD[:, 0, :].rearrange("p (k t) -> p k t", k=KD)
        QT = E[:, 0, :, :].rearrange("p (g a) t -> p g (a t)", g=4)
        KT = E[:, 1, :, :].rearrange("p (g a) t -> p g (a t)", g=4)
        UO, UOT = Y1[:, 0, :], G[:, 0, :]
        sso = sb("sso", [P, 2])
        tiny = sb("tiny", [P, 2])
        blockb = sb("blockb", [P, 4 * P], BF16)
        XA = sb("XA", [P, NT, 8, LD + 1])
        MXS = sb("MXS", [P, 2, 8])
        RS = sb("RS", [P, 2, 8])
        AV = sb("AV", [P, 2, 8, LD])

        consts_loaded, x_loaded, rows_loaded, cols_loaded = sem("consts_loaded"), sem("x_loaded"), sem("rows_loaded"), sem("cols_loaded")
        wb_loaded, wx_loaded, chan_loaded = sem("wb_loaded"), sem("wx_loaded"), sem("chan_loaded")
        wz_loaded, wo_loaded, h0_loaded = sem("wz_loaded"), sem("wo_loaded"), sem("h0_loaded")
        out_stored = sem("out_stored")
        dve_self, act_self, pool_self = sem("dve_self"), sem("act_self"), sem("pool_self")
        half_ready = sem("half_ready")
        stats_ready, rstd_ready, xn_ready, xt_in_psum, xt_ready = (
            sem(n) for n in ("stats_ready", "rstd_ready", "xn_ready", "xt_in_psum", "xt_ready"))
        masks_ready = sem("masks_ready")
        bc_in_psum, bc_ready, bdt_in_psum, b_ready, dt_ready = (
            sem(n) for n in ("bc_in_psum", "bc_ready", "bdt_in_psum", "b_ready", "dt_ready"))
        gt_in_psum, gt_ready, softplus_step, da_ready, cum_in_psum, cum_ready, ea_ready = (
            sem(n) for n in ("gt_in_psum", "gt_ready", "softplus_step", "da_ready", "cum_in_psum", "cum_ready", "ea_ready"))
        group_ready, wo_ready = sem("group_ready"), sem("wo_ready")
        up_in_psum, xp_ready, conv_begun, conv_tap, conv_done, tanh_done, xc_ready, xc_in_psum, xtok_ready = (
            sem(n) for n in ("up_in_psum", "xp_ready", "conv_begun", "conv_tap", "conv_done", "tanh_done",
                             "xc_ready", "xc_in_psum", "xtok_ready"))
        cumt_in_psum, cumt_ready, cumt_stored, gt_masked = (
            sem(n) for n in ("cumt_in_psum", "cumt_ready", "cumt_stored", "gt_masked"))
        rb_loaded = [sem("rb0_loaded"), sem("rb1_loaded")]
        nw_loaded, masked = sem("nw_loaded"), sem("masked")
        decay_ready, mix_ready, xs_ready, xd_ready = (
            sem(n) for n in ("decay_ready", "mix_ready", "xs_ready", "xd_ready"))
        z_in_psum, y_in_psum, i_in_psum, s_in_psum = (
            sem(n) for n in ("z_in_psum", "y_in_psum", "i_in_psum", "s_in_psum"))
        ztanh_ready, zsilu_ready, y0_ready, y1_ready, h1_ready, y_ready, gated_ready = (
            sem(n) for n in ("ztanh_ready", "zsilu_ready", "y0_ready", "y1_ready", "h1_ready", "y_ready", "gated_ready"))
        g_in_psum, gtr_ready, o_in_psum, o_added, squares_ready, squares_added = (
            sem(n) for n in ("g_in_psum", "gtr_ready", "o_in_psum", "o_added", "squares_ready", "squares_added"))
        h1_begun = sem("h1_begun")
        ss_ready, rms_ready = sem("ss_ready"), sem("rms_ready")
        layer_done = sem("layer_done")
        small_loaded, wg_loaded, bd_loaded = sem("small_loaded"), sem("wg_loaded"), sem("bd_loaded")
        wu_loaded = [sem("wu0_loaded"), sem("wu1_loaded")]
        wd_loaded = [sem("wd0_loaded"), sem("wd1_loaded")]
        hidden_in_psum, act_ready, gate_ready, down_in_psum, down_added = (
            sem(n) for n in ("hidden_in_psum", "act_ready", "gate_ready", "down_in_psum", "down_added"))
        hop_in_psum, hop_ready, logits_in_psum, logits_ready, weights_ready = (
            sem(n) for n in ("hop_in_psum", "hop_ready", "logits_in_psum", "logits_ready", "weights_ready"))
        scores_in_psum, scores_ready, bias_in_psum, bias_added = (
            sem(n) for n in ("scores_in_psum", "scores_ready", "bias_in_psum", "bias_added"))
        w3_loaded, wo3_loaded, t3_loaded, gate_loaded = sem("w3_loaded"), sem("wo3_loaded"), sem("t3_loaded"), sem("gate_loaded")
        gate_tanh, gate_set, kept_ready, shift_in_psum = sem("gate_tanh"), sem("gate_set"), sem("kept_ready"), sem("shift_in_psum")
        kv_in_psum, time_ready, kexp_ready, wkv_ready, states_ready, out3_in_psum = (
            sem(n) for n in ("kv_in_psum", "time_ready", "kexp_ready", "wkv_ready", "states_ready", "out3_in_psum"))
        w5_loaded, wo5_loaded, slope_loaded, permuted = sem("w5_loaded"), sem("wo5_loaded"), sem("slope_loaded"), sem("permuted")
        dec_begun, dec_exp, dec_ready = sem("dec_begun"), sem("dec_exp"), sem("dec_ready")
        xb_ready, qk_in_psum, qktanh_ready, qk_ready, vu_in_psum, vu_ready = (
            sem(n) for n in ("xb_ready", "qk_in_psum", "qktanh_ready", "qk_ready", "vu_in_psum", "vu_ready"))
        sc_in_psum, p_ready, oss_ready, oeps_ready, or_ready, uo_ready, uot_in_psum, uot_ready, out5_in_psum, x5_ready = (
            sem(n) for n in ("sc_in_psum", "p_ready", "oss_ready", "oeps_ready", "or_ready", "uo_ready", "uot_in_psum",
                             "uot_ready", "out5_in_psum", "x5_ready"))
        silu_ready, pair_ready, biased_ready, pv_done = sem("silu_ready"), sem("pair_ready"), sem("biased_ready"), sem("pv_done")
        max_ready, recip_ready, av_ready = sem("max_ready"), sem("recip_ready"), sem("av_ready")
        xb7_ready, xa_ready, s7_in_psum, s7_ready, e7_ready, et7_ready, av_in_psum, x7_ready = (
            sem(n) for n in ("xb7_ready", "xa_ready", "s7_in_psum", "s7_ready", "e7_ready", "et7_ready", "av_in_psum", "x7_ready"))

        cum_rows = nc.dram_tensor("cum_rows", (NH, NT, P), FP32, kind="Internal").ap()

        def after(eng, sem, count):
            if not isinstance(count, int) or count > 0:
                eng.wait_ge(sem, count)

        def groups_of(eng, group):
            group(0, 0)
            with eng.Fori(0, (NG - 2) // 2) as i:
                group(2 * i + 1, 1)
                group(2 * i + 2, 0)
            group(NG - 1, 1)

        block = ctx.enter_context(nc.Block())

        @block.sync
        def _(sp):
            sp.dma_start(K[:, :], consts).then_inc(consts_loaded, 16)
            sp.dma_start(X[:, :, :], x.rearrange("(t p) d -> p t d", p=P)).then_inc(x_loaded, 16)
            sp.dma_start(WB[:, :, :], wbcdt).then_inc(wb_loaded, 16)
            sp.dma_start(COL[:, :, :], cols).then_inc(cols_loaded, 16)
            sp.dma_start(ROW[:, :], rows[0:3 * NH].partition_broadcast(P)).then_inc(rows_loaded, 16)

            def load_conv(g):
                sp.dma_start(WX[:, :, :], wx[g]).then_inc(wx_loaded, 16)
                sp.dma_start(CH[:, :, :], chan[g]).then_inc(chan_loaded, 16)

            def load_heads(g, slot):
                sp.dma_start(WZ[:, slot, :, :], wz[g]).then_inc(wz_loaded, 16)
                sp.dma_start(WO[:, slot, :, :], wout[g]).then_inc(wo_loaded, 16)
                sp.dma_start(NW[:, slot, :], inw[g]).then_inc(nw_loaded, 16)
                sp.dma_start(H0[:, slot, :], h0[g]).then_inc(h0_loaded, 16)

            def load_decays(g, c):
                src = cum_rows[bass.ds(g * GH, GH), c, :] if not isinstance(g, int) else cum_rows[g * GH:g * GH + GH, c, :]
                sp.dma_start(RB[:, c % 2, :, :], src.partition_broadcast(P)).then_inc(rb_loaded[c % 2], 16)

            load_conv(0)
            load_heads(0, 0)
            sp.wait_ge(cumt_ready, 2)
            sp.dma_start(cum_rows.rearrange("h t p -> h (t p)"), CUMT).then_inc(cumt_stored, 16)
            sp.wait_ge(cumt_stored, 16)
            sp.wait_ge(gt_in_psum, 2)
            load_decays(0, 0)
            load_decays(0, 1)

            def group(g, slot):
                last = isinstance(g, int) and g == NG - 1
                if not last:
                    sp.wait_ge(xc_ready, (g + 1) * NT)
                    load_conv(g + 1)
                for c in range(NT):
                    n = g * NT + c
                    if c == 2 and not last:
                        after(sp, o_added, n - 2)
                        load_heads(g + 1, 1 - slot)
                    sp.wait_ge(masked, n + 1)
                    if c < NT - 2:
                        load_decays(g, c + 2)
                    elif not last:
                        load_decays(g + 1, c + 2 - NT)

            groups_of(sp, group)
            sp.dma_start(SM[:, :, :], small).then_inc(small_loaded, 16)
            sp.dma_start(WG[:, :], wg6).then_inc(wg_loaded, 16)
            sp.dma_start(BD[:, :], bd6).then_inc(bd_loaded, 16)
            sp.dma_start(W3[:, :, :], w3).then_inc(w3_loaded, 16)
            sp.dma_start(WO3[:, :], wo3).then_inc(wo3_loaded, 16)
            sp.dma_start(T3[:, :], t3).then_inc(t3_loaded, 16)
            sp.dma_start(GATE[:, 0, :], rows[3 * NH:3 * NH + D].partition_broadcast(P)).then_inc(gate_loaded, 16)
            sp.dma_start(SLOPE[:, :], rows[3 * NH + D:3 * NH + D + LH].partition_broadcast(P)).then_inc(slope_loaded, 16)

            def load_experts(f, wu, wd):
                def up(e, slot):
                    sp.dma_start(WU[slot][:, 0:f.width], wu[e]).then_inc(wu_loaded[slot], 16)

                def down(e, slot):
                    sp.dma_start(WD[slot][:, :], wd[e]).then_inc(wd_loaded[slot], 16)

                if f.s0:
                    sp.wait_ge(down_in_psum, f.s0)
                    sp.wait_ge(act_ready, f.s0)
                for slot in range(2):
                    up(slot, slot)
                    down(slot, slot)
                with sp.Fori(0, f.pairs - 1) as i:
                    for slot in range(2):
                        sp.wait_ge(hidden_in_psum, f.s0 + 4 * i + 2 * slot + 2)
                        if not f.gated:
                            sp.wait_ge(act_ready, f.s0 + 4 * i + 2 * slot + 2)
                        up(2 * i + 2 + slot, slot)
                        sp.wait_ge(down_in_psum, f.s0 + 4 * i + 2 * slot + 2)
                        down(2 * i + 2 + slot, slot)

            load_experts(F2, wu2, wd2)
            load_experts(F4, wu2, wd2)
            sp.dma_start(W5, w5).then_inc(w5_loaded, 16)
            sp.dma_start(WO5, wo5).then_inc(wo5_loaded, 16)
            sp.wait_ge(layer_done, 4)
            for seg in range(4):
                for par in range(2):
                    r0 = 64 * (seg % 2) + par
                    sp.dma_start(OUT[32 * seg:32 * seg + 32, par::2, :],
                                 X[r0:r0 + 63:2, seg // 2::2, :]).then_inc(permuted, 16)
            load_experts(F6, wu6, wd6)
            load_experts(F8, wu6, wd6)
            sp.wait_ge(layer_done, 8)
            rows_of = out.rearrange("(b s j a) d -> b a (s j) d", b=NB, s=4, a=2)
            for t in range(NT):
                sp.dma_start(rows_of[t // 2, t % 2], X[:, t, :]).then_inc(out_stored, 16)
            sp.wait_ge(out_stored, 16 * NT)

        @block.gpsimd
        def _(pool):
            chain = Chain(pool, pool_self)

            def norm_scales(layer):
                for q in range(2):
                    s = slice(4 * q, 4 * q + 4)
                    pool.wait_ge(stats_ready, 2 * layer + q + 1)
                    chain.link(pool.tensor_scalar(rstd[:, s], mv[:, s, 1], LN_EPS, None, ALU.add))
                    ins = pool.tensor_tensor(rstd[:, s], rstd[:, s], half[:, s], op=ALU.pow)
                    if layer:
                        ins.then_inc(rstd_ready, 1)
                    else:
                        chain.link(ins)
                        chain.link(pool.tensor_tensor(rms[:, s], rstd[:, s], rstd[:, s], op=ALU.mult))
                        chain.link(pool.tensor_tensor(rms[:, s], rms[:, s], mv[:, s, 1], op=ALU.mult))
                        chain.link(pool.tensor_scalar(rms[:, s], rms[:, s], LN_EPS, None, ALU.add))
                        pool.tensor_tensor(rms[:, s], rms[:, s], half[:, s], op=ALU.pow).then_inc(rstd_ready, 1)

            chain.link(pool.memset(half[:, :], -0.5))
            pool.memset(tiny[:, :], 1e-6)
            pool.memset(XA[:, :, :, LD:LD + 1], 1.0)
            pool.memset(XN[:, :, D:], 0.0)
            pool.memset(ones[:, :], 1.0).then_inc(masks_ready, 1)
            norm_scales(0)

            def heads(ap):
                return ap.rearrange("p (h d) -> p h d", h=GH)

            def mask(n, c):
                pool.wait_ge(rb_loaded[c % 2], (n - c % 2) * 8 + 16)
                after(pool, mix_ready, n - 1)
                if c % 2 == 0:
                    after(pool, xs_ready, n // 2 if isinstance(n, int) else (n - c) // 2 + c // 2)
                pool.tensor_tensor(E[:, c % 2, :, :], RB[:, c % 2, :, :], CMASK[:, :].unsqueeze(1).to_broadcast([P, GH, P]),
                                   op=ALU.add).then_inc(masked, 1)

            def skip(n, c, slot):
                after(pool, y0_ready, n - 1)
                pool.tensor_tensor(heads(XD[:, c % 2, :]), heads(XTOK[:, slot, c, :]), Dg[:, slot, :].unsqueeze(2).to_broadcast([P, GH, HD]),
                                   op=ALU.mult).then_inc(xd_ready, 1)

            def to_end(g, c, slot):
                pool.wait_ge(decay_ready, g * NT + c + 1)
                after(pool, s_in_psum, g * NB + c // 2)
                pool.tensor_tensor(heads(XS[:, :]), heads(XTOK[:, slot, c, :]), E[:, c % 2, :, P - 1:P].to_broadcast([P, GH, HD]),
                                   op=ALU.mult).then_inc(xs_ready, 1)

            def gate(n, c):
                pool.wait_ge(y0_ready, n + 1)
                pool.wait_ge(y1_ready, n + 1)
                pool.tensor_tensor(Y1[:, c % 2, :], Y0[:, c % 2, :], Y1[:, c % 2, :], op=ALU.add).then_inc(y_ready, 1)
                pool.wait_ge(zsilu_ready, n + 1)
                pool.wait_ge(y_ready, n + 1)
                after(pool, g_in_psum, n - 1)
                pool.tensor_tensor(G[:, c % 2, :], Y1[:, c % 2, :], SZ[:, c % 2, :], op=ALU.mult).then_inc(gated_ready, 1)

            def norm_weights(g, slot):
                pool.wait_ge(wo_loaded, (g + 1) * 16)
                pool.wait_ge(nw_loaded, (g + 1) * 16)
                pool.tensor_tensor(WO[:, slot, :, :], WO[:, slot, :, :],
                                   NW[:, slot, :].unsqueeze(2).to_broadcast([P, GC, D]), op=ALU.mult).then_inc(wo_ready, 1)

            def group(g, slot):
                first, last = isinstance(g, int) and g == 0, isinstance(g, int) and g == NG - 1
                for c in range(NT):
                    n = g * NT + c
                    if c % 2 == 0:
                        to_end(g, c, slot)
                    if not (first and c == 0):
                        gate(n - 1, (c - 1) % NT)
                    if c == 4 and not last:
                        norm_weights(g + 1, 1 - slot)
                    if not (last and c == NT - 1):
                        mask(n + 1, (c + 1) % NT)
                        if c == NT - 1:
                            pool.wait_ge(group_ready, g + 2)
                            pool.wait_ge(xtok_ready, (g + 2) * NT)
                        skip(n + 1, (c + 1) % NT, slot if c < NT - 1 else 1 - slot)

            norm_weights(0, 0)
            pool.wait_ge(masks_ready, 2)
            mask(0, 0)
            pool.wait_ge(group_ready, 1)
            pool.wait_ge(xtok_ready, NT)
            skip(0, 0, 0)
            groups_of(pool, group)
            gate(NG * NT - 1, NT - 1)
            pool.wait_ge(ss_ready, 1)
            chain.link(pool.tensor_scalar(SS[:, :], SS[:, :], 1.0 / DI, LN_EPS, ALU.mult, ALU.add))
            pool.tensor_tensor(SS[:, :], SS[:, :], half[:, :], op=ALU.pow).then_inc(rms_ready, 1)

            norm_scales(1)
            norm_scales(2)
            pool.wait_ge(gate_set, 1)
            for t in range(NT):
                pool.wait_ge(xn_ready, NT * 2 + t + 1)
                pool.tensor_tensor(OUT[:, t, :], XN[:, t, 0:D], GATE[:, 1, :], op=ALU.mult).then_inc(kept_ready, 1)
            norm_scales(3)
            for f in range(4, 9):
                norm_scales(f)
                if f == 5:
                    with pool.Fori(0, NB) as b:
                        pool.wait_ge(oss_ready, b + 1)
                        pool.tensor_tensor(sso[:, :], sso[:, :], tiny[:, :], op=ALU.add).then_inc(oeps_ready, 1)
                        pool.wait_ge(oeps_ready, b + 1)
                        pool.tensor_tensor(sso[:, :], sso[:, :], half[:, 0:2], op=ALU.pow).then_inc(or_ready, 1)
                if f == 7:
                    heads = XN[:, :, 0:D].rearrange("p t (h a d) -> p t h a d", a=2, d=LD)
                    for t in range(NT):
                        pool.wait_ge(xn_ready, NT * 7 + t + 1)
                        pool.tensor_copy(XA[:, t, :, 0:LD], heads[:, t, :, t % 2, :]).then_inc(xa_ready, 1)

        @block.scalar
        def _(act):
            chain = Chain(act, act_self)

            def xt_out(layer, scale=None, bias=None):
                for q in range(NT // 2):
                    act.wait_ge(xt_in_psum, 4 * layer + q + 1)
                    for k in range(KD):
                        ins = act.activation(XT[:, k, q * 256:q * 256 + 256], PS[6 + q % 2][:, k * 256:k * 256 + 256],
                                             ACT.Identity, bias=bias(k) if bias else 0.0, scale=scale(k) if scale else 1.0)
                    ins.then_inc(xt_ready, 1)

            act.wait_ge(cols_loaded, 16)
            xt_out(0, scale=lambda k: COL[:, 0, k:k + 1])

            for n, to in enumerate((BT, BT, CT, CT)):
                act.wait_ge(bc_in_psum, n + 1)
                act.copy(to[:, (n % 2) * 512:(n % 2) * 512 + 512], PS[n]).then_inc(bc_ready, 1)
            for q in range(2):
                act.wait_ge(gt_in_psum, q + 1)
                act.copy(GT[:, 4 * q:4 * q + 4, :].rearrange("p t s -> p (t s)"), PS[2 + q]).then_inc(gt_ready, 1)
            act.wait_ge(rows_loaded, 16)
            act.activation(eA[:, :], ROW[:, NH:2 * NH], ACT.Exp).then_inc(ea_ready, 1)
            act.wait_ge(softplus_step, 1)
            chain.link(act.activation(dta[:, :, :], dta[:, :, :], ACT.Exp, scale=-1.0))
            act.activation(dta[:, :, :], dta[:, :, :], ACT.Ln, bias=1.0).then_inc(softplus_step, 1)
            act.wait_ge(cum_in_psum, 2)
            for q in range(2):
                act.wait_ge(cumt_in_psum, q + 1)
                act.copy(CUMT[:, q * 512:q * 512 + 512], PS[4 + q][0:NH, :]).then_inc(cumt_ready, 1)
            act.activation(ncum[:, :, :].rearrange("p t h -> p (t h)"), PS[0][:, 0:NT * NH], ACT.Copy, scale=-1.0).then_inc(cum_ready, 1)
            act.activation(ecum[:, :, :].rearrange("p t h -> p (t h)"), PS[0][:, 0:NT * NH], ACT.Exp).then_inc(cum_ready, 1)
            act.activation(eend[:, :, :].rearrange("p t h -> p (t h)"), PS[1][:, 0:NT * NH], ACT.Exp).then_inc(cum_ready, 1)

            def conv_in(m, u):
                if u == 0:
                    act.wait_ge(chan_loaded, m * 2 + 16)
                act.wait_ge(up_in_psum, m + 1)
                after(act, conv_done, m - 1)
                act.copy(XP[:, u % 2, :, 0:TAPS - 1], CH[:, u // 2, TAPS + 1:2 * TAPS].unsqueeze(1).to_broadcast([P, 2, TAPS - 1]))
                act.copy(XP[:, u % 2, :, TAPS - 1:], PS[0].rearrange("p (b t) -> p b t", b=2)).then_inc(xp_ready, 1)
                act.wait_ge(xp_ready, m + 1)
                after(act, xc_ready, m - 1)
                act.activation(CV[:, u % 2, :, :], XP[:, u % 2, :, TAPS - 1:], ACT.Identity,
                               scale=CH[:, u // 2, TAPS - 1:TAPS], bias=CH[:, u // 2, TAPS:TAPS + 1]).then_inc(conv_begun, 1)

            def conv_tanh(m, u):
                act.wait_ge(conv_done, m + 1)
                after(act, xc_in_psum, m - 1)
                act.activation(TH[:, u % 2, :, :], CV[:, u % 2, :, :], ACT.Tanh, scale=0.5).then_inc(tanh_done, 1)

            def tokens_out(m, u, slot):
                act.wait_ge(xc_in_psum, m + 1)
                act.activation(XTOK[:, slot, 4 * (u % 2):4 * (u % 2) + 4, (u // 2) * P:(u // 2) * P + P],
                               PS[1].rearrange("p (t c) -> p t c", t=4), ACT.Copy, scale=0.5).then_inc(xtok_ready, 1)

            for u in range(NT + 2):
                if u < NT:
                    conv_in(u, u)
                if 1 <= u <= NT:
                    conv_tanh(u - 1, u - 1)
                if u >= 2:
                    tokens_out(u - 2, u - 2, 0)

            def decay(n, c, slot):
                act.wait_ge(masked, n + 1)
                for h in range(GH):
                    ins = act.activation(E[:, c % 2, h, :], E[:, c % 2, h, :], ACT.Exp, bias=GRP[:, slot, 0, c, h:h + 1])
                ins.then_inc(decay_ready, 1)

            def gated_out(n, c):
                act.wait_ge(g_in_psum, n + 1)
                after(act, o_in_psum, n - 1)
                act.copy(GTR[:, c % 2, :], PS[6]).then_inc(gtr_ready, 1)

            def squares(n, c, slot):
                act.wait_ge(y_ready, n + 1)
                after(act, squares_ready, n)
                act.activation(junk[:, :], Y1[:, c % 2, :], ACT.Square, accum_out=SQ[:, slot, c:c + 1]).then_inc(squares_ready, 1)

            def group(g, slot):
                first, last = isinstance(g, int) and g == 0, isinstance(g, int) and g == NG - 1
                for c in range(NT):
                    n = g * NT + c
                    if first and c == 0:
                        act.wait_ge(group_ready, 1)
                        decay(0, 0, 0)
                    act.wait_ge(z_in_psum, n + 1)
                    after(act, gated_ready, n - 1)
                    act.activation(SZ[:, c % 2, :], PS[4], ACT.Tanh, scale=0.5).then_inc(ztanh_ready, 1)
                    if not last:
                        conv_in(n + NT, c)
                    if c and not last:
                        tokens_out(n + NT - 1, c - 1, 1 - slot)
                    if not (first and c == 0):
                        squares(n - 1, (c - 1) % NT, slot if c else 1 - slot)
                    if not (first and c == 0):
                        gated_out(n - 1, (c - 1) % NT)
                    if not last:
                        conv_tanh(n + NT, c)
                    if not (last and c == NT - 1):
                        if c == NT - 1:
                            act.wait_ge(group_ready, g + 2)
                        decay(n + 1, (c + 1) % NT, slot if c < NT - 1 else 1 - slot)
                if not last:
                    tokens_out(n + NT, NT - 1, 1 - slot)

            groups_of(act, group)
            n = NG * NT - 1
            gated_out(n, NT - 1)
            squares(n, NT - 1, 1)

            def experts(f):
                if not f.gated:
                    for q in range(2):
                        act.wait_ge(hop_in_psum, 2 * (f.n - 2) + q + 1)
                        act.activation(TT[:, q * 512:q * 512 + 512], PS[4 + q][0:8, :], ACT.Tanh).then_inc(hop_ready, 1)
                act.wait_ge(logits_ready, 2 * f.n + 1)
                act.activation(LR[:, :, 0:f.routed], LR[:, :, 0:f.routed], ACT.Exp).then_inc(logits_ready, 1)
                if not f.gated:
                    for q in range(2):
                        act.wait_ge(scores_in_psum, 2 * (f.n - 2) + q + 1)
                        act.copy(SCT[:, q * 512:q * 512 + 512], PS[6 + q][0:8, :]).then_inc(scores_ready, 1)

                def hidden(s, r):
                    act.wait_ge(hidden_in_psum, s + 1)
                    if s is not f.s0 and not (isinstance(s, int) and s < f.s0 + 2):
                        act.wait_ge(gate_ready, s - 1)
                    if f.gated:
                        act.activation(FT[:, r % 2, :], PS[2 * (r % 2)], ACT.Tanh, scale=0.5).then_inc(act_ready, 1)
                    else:
                        if not (isinstance(s, int) and s < f.s0 + 2):
                            act.wait_ge(down_in_psum, s - 1)
                        act.activation(FG[:, r % 2, :], PS[2 * (r % 2)], ACT.Identity,
                                       bias=WU[r // 2][:, 256:257]).then_inc(biased_ready, 1)
                        act.wait_ge(biased_ready, s - F6.s0 + 1)
                        act.activation(FT[:, r % 2, :], FG[:, r % 2, :], ACT.Tanh, scale=0.5).then_inc(act_ready, 1)

                hidden(f.s0, 0)
                hidden(f.s0 + 1, 1)
                with act.Fori(0, f.pairs - 1) as i:
                    for r in (2, 3, 4, 5):
                        hidden(f.s0 + 4 * i + r, r % 4)
                for r in (2, 3):
                    hidden(f.s0 + 4 * (f.pairs - 1) + r, r)

            xt_out(1)
            experts(F2)
            act.wait_ge(gate_loaded, 16)
            act.activation(GATE[:, 0, :], GATE[:, 0, :], ACT.Tanh, scale=0.5).then_inc(gate_tanh, 1)
            act.wait_ge(t3_loaded, 16)
            act.activation(T3[:, :], T3[:, :], ACT.Exp).then_inc(gate_tanh, 1)
            xt_out(2)
            xt_out(3, scale=lambda k: COL[:, 1, k:k + 1], bias=lambda k: COL[:, 2, k:k + 1])
            act.wait_ge(time_ready, 1)
            for q in range(2):
                s = slice(q * 512, q * 512 + 512)
                act.wait_ge(kv_in_psum, q + 1)
                act.activation(KS[:, s], PS[q][0:64, :], ACT.Tanh, scale=0.5).then_inc(kexp_ready, 1)
                act.wait_ge(kexp_ready, 2 * q + 1)
                act.activation(KS[:, s], KS[:, s], ACT.Exp, scale=T3[:, 1:2], bias=T3[:, 1:2]).then_inc(kexp_ready, 1)
            xt_out(4)
            experts(F4)
            act.wait_ge(dec_begun, 1)
            act.activation(DEC, DEC, ACT.Exp).then_inc(dec_exp, 1)
            xt_out(5)
            act.wait_ge(xt_ready, 4 * 6)
            with act.Fori(0, NB) as b:
                act.copy(XB, XT[:, :, bass.ds(b * D, D)]).then_inc(xb_ready, 1)
                for n in range(4):
                    act.wait_ge(qk_in_psum, 4 * b + n + 1)
                    act.activation((QT if n < 2 else KT)[:, 2 * (n % 2):2 * (n % 2) + 2, :],
                                   PS[n].rearrange("p (g t) -> p g t", g=2), ACT.Tanh, scale=0.5).then_inc(qktanh_ready, 1)
                for c in range(2):
                    act.wait_ge(vu_in_psum, 2 * b + c + 1)
                    act.copy(Y0[:, c, :], PS[4 + c]).then_inc(vu_ready, 1)
                act.wait_ge(pv_done, 4 * b + 4)
                for c in range(2):
                    ins = act.activation(junk[:, c * D:c * D + D], PS[6][:, c * D:c * D + D], ACT.Square, scale=1.0 / 16, accum_out=sso[:, c:c + 1])
                ins.then_inc(oss_ready, 1)
                act.wait_ge(uot_in_psum, b + 1)
                act.copy(UOT, PS[7]).then_inc(uot_ready, 1)
            xt_out(6)
            experts(F6)
            xt_out(7)
            act.wait_ge(xt_ready, 4 * 8)
            with act.Fori(0, NB) as b:
                act.copy(XB, XT[:, :, bass.ds(b * D, D)]).then_inc(xb7_ready, 1)
                for c in range(2):
                    act.wait_ge(s7_ready, 2 * b + c + 1)
                    act.activation(E[:, c, :, :], E[:, c, :, :], ACT.Exp, scale=0.25).then_inc(e7_ready, 1)
            xt_out(8)
            experts(F8)

        @block.vector
        def _(dve):
            chain = Chain(dve, dve_self)

            def layer_norm(layer, src=X):
                for q in range(2):
                    for t in range(4 * q, 4 * q + 4):
                        ins = dve.bn_stats(bn[:, t, :], src[:, t, :])
                    chain.link(ins)
                    for t in range(4 * q, 4 * q + 4):
                        ins = dve.bn_aggr(mv[:, t, :], bn[:, t, :])
                    ins.then_inc(stats_ready, 1)
                for t in range(NT):
                    if t % 4 == 0:
                        dve.wait_ge(rstd_ready, 2 * layer + t // 4 + 1)
                    ins = dve.tensor_scalar(XN[:, t, 0:D], src[:, t, :], mv[:, t, 0:1], rstd[:, t:t + 1], ALU.subtract, ALU.mult)
                    if layer:
                        ins.then_inc(xn_ready, 1)
                    else:
                        chain.link(ins)
                        dve.tensor_tensor(X[:, t, :], X[:, t, :], XN[:, t, 0:D], op=ALU.add)
                        chain.link(dve.tensor_scalar(XN[:, t, 0:D], XN[:, t, 0:D], rms[:, t:t + 1], None, ALU.mult))
                        dve.sem_inc(xn_ready, 1)

            dve.wait_ge(consts_loaded, 16)
            dve.tensor_copy(identb[:, :], ident)
            dve.tensor_scalar(CMASK[:, :], tri, 1.0, -NEG, ALU.subtract, ALU.mult).then_inc(masks_ready, 1)
            dve.wait_ge(x_loaded, 16)
            layer_norm(0)

            for q in range(4):
                dve.wait_ge(bdt_in_psum, q + 1)
                b = PS[4 + q].rearrange("p (t n) -> p t n", t=2)
                dve.tensor_copy(BN[:, q, :], b[:, 0, 0:NS]).then_inc(b_ready, 1)
                if q == 0:
                    dve.wait_ge(rows_loaded, 16)
                ins = dve.tensor_tensor(dtr[:, 2 * q:2 * q + 2, :], b[:, :, NS:NS + NH],
                                        ROW[:, 0:NH].unsqueeze(1).to_broadcast([P, 2, NH]), op=ALU.add)
            chain.link(ins)
            chain.link(dve.scalar_tensor_tensor(dta[:, :, :], dtr[:, :, :], -1.0, dtr[:, :, :], ALU.mult, ALU.max))
            dve.sem_inc(softplus_step, 1)
            dve.wait_ge(softplus_step, 2)
            chain.link(dve.scalar_tensor_tensor(dtr[:, :, :], dtr[:, :, :], 0.0, dta[:, :, :], ALU.max, ALU.add))
            dve.wait_ge(ea_ready, 1)
            dve.scalar_tensor_tensor(dA[:, :, :], dtr[:, :, :], -1.0, eA[:, :].unsqueeze(1).to_broadcast([P, NT, NH]),
                                     ALU.mult, ALU.mult).then_inc(da_ready, 1)
            dve.memset(OUT[:, :, :], 0.0)
            dve.wait_ge(gt_ready, 2)
            for q in range(2):
                chain.link(dve.tensor_tensor(GT[:, 4 * q:4 * q + 4, :], GT[:, 4 * q:4 * q + 4, :],
                                             tri.unsqueeze(1).to_broadcast([P, 4, P]), op=ALU.mult))
            chain.link(dve.memset(SS[:, :], 0.0))
            dve.wait_ge(da_ready, 1)
            dve.wait_ge(cum_ready, 3)

            def heads(ap):
                return ap.rearrange("p (h d) -> p h d", h=GH)

            def conv_taps(m, u):
                dve.wait_ge(conv_begun, m + 1)
                for tap in range(TAPS - 1):
                    if tap:
                        dve.wait_ge(conv_tap, (TAPS - 2) * m + tap)
                    dve.scalar_tensor_tensor(CV[:, u % 2, :, :], XP[:, u % 2, :, tap:tap + D], CH[:, u // 2, tap:tap + 1],
                                             CV[:, u % 2, :, :], ALU.mult, ALU.add).then_inc(conv_done if tap == TAPS - 2 else conv_tap, 1)

            def conv_silu(m, u):
                dve.wait_ge(tanh_done, m + 1)
                dve.scalar_tensor_tensor(TH[:, u % 2, :, :], TH[:, u % 2, :, :], 1.0, CV[:, u % 2, :, :],
                                         ALU.add, ALU.mult).then_inc(xc_ready, 1)

            def group_scalars(g, slot):
                at = bass.ds(g * GH, GH) if not isinstance(g, int) else slice(g * GH, g * GH + GH)
                row = bass.ds(g * GH + 2 * NH, GH) if not isinstance(g, int) else slice(2 * NH + g * GH, 2 * NH + g * GH + GH)
                dve.tensor_copy(Dg[:, slot, :], ROW[:, row])
                for k, src in enumerate((ncum, ecum, eend)):
                    ins = dve.tensor_copy(GRP[:, slot, k, :, :], src[:, :, at])
                ins.then_inc(group_ready, 1)
                dve.wait_ge(group_ready, g + 1)

            def add_out(n, c):
                dve.wait_ge(o_in_psum, n + 1)
                dve.tensor_tensor(OUT[:, c, :], PS[7][:, 0:D], OUT[:, c, :], op=ALU.add).then_inc(o_added, 1)

            def add_squares(g, slot):
                dve.wait_ge(squares_ready, (g + 1) * NT)
                dve.tensor_tensor(SS[:, :], SQ[:, slot, :], SS[:, :], op=ALU.add).then_inc(squares_added, 1)
                dve.wait_ge(squares_added, g + 1)

            def group(g, slot):
                first, last = isinstance(g, int) and g == 0, isinstance(g, int) and g == NG - 1
                dve.wait_ge(h0_loaded, (g + 1) * 16)
                for c in range(NT):
                    n = g * NT + c
                    dve.wait_ge(decay_ready, n + 1)
                    after(dve, y_in_psum, n - 1)
                    dve.tensor_tensor(M[:, c % 2, :, :], E[:, c % 2, :, :],
                                      GT[:, c, :].unsqueeze(1).to_broadcast([P, GH, P]), op=ALU.mult).then_inc(mix_ready, 1)
                    dve.wait_ge(ztanh_ready, n + 1)
                    dve.scalar_tensor_tensor(SZ[:, c % 2, :], SZ[:, c % 2, :], 1.0, PS[4],
                                             ALU.add, ALU.mult).then_inc(zsilu_ready, 1)
                    if not (first and c < 2):
                        add_out(n - 2, (c - 2) % NT)
                    if c % 2 == 0:
                        after(dve, i_in_psum, n)
                        dve.tensor_tensor(heads(H1[:, :]), heads(H0[:, slot, :]), GRP[:, slot, 2, c, :].unsqueeze(2).to_broadcast([P, GH, HD]),
                                          op=ALU.mult).then_inc(h1_begun, 1)
                    if not last:
                        conv_taps(n + NT, c)
                    if c == 2 and not first:
                        add_squares(g - 1, 1 - slot)
                    dve.wait_ge(y_in_psum, n + 1)
                    dve.wait_ge(xd_ready, n + 1)
                    after(dve, y_ready, n - 1)
                    dve.tensor_tensor(Y0[:, c % 2, :], PS[2], XD[:, c % 2, :], op=ALU.add).then_inc(y0_ready, 1)
                    if c % 2 == 0:
                        dve.wait_ge(s_in_psum, g * NB + c // 2 + 1)
                        dve.wait_ge(h1_begun, g * NB + c // 2 + 1)
                        dve.tensor_tensor(H1[:, :], PS[5], H1[:, :], op=ALU.add).then_inc(h1_ready, 1)
                    if c == NT - 2 and not last:
                        group_scalars(g + 1, 1 - slot)
                    if not last:
                        conv_silu(n + NT, c)
                    dve.wait_ge(i_in_psum, n + 1)
                    after(dve, squares_ready, n - 1)
                    after(dve, gated_ready, n - 1)
                    dve.tensor_tensor(heads(Y1[:, c % 2, :]), heads(PS[3]),
                                      GRP[:, slot, 1, c, :].unsqueeze(2).to_broadcast([P, GH, HD]), op=ALU.mult).then_inc(y1_ready, 1)

            group_scalars(0, 0)
            for u in range(NT + 1):
                if u < NT:
                    conv_taps(u, u)
                if u:
                    conv_silu(u - 1, u - 1)
            groups_of(dve, group)
            add_out(NG * NT - 2, NT - 2)
            add_out(NG * NT - 1, NT - 1)
            add_squares(NG - 1, 1)
            dve.sem_inc(ss_ready, 1)
            dve.wait_ge(rms_ready, 1)
            chain.link(dve.tensor_scalar(SS[:, :], SS[:, :], 0.5, None, ALU.mult))
            for t in range(NT):
                ins = dve.scalar_tensor_tensor(X[:, t, :], OUT[:, t, :], SS[:, t:t + 1], X[:, t, :], ALU.mult, ALU.add)
            ins.then_inc(layer_done, 1)

            def route(f):
                n, w, k = f.routed, f.routed + 8 - f.top, f.top
                chain.link(dve.memset(LG[:, :, n:w], TINY))
                dve.wait_ge(logits_in_psum, f.n + 1)
                chain.link(dve.tensor_copy(LG[:, :, 0:n], PS[4][:, 0:NT * n].rearrange("p (t e) -> p t e", t=NT)))
                for t in range(NT):
                    ins = dve.max(MX[:, t, :], LG[:, t, 0:n])
                chain.link(ins)
                dve.tensor_tensor(LR[:, :, 0:n], LG[:, :, 0:n], MX[:, :, 0:1].to_broadcast([P, NT, n]),
                                  op=ALU.subtract).then_inc(logits_ready, 1)
                chain.link(dve.memset(MX[:, :, k:8], TINY))
                for t in range(NT):
                    ins = dve.match_replace(LG[:, t, 0:w], MX[:, t, :], LG[:, t, 0:w], TAKEN)
                chain.link(ins)
                chain.link(dve.tensor_scalar(LG[:, :, 0:n], LG[:, :, 0:n], TAKEN, None, ALU.is_equal))
                dve.wait_ge(logits_ready, 2 * f.n + 2)
                chain.link(dve.tensor_tensor(LR[:, :, 0:n], LR[:, :, 0:n], LG[:, :, 0:n], op=ALU.mult))
                chain.link(dve.tensor_reduce(SUM[:, :], LR[:, :, 0:n], AX.X, ALU.add))
                chain.link(dve.reciprocal(SUM[:, :], SUM[:, :]))
                ins = dve.tensor_tensor(LR[:, :, 0:n], LR[:, :, 0:n], SUM[:, :].unsqueeze(2).to_broadcast([P, NT, n]), op=ALU.mult)
                if not f.gated:
                    ins.then_inc(weights_ready, 1)
                    dve.wait_ge(weights_ready, f.n - 1)
                else:
                    chain.link(ins)
                share = k / (k + 1) if f.shared else 1.0
                ins = dve.tensor_scalar(CW[:, 0:n, :], LR[:, :, 0:n].rearrange("p t e -> p e t"), 0.5 * share, None, ALU.mult)
                if f.shared:
                    chain.link(ins)
                    ins = dve.memset(CW[:, n:n + f.shared, :], 0.5 / (k + 1))
                chain.link(ins)

            def experts(f):
                route(f)
                if not f.gated:
                    for q in range(4):
                        dve.wait_ge(bias_in_psum, 4 * (f.n - 2) + q + 1)
                        ins = dve.tensor_tensor(X[:, 2 * q:2 * q + 2, :].rearrange("p t d -> p (t d)"), PS[4 + q % 2],
                                                X[:, 2 * q:2 * q + 2, :].rearrange("p t d -> p (t d)"), op=ALU.add)
                        ins.then_inc(bias_added, 1)
                    dve.wait_ge(bias_added, 4 * (f.n - 1))

                def gate(s, r):
                    dve.wait_ge(act_ready, s + 1)
                    if not (isinstance(s, int) and s < f.s0 + 2):
                        dve.wait_ge(down_in_psum, s - 1)
                    if f.gated:
                        dve.scalar_tensor_tensor(FT[:, r % 2, :], FT[:, r % 2, :], 1.0, PS[2 * (r % 2)],
                                                 ALU.add, ALU.mult).then_inc(silu_ready, 1)
                        dve.wait_ge(silu_ready, s + 1)
                        dve.tensor_tensor(FG[:, r % 2, :], PS[2 * (r % 2) + 1], FT[:, r % 2, :], op=ALU.mult).then_inc(gate_ready, 1)
                    else:
                        dve.scalar_tensor_tensor(FG[:, r % 2, :], FT[:, r % 2, :], 1.0, FG[:, r % 2, :],
                                                 ALU.add, ALU.mult).then_inc(gate_ready, 1)

                def add(s, r):
                    dve.wait_ge(down_in_psum, s + 1)
                    if not (isinstance(s, int) and s < f.s0 + 2):
                        dve.wait_ge(down_added, s - 1)
                    for t in range(4):
                        tile = 4 * (r % 2) + t
                        ins = dve.scalar_tensor_tensor(X[:, tile, :], PS[4 + 2 * (r % 2) + t // 2][:, (t % 2) * D:(t % 2) * D + D],
                                                       CWP[:, r // 2, tile:tile + 1], X[:, tile, :], ALU.mult, ALU.add)
                    ins.then_inc(down_added, 1)

                def pair_weights(i):
                    dve.tensor_copy(CWP[:, :, :], CW[:, bass.ds(2 * i, 2), :]).then_inc(pair_ready, 1)
                    dve.wait_ge(pair_ready, f.p0 + i + 1)

                gate(f.s0, 0)
                gate(f.s0 + 1, 1)
                pair_weights(0)
                add(f.s0, 0)
                gate(f.s0 + 2, 2)
                add(f.s0 + 1, 1)
                gate(f.s0 + 3, 3)
                add(f.s0 + 2, 2)
                with dve.Fori(1, f.pairs) as i:
                    s = f.s0 + 4 * i
                    gate(s, 0)
                    add(s - 1, 3)
                    dve.wait_ge(down_added, s)
                    pair_weights(i)
                    for r in range(1, 4):
                        gate(s + r, r)
                        add(s + r - 1, r - 1)
                add(f.s0 + 4 * f.pairs - 1, 3)
                dve.wait_ge(down_added, f.s0 + 4 * f.pairs)
                dve.sem_inc(layer_done, 1)

            dve.wait_ge(layer_done, 1)
            layer_norm(1)
            experts(F2)
            dve.wait_ge(gate_tanh, 2)
            chain.link(dve.tensor_scalar(GATE[:, 0, :], GATE[:, 0, :], 0.5, 0.5, ALU.mult, ALU.add))
            dve.tensor_scalar(GATE[:, 1, :], GATE[:, 0, :], -1.0, 1.0, ALU.mult, ALU.add).then_inc(gate_set, 1)
            dve.tensor_scalar(T3[:, 1:2], T3[:, 1:2], -0.5, None, ALU.mult).then_inc(time_ready, 1)
            layer_norm(2)
            for q in range(4):
                dve.wait_ge(shift_in_psum, q + 1)
                if q == 0:
                    dve.wait_ge(gate_set, 1)
                dve.wait_ge(kept_ready, 2 * q + 2)
                chain.link(dve.tensor_tensor(SZ[:, q % 2, :].rearrange("p (t d) -> p t d", t=2), PS[q].rearrange("p (t d) -> p t d", t=2),
                                             GATE[:, 0, :].unsqueeze(1).to_broadcast([P, 2, D]), op=ALU.mult))
                ins = dve.tensor_tensor(OUT[:, 2 * q:2 * q + 2, :].rearrange("p t d -> p (t d)"), SZ[:, q % 2, :],
                                        OUT[:, 2 * q:2 * q + 2, :].rearrange("p t d -> p (t d)"), op=ALU.add)
            chain.link(ins)
            layer_norm(3, OUT)
            for q in range(2):
                s = slice(q * 512, q * 512 + 512)
                dve.wait_ge(kexp_ready, 2 * q + 2)
                ins = dve.tensor_tensor(WKV[:, s], PS[2 + q][0:64, :], KS[:, s], op=ALU.mult)
                chain.link(ins)
                for b in range(2 * q, 2 * q + 2):
                    dve.tensor_tensor_scan(ST[:, b * D:b * D + D], T3[:, 0:1].to_broadcast([64, D]), WKV[:, b * D:b * D + D],
                                           0.0, ALU.mult, ALU.add).then_inc(states_ready, 1)
            for q in range(4):
                dve.wait_ge(out3_in_psum, q + 1)
                ins = dve.tensor_tensor(X[:, 2 * q:2 * q + 2, :].rearrange("p t d -> p (t d)"), PS[4 + q],
                                        X[:, 2 * q:2 * q + 2, :].rearrange("p t d -> p (t d)"), op=ALU.add)
            ins.then_inc(layer_done, 1)
            dve.wait_ge(layer_done, 3)
            layer_norm(4)
            experts(F4)
            dve.wait_ge(slope_loaded, 16)
            chain.link(dve.tensor_scalar(SLOPE[:, :], SLOPE[:, :], -1.0, None, ALU.mult))
            chain.link(dve.tensor_scalar(DMASK[:, :], dist, 0.0, NEG, ALU.is_lt, ALU.mult))
            for h in range(LH):
                ins = dve.scalar_tensor_tensor(DEC[:, h, :], dist, SLOPE[:, h:h + 1], DMASK[:, :], ALU.mult, ALU.add)
            ins.then_inc(dec_begun, 1)
            dve.wait_ge(dec_exp, 1)
            dve.tensor_scalar(DEC, DEC, 0.25, None, ALU.mult).then_inc(dec_ready, 1)
            dve.wait_ge(layer_done, 4)
            layer_norm(5)
            dve.wait_ge(permuted, 16 * 8)
            dve.wait_ge(dec_ready, 1)
            with dve.Fori(0, NB) as b:
                for n in range(4):
                    dve.wait_ge(qktanh_ready, 4 * b + n + 1)
                    v = (QT if n < 2 else KT)[:, 2 * (n % 2):2 * (n % 2) + 2, :]
                    dve.scalar_tensor_tensor(v, v, 1.0, PS[n].rearrange("p (g t) -> p g t", g=2),
                                             ALU.add, ALU.mult).then_inc(qk_ready, 1)
                for g in range(4):
                    dve.wait_ge(sc_in_psum, 4 * b + g + 1)
                    if g >= 2:
                        dve.wait_ge(pv_done, 4 * b + g - 1)
                    p0 = M[:, g % 2, :, :].rearrange("p (h a) t -> p h (a t)", h=4)
                    dve.tensor_tensor(p0, BANKS[:, 0:4, 0:D], DEC[:, 4 * g:4 * g + 4, :], op=ALU.mult)
                    dve.tensor_tensor(SZ[:, g % 2, :].rearrange("p (h t) -> p h t", h=4), BANKS[:, 0:4, D:D + P],
                                      DEC[:, 4 * g:4 * g + 4, 0:P], op=ALU.mult).then_inc(p_ready, 1)
                dve.wait_ge(or_ready, b + 1)
                dve.wait_ge(pv_done, 4 * b + 4)
                for c in range(2):
                    ins = dve.scalar_tensor_tensor(UO[:, c * D:c * D + D], PS[6][:, c * D:c * D + D], sso[:, c:c + 1],
                                                   Y0[:, c, D:2 * D], ALU.mult, ALU.mult)
                ins.then_inc(uo_ready, 1)
                dve.wait_ge(out5_in_psum, b + 1)
                dve.tensor_tensor(X[:, bass.ds(2 * b, 2), :], PS[4].rearrange("p (t d) -> p t d", t=2),
                                  OUT[:, bass.ds(2 * b, 2), :], op=ALU.add).then_inc(x5_ready, 1)
            dve.wait_ge(x5_ready, NB)
            dve.sem_inc(layer_done, 1)
            layer_norm(6)
            experts(F6)
            dve.tensor_scalar(blockb[:, 0:P], blk, 1.0, -NEG, ALU.subtract, ALU.mult)
            for n in range(1, 4):
                ins = dve.tensor_scalar(blockb[:, n * P:n * P + P], blk, 1.0, -NEG, ALU.subtract, ALU.mult)
            ins.then_inc(masks_ready, 1)
            dve.sem_inc(av_ready, 1)
            layer_norm(7)
            heads = X[:, :, :].rearrange("p t (h a d) -> p t h a d", a=2, d=LD)
            with dve.Fori(0, NB) as b:
                for c in range(2):
                    n = 2 * b + c
                    dve.wait_ge(s7_in_psum, n + 1)
                    sc = BANKS[:, 4 * c:4 * c + 4, 0:D].rearrange("p j (k t) -> p j k t", k=KD)
                    dve.tensor_reduce(MXS[:, c, :].rearrange("p (j k) -> p j k", k=KD), sc, AX.X, ALU.max).then_inc(max_ready, 1)
                    dve.wait_ge(max_ready, n + 1)
                    dve.tensor_tensor(E[:, c, :, :].rearrange("p (j k) t -> p j k t", k=KD), sc,
                                      MXS[:, c, :].rearrange("p (j k) -> p j k", k=KD).unsqueeze(3).to_broadcast([P, 4, KD, P]),
                                      op=ALU.subtract).then_inc(s7_ready, 1)
                for c in range(2):
                    n = 2 * b + c
                    dve.wait_ge(e7_ready, n + 1)
                    dve.transpose(M[:, c, :, :].rearrange("p h k -> p (h k)"), E[:, c, :, :].rearrange("p h k -> p (h k)")).then_inc(et7_ready, 1)
                for c in range(2):
                    n = 2 * b + c
                    dve.wait_ge(av_in_psum, n + 1)
                    av = PS[4 * c][:, D:D + 8 * (LD + 1)].rearrange("p (h d) -> p h d", h=8)
                    dve.reciprocal(RS[:, c, :], av[:, :, LD]).then_inc(recip_ready, 1)
                    dve.wait_ge(recip_ready, n + 1)
                    dve.tensor_tensor(AV[:, c, :, :], av[:, :, 0:LD], RS[:, c, :].unsqueeze(2).to_broadcast([P, 8, LD]),
                                      op=ALU.mult).then_inc(av_ready, 1)
                    dve.wait_ge(av_ready, n + 2)
                    xh = heads[:, bass.ds(n, 1), :, c, :].rearrange("p a h d -> p (a h) d")
                    ins = dve.tensor_tensor(xh, xh, AV[:, c, :, :], op=ALU.add)
                    ins.then_inc(x7_ready, 1)
            dve.wait_ge(x7_ready, NT)
            dve.sem_inc(layer_done, 1)
            layer_norm(8)
            experts(F8)

        @block.tensor
        def _(pe):
            def transpose_xn(layer, odd_from=0):
                for q in range(NT // 2):
                    if q >= 2:
                        pe.wait_ge(xt_ready, 4 * layer + q - 1)
                    for t in range(2 * q, 2 * q + 2):
                        pe.wait_ge(xn_ready, NT * layer + t + 1)
                        for k in range(KD):
                            ins = pe.transpose(PS[6 + q % 2][:, k * 256 + (t % 2) * P:k * 256 + (t % 2) * P + P],
                                               XN[:, t, k * P + (t % 2) * odd_from:k * P + (t % 2) * odd_from + P], ident)
                    ins.then_inc(xt_in_psum, 1)

            pe.wait_ge(consts_loaded, 16)
            transpose_xn(0)
            pe.wait_ge(xt_ready, 4)
            pe.wait_ge(wb_loaded, 16)
            for n in range(4):
                for k in range(KD):
                    ins = pe.matmul(PS[n], WB[:, k, (n // 2) * (NS + NH):(n // 2) * (NS + NH) + NS],
                                    XT[:, k, (n % 2) * 512:(n % 2) * 512 + 512], start=k == 0, stop=k == KD - 1)
                ins.then_inc(bc_in_psum, 1)
            for q in range(4):
                for t in range(2 * q, 2 * q + 2):
                    for k in range(KD):
                        ins = pe.matmul(PS[4 + q][:, (t % 2) * 256:(t % 2) * 256 + NS + NH], XT[:, k, t * P:t * P + P],
                                        WB[:, k, 0:NS + NH], start=k == 0, stop=k == KD - 1)
                ins.then_inc(bdt_in_psum, 1)
            pe.wait_ge(bc_ready, 4)
            for q in range(2):
                for t in range(4 * q, 4 * q + 4):
                    ins = pe.matmul(PS[2 + q][:, (t % 4) * P:(t % 4) * P + P], BT[:, t * P:t * P + P],
                                    CT[:, t * P:t * P + P], start=True, stop=True)
                ins.then_inc(gt_in_psum, 1)
            pe.wait_ge(da_ready, 1)
            pe.wait_ge(masks_ready, 2)
            for n, lower in enumerate((tri, ones[:, :])):
                pe.matmul(PS[n][:, 0:NT * NH], lower, dA[:, :, :].rearrange("p t h -> p (t h)"),
                          start=True, stop=True).then_inc(cum_in_psum, 1)
            for t in range(NT):
                ins = pe.matmul(PS[4 + t // 4][0:NH, (t % 4) * P:(t % 4) * P + P], dA[:, t, :], tri, start=True, stop=True)
                if t % 4 == 3:
                    ins.then_inc(cumt_in_psum, 1)
            pe.wait_ge(gt_ready, 2)
            pe.wait_ge(b_ready, 4)
            pe.wait_ge(cum_ready, 3)
            pe.wait_ge(cumt_ready, 2)

            def up(m, u):
                if u == 0:
                    pe.wait_ge(wx_loaded, m * 2 + 16)
                after(pe, xp_ready, m)
                for k in range(KD):
                    ins = pe.matmul(PS[0], WX[:, k, (u // 2) * P:(u // 2) * P + P], XT[:, k, (u % 2) * 512:(u % 2) * 512 + 512],
                                    start=k == 0, stop=k == KD - 1)
                ins.then_inc(up_in_psum, 1)

            def to_tokens(m, u):
                pe.wait_ge(xc_ready, m + 1)
                after(pe, xtok_ready, m)
                for t in range(4):
                    ins = pe.transpose(PS[1][:, t * P:t * P + P], TH[:, u % 2, t // 2, (t % 2) * P:(t % 2) * P + P], ident)
                ins.then_inc(xc_in_psum, 1)

            for u in range(NT + 1):
                if u < NT:
                    up(u, u)
                if u:
                    to_tokens(u - 1, u - 1)

            def gated_transposed(n, c):
                pe.wait_ge(gated_ready, n + 1)
                after(pe, gtr_ready, n)
                for k in range(GC):
                    ins = pe.transpose(PS[6][:, k * P:k * P + P], G[:, c % 2, k * P:k * P + P], ident)
                ins.then_inc(g_in_psum, 1)

            def project_out(n, c, slot):
                pe.wait_ge(gtr_ready, n + 1)
                after(pe, o_added, n)
                for k in range(GC):
                    ins = pe.matmul(PS[7][:, 0:D], GTR[:, c % 2, k * P:k * P + P], WO[:, slot, k, :], start=k == 0, stop=k == GC - 1)
                ins.then_inc(o_in_psum, 1)

            def values(c, slot):
                for h in reversed(range(GH)):
                    cols_ = slice(max(h * HD - 32, 0), h * HD + HD)
                    ins = pe.matmul(PS[2][:, cols_], M[:, c % 2, h, :], XTOK[:, slot, c, cols_], start=True, stop=True)
                ins.then_inc(y_in_psum, 1)

            def group(g, slot):
                first, last = isinstance(g, int) and g == 0, isinstance(g, int) and g == NG - 1
                pe.wait_ge(wz_loaded, (g + 1) * 16)
                pe.wait_ge(h0_loaded, (g + 1) * 16)
                pe.wait_ge(wo_ready, g + 1)
                for c in range(NT):
                    n = g * NT + c
                    after(pe, zsilu_ready, n)
                    for k in range(KD):
                        ins = pe.matmul(PS[4], XT[:, k, c * P:c * P + P], WZ[:, slot, k, :], start=k == 0, stop=k == KD - 1)
                    ins.then_inc(z_in_psum, 1)
                    if not last:
                        up(n + NT, c)
                    if c and not last:
                        to_tokens(n + NT - 1, c - 1)
                    if c == 0:
                        pe.wait_ge(xtok_ready, (g + 1) * NT)
                    pe.wait_ge(mix_ready, n + 1)
                    after(pe, y0_ready, n)
                    values(c, slot)
                    if not (first and c == 0):
                        gated_transposed(n - 1, (c - 1) % NT)
                    if c % 2 == 0:
                        pe.wait_ge(xs_ready, g * NB + c // 2 + 1)
                        after(pe, h1_ready, g * NB + c // 2)
                        pe.matmul(PS[5], BN[:, c // 2, :], XS[:, :], start=True, stop=True).then_inc(s_in_psum, 1)
                    else:
                        pe.wait_ge(h1_ready, g * NB + c // 2 + 1)
                    after(pe, y1_ready, n)
                    pe.matmul(PS[3], CT[:, c * P:c * P + P], H1[:, :] if c % 2 else H0[:, slot, :], start=True, stop=True).then_inc(i_in_psum, 1)
                    if not (first and c == 0):
                        project_out(n - 1, (c - 1) % NT, slot if c else 1 - slot)
                if not last:
                    to_tokens(n + NT, NT - 1)

            groups_of(pe, group)
            n = NG * NT - 1
            gated_transposed(n, NT - 1)
            project_out(n, NT - 1, 1)

            def experts(f):
                pe.wait_ge(xt_ready, 4 * (f.norm + 1))
                if f.n == 0:
                    pe.wait_ge(small_loaded, 16)
                if f.gated:
                    logits = [(XT[:, k, t * P:t * P + P], SM[:, k, 0:16]) for t in range(NT) for k in range(KD)]
                else:
                    if f.n == 2:
                        pe.wait_ge(wg_loaded, 16)
                        pe.wait_ge(bd_loaded, 16)
                    for q in range(2):
                        for k in range(KD):
                            ins = pe.matmul(PS[4 + q][0:8, :], SM[:, k, 16:24], XT[:, k, q * 512:q * 512 + 512], start=k == 0, stop=k == KD - 1)
                        ins.then_inc(hop_in_psum, 1)
                    pe.wait_ge(hop_ready, 2 * (f.n - 1))
                    logits = [(TT[:, t * P:t * P + P], WG[:, :]) for t in range(NT)]
                m = f.routed
                per = len(logits) // NT
                for n, (l, r) in enumerate(logits):
                    ins = pe.matmul(PS[4][:, n // per * m:n // per * m + m], l, r, start=n % per == 0, stop=n % per == per - 1)
                ins.then_inc(logits_in_psum, 1)

                def up(s, r, pair):
                    pe.wait_ge(wu_loaded[r // 2], 16 * (pair + 1))
                    if not (isinstance(s, int) and s < f.s0 + 2):
                        pe.wait_ge(gate_ready, s - 1)
                    for w in range(2 if f.gated else 1):
                        for k in range(KD):
                            ins = pe.matmul(PS[2 * (r % 2) + w], WU[r // 2][:, (2 * w + k) * P:(2 * w + k) * P + P],
                                            XT[:, k, (r % 2) * 512:(r % 2) * 512 + 512], start=k == 0, stop=k == KD - 1)
                    ins.then_inc(hidden_in_psum, 1)

                def down(s, r, pair):
                    pe.wait_ge(wd_loaded[r // 2], 16 * (pair + 1))
                    pe.wait_ge(gate_ready, s + 1)
                    if not (isinstance(s, int) and s < f.s0 + 2):
                        pe.wait_ge(down_added, s - 1)
                    for t in range(4):
                        ins = pe.matmul(PS[4 + 2 * (r % 2) + t // 2][:, (t % 2) * D:(t % 2) * D + D], FG[:, r % 2, t * P:t * P + P],
                                        WD[r // 2][:, :], start=True, stop=True)
                    ins.then_inc(down_in_psum, 1)

                if not f.gated:
                    pe.wait_ge(weights_ready, f.n - 1)
                    for t in range(NT):
                        ins = pe.transpose(PS[6 + t // 4][0:8, (t % 4) * P:(t % 4) * P + P], LR[:, t, 0:8], ident)
                        if t % 4 == 3:
                            ins.then_inc(scores_in_psum, 1)
                    pe.wait_ge(scores_ready, 2 * (f.n - 1))
                    for q in range(4):
                        if q >= 2:
                            pe.wait_ge(bias_added, 4 * (f.n - 2) + q - 1)
                        for t in range(2 * q, 2 * q + 2):
                            ins = pe.matmul(PS[4 + q % 2][:, (t % 2) * D:(t % 2) * D + D], SCT[:, t * P:t * P + P], BD[:, :], start=True, stop=True)
                        ins.then_inc(bias_in_psum, 1)
                    pe.wait_ge(bias_added, 4 * (f.n - 1))

                up(f.s0, 0, f.p0)
                for r in range(3):
                    up(f.s0 + r + 1, r + 1, f.p0)
                    down(f.s0 + r, r, f.p0)
                with pe.Fori(1, f.pairs) as i:
                    s, pair = f.s0 + 4 * i, f.p0 + i
                    up(s, 0, pair)
                    down(s - 1, 3, pair - 1)
                    for r in range(3):
                        up(s + r + 1, r + 1, pair)
                        down(s + r, r, pair)
                down(f.s0 + 4 * f.pairs - 1, 3, f.p0 + f.pairs - 1)

            transpose_xn(1)
            experts(F2)
            transpose_xn(2)
            pe.wait_ge(xt_ready, 4 * 3)
            pe.wait_ge(w3_loaded, 16)
            for q in range(4):
                for t in range(2 * q, 2 * q + 2):
                    for k in range(KD):
                        ins = pe.matmul(PS[q][:, (t % 2) * D:(t % 2) * D + D], XT[:, k, (t ^ 1) * P:(t ^ 1) * P + P],
                                        W3[:, k, 0:D], start=k == 0, stop=k == KD - 1)
                ins.then_inc(shift_in_psum, 1)
            transpose_xn(3)
            pe.wait_ge(xt_ready, 4 * 4)
            for q in range(2):
                for n in range(2):
                    for k in range(KD):
                        ins = pe.matmul(PS[2 * n + q][0:64, :], W3[:, k, D + 64 * n:D + 64 * n + 64],
                                        XT[:, k, q * 512:q * 512 + 512], start=k == 0, stop=k == KD - 1)
                ins.then_inc(kv_in_psum, 1)
            pe.wait_ge(wo3_loaded, 16)
            for q in range(4):
                pe.wait_ge(states_ready, q + 1)
                for t in range(2 * q, 2 * q + 2):
                    ins = pe.matmul(PS[4 + q][:, (t % 2) * D:(t % 2) * D + D], ST[:, t * P:t * P + P], WO3[:, :], start=True, stop=True)
                ins.then_inc(out3_in_psum, 1)
            transpose_xn(4)
            experts(F4)
            transpose_xn(5)
            pe.wait_ge(w5_loaded, 16)
            pe.wait_ge(wo5_loaded, 16)
            with pe.Fori(0, NB) as b:
                pe.wait_ge(xb_ready, b + 1)
                for n in range(4):
                    for g in range(2 * n, 2 * n + 2):
                        for k in range(KD):
                            ins = pe.matmul(PS[n][:, (g % 2) * D:(g % 2) * D + D], W5[:, k, g * P:g * P + P], XB[:, k, :],
                                            start=k == 0, stop=k == KD - 1)
                    ins.then_inc(qk_in_psum, 1)
                for c in range(2):
                    for k in range(KD):
                        ins = pe.matmul(PS[4 + c], XB[:, k, c * P:c * P + P], W5[:, k, 2 * LQ:], start=k == 0, stop=k == KD - 1)
                    ins.then_inc(vu_in_psum, 1)
                pe.wait_ge(qk_ready, 4 * b + 4)
                pe.wait_ge(vu_ready, 2 * b + 2)

                def values(g):
                    pe.wait_ge(p_ready, 4 * b + g + 1)
                    p0 = M[:, g % 2, :, :].rearrange("p (h a) t -> p h (a t)", h=4)
                    for j in range(4):
                        h = 4 * g + j
                        v = slice(h * LD, h * LD + LD)
                        pe.matmul(PS[6][:, h * LD:h * LD + LD], p0[:, j, 0:P], Y0[:, 0, v], start=True, stop=True)
                        o1 = PS[6][:, D + h * LD:D + h * LD + LD]
                        pe.matmul(o1, p0[:, j, P:2 * P], Y0[:, 0, v], start=True, stop=False)
                        ins = pe.matmul(o1, SZ[:, g % 2, j * P:j * P + P], Y0[:, 1, v], start=False, stop=True)
                    ins.then_inc(pv_done, 1)

                for g in range(4):
                    if g:
                        pe.wait_ge(p_ready, 4 * b + g)
                    for j in range(4):
                        rows_ = slice(32 * j, 32 * j + LD)
                        pe.matmul(PS[j][:, 0:D], KT[rows_, g, 0:P], QT[rows_, g, :], start=True, stop=True)
                        ins = pe.matmul(PS[j][:, D:D + P], KT[rows_, g, P:2 * P], QT[rows_, g, P:2 * P], start=True, stop=True)
                    ins.then_inc(sc_in_psum, 1)
                    if g:
                        values(g - 1)
                values(3)
                pe.wait_ge(uo_ready, b + 1)
                for k in range(KD):
                    for c in range(2):
                        ins = pe.transpose(PS[7][:, k * D + c * P:k * D + c * P + P], UO[:, c * D + k * P:c * D + k * P + P], ident)
                ins.then_inc(uot_in_psum, 1)
                pe.wait_ge(uot_ready, b + 1)
                uot = UOT.rearrange("p (k t a) -> p k t a", k=KD, a=2)
                for par in range(2):
                    for k in range(KD):
                        ins = pe.matmul(PS[4][:, par * D:par * D + D], uot[:, k, :, par], WO5[:, k, :], start=k == 0, stop=k == KD - 1)
                ins.then_inc(out5_in_psum, 1)
                pe.wait_ge(x5_ready, b + 1)
            transpose_xn(6)
            experts(F6)
            transpose_xn(7, odd_from=LD)
            pe.wait_ge(masks_ready, 3)
            pe.wait_ge(xa_ready, NT)
            with pe.Fori(0, NB) as b:
                pe.wait_ge(xb7_ready, b + 1)
                for c in range(2):
                    if c == 0:
                        pe.wait_ge(av_ready, 2 * b + 1)
                    for j in range(4):
                        pe.matmul(PS[4 * c + j][:, 0:D], identb[:, :], blockb[:, 0:D], start=True, stop=False, skip_group_check=True)
                    for j in range(4):
                        for k in range(KD):
                            g = XB[32 * j:32 * j + LD, k, c * P:c * P + P]
                            ins = pe.matmul(PS[4 * c + j][:, k * P:k * P + P], g, g, start=False, stop=k == KD - 1, skip_group_check=True)
                    ins.then_inc(s7_in_psum, 1)
                for c in range(2):
                    pe.wait_ge(et7_ready, 2 * b + c + 1)
                    for h in range(8):
                        ins = pe.matmul(PS[4 * c][:, D + h * (LD + 1):D + (h + 1) * (LD + 1)], M[:, c, 2 * (h % 4) + h // 4, :],
                                        XA[:, bass.ds(2 * b + c, 1), h, :].rearrange("p a d -> p (a d)"), start=True, stop=True)
                    ins.then_inc(av_in_psum, 1)
            transpose_xn(8)
            experts(F8)


def kernel(**inputs):
    import numpy as np
    import concourse.bacc as bacc
    from concourse.bass_utils import run_bass_kernel_spmd

    a = {n: np.asarray(v) for n, v in inputs.items()}
    t = lambda m: np.ascontiguousarray(m.T)

    def blocks(m):
        return np.ascontiguousarray(m.reshape(KD, P, -1).transpose(1, 0, 2))

    def groups(m):
        return np.ascontiguousarray(m.reshape(KD, P, NG, GW).transpose(2, 1, 0, 3))

    win = t(a["L0_attn_a_in_proj_w"])
    idx = np.arange(P)
    consts = np.concatenate([
        np.eye(P), idx[:, None] <= idx[None, :], np.arange(2 * P)[None, :] - idx[:, None],
        idx[:, None] // 32 == idx[None, :] // 32], axis=1).astype(np.float32)
    b, c, dt = win[:, 2 * DI:2 * DI + NS], win[:, 2 * DI + NS:2 * DI + 2 * NS], win[:, 2 * DI + 2 * NS:]
    chan = np.concatenate([a["L0_attn_a_conv_w"], a["L0_attn_a_conv_b"][:, None], a["L0_attn_a_conv_state"][0]], axis=1)
    def rows_of(w):
        return w.reshape(-1, KD, P, P).transpose(0, 2, 1, 3).reshape(-1, P, KD * P)

    def experts_up(routed, shared):
        return np.concatenate([rows_of(a[routed]), rows_of(a[shared].reshape(D, 4, P).transpose(1, 0, 2))])

    qkvu = t(a["L1_attn_a_W_qkvu"])
    w5 = np.zeros((D, 2 * LQ + 512), qkvu.dtype)
    w5[:, 0:2 * LQ].reshape(D, 2 * LH, 32)[:, :, 0:LD] = qkvu[:, 0:512].reshape(D, 2 * LH, LD)
    w5[:, 2 * LQ:] = qkvu[:, 512:]
    col = lambda v: v.reshape(KD, P).T
    arrays = {
        "x": a["L0_attn_a_x"].reshape(T, D),
        "consts": consts,
        "rows": np.concatenate([a["L0_attn_a_dt_bias"], a["L0_attn_a_A_log"], a["L0_attn_a_D_param"], a["L0_attn_b_gate"],
                                a["L1_attn_a_slope_rate"].reshape(-1)]),
        "cols": np.stack([col(a["L0_attn_a_norm_w"]), col(a["L0_attn_b_ln_gamma"]), col(a["L0_attn_b_ln_beta"])], axis=1),
        "wx": groups(win[:, DI:2 * DI]),
        "wz": groups(win[:, 0:DI]),
        "wbcdt": blocks(np.concatenate([b, dt, c], axis=1)),
        "wout": t(a["L0_attn_a_out_proj_w"]).reshape(NG, GC, P, D).transpose(0, 2, 1, 3),
        "chan": chan.reshape(NG, GC, P, NPC).transpose(0, 2, 1, 3),
        "inw": a["L0_attn_a_inner_norm_w"].reshape(NG, GC, P).transpose(0, 2, 1),
        "h0": a["L0_attn_a_ssm_state"][0].reshape(NG, GH, NS, HD).transpose(0, 2, 1, 3).reshape(NG, NS, GW),
        "small": np.concatenate([blocks(a["L0_ffn_w_router"]), blocks(t(a["L1_ffn_Wg1"]))], axis=2),
        "w3": np.concatenate([blocks(t(a[f"L0_attn_b_W_{n}"])) for n in ("shift", "key", "value")], axis=2),
        "wo3": t(a["L0_attn_b_W_output"]),
        "t3": np.stack([a["L0_attn_b_time_decay"], a["L0_attn_b_time_first"]], axis=1),
        "wu2": np.concatenate([experts_up("L0_ffn_we1", "L0_ffn_ws1"), experts_up("L0_ffn_we3", "L0_ffn_ws3")], axis=2),
        "wd2": np.concatenate([a["L0_ffn_we2"], a["L0_ffn_ws2"].reshape(4, P, D)]),
        "wu6": np.concatenate([rows_of(a["L1_ffn_Wup"].transpose(0, 2, 1)), a["L1_ffn_bup"][:, :, None]], axis=2),
        "wd6": a["L1_ffn_Wdown"].transpose(0, 2, 1),
        "wg6": t(a["L1_ffn_Wg2"]),
        "bd6": a["L1_ffn_bdown"],
        "w5": blocks(w5),
        "wo5": blocks(t(a["L1_attn_a_W_out"])),
    }
    nc = bacc.Bacc("TRN2", target_bir_lowering=False, num_devices=1)
    arrays = {f"in_{n}": np.ascontiguousarray(v) for n, v in arrays.items()}
    args = {n[3:]: nc.dram_tensor(n, v.shape, mybir.dt.from_np(v.dtype), kind="ExternalInput").ap() for n, v in arrays.items()}
    out = nc.dram_tensor("out_x", (T, D), FP32, kind="ExternalOutput").ap()
    mixer_program(nc, out=out, **args)
    r = run_bass_kernel_spmd(nc, [arrays], core_ids=[0])
    return r.results[0]["out_x"].reshape(4, 256, 256)
```

```python
from contextlib import ExitStack

import concourse.bass as bass
from concourse import mybir

FP32 = mybir.dt.float32
FP32R = mybir.dt.float32r
BF16 = mybir.dt.bfloat16
ALU = mybir.AluOpType
ACT = mybir.ActivationFunctionType
AX = mybir.AxisListType

P = 128
D = 256
KD = D // P
T = 1024
NT = T // P
NB = 4
LN_EPS = 1e-5
NEG = -1e30

DI = 3072
NH = 48
HD = 64
NS = 128
GH = 8
NG = NH // GH
GW = GH * HD
GC = GW // P
TAPS = 4
NPC = TAPS + 1 + (TAPS - 1)

LH = 16
LD = 16
AW = 8 * (LD + 1)
SW = D + P
TINY = -3e38
TAKEN = 3e38


class Experts:

    def __init__(self, n, gated, routed, shared, top, norm, before):
        self.n, self.gated, self.routed, self.shared, self.top, self.norm = n, gated, routed, shared, top, norm
        self.count = routed + shared
        self.pairs = self.count // 2
        self.s0 = before.s0 + 4 * before.pairs if before else 0
        self.p0 = before.p0 + before.pairs if before else 0
        self.width = 256 * (2 if gated else 1) + (0 if gated else 1)


F2 = Experts(0, True, 16, 4, 4, 1, None)
F4 = Experts(1, True, 16, 4, 4, 4, F2)
F6 = Experts(2, False, 8, 0, 2, 6, F4)
F8 = Experts(3, False, 8, 0, 2, 8, F6)


class Chain:

    def __init__(self, eng, sem):
        self.eng, self.sem, self.base, self.n = eng, sem, 0, 0

    def link(self, ins):
        self.n += 1
        ins.then_inc(self.sem, 1)
        self.eng.wait_ge(self.sem, self.base + self.n)

    def enter(self, i, per):
        self.start, self.per = self.n, per
        self.base, self.n = i * per + self.n, 0

    def leave(self, times):
        assert self.n == self.per, self.n
        self.base, self.n = 0, self.start + self.per * times


def mixer_program(nc, x, consts, rows, cols, wx, wz, wbcdt, wout, chan, inw, h0, small, w3, wo3, t3,
                  wu2, wd2, wu6, wd6, wg6, bd6, w5, wo5, out):
    ctx = ExitStack()
    with ctx:
        def sb(name, shape, dt=FP32):
            return ctx.enter_context(nc.sbuf_tensor(name, shape, dt))

        def sem(name):
            return ctx.enter_context(nc.semaphore(name))

        BANKS = ctx.enter_context(nc.psum_tensor("BANKS", [P, 8, 512], FP32))
        PS = [BANKS[:, n, :] for n in range(8)]

        X = sb("X", [P, NT, D])
        XN = sb("XN", [P, NT, D + 16])
        XT = sb("XT", [P, KD, T])
        K = sb("K", [P, 652])
        ident, tri, dist, blk, own_head = K[:, 0:128], K[:, 128:256], K[:, 256:512], K[:, 512:640], K[:, 640:648]
        own_rows = K[:, 648:652]
        CMASK = sb("CMASK", [P, P])
        identb = sb("identb", [P, P], BF16)
        ROW = sb("ROW", [P, 3 * NH])
        COL = sb("COL", [P, 3, KD])
        bn = sb("bn", [P, NT, 6])
        mv = sb("mv", [P, NT, 2])
        rstd = sb("rstd", [P, NT])
        rms = sb("rms", [P, NT])
        half = sb("half", [P, NT])

        WB = sb("WB", [P, KD, 2 * NS + NH])
        CT = sb("CT", [P, T])
        BN = sb("BN", [P, NB, NS])
        GT = sb("GT", [P, NT, P])
        ones = sb("ones", [P, P])
        dA = sb("dA", [P, NT, NH])
        ncum = sb("ncum", [P, NT, NH])
        ecum = sb("ecum", [P, NT, NH])
        eend = sb("eend", [P, NT, NH])
        eA = sb("eA", [P, NH])
        GRP = sb("GRP", [P, 2, 3, NT, GH])
        Dg = sb("Dg", [P, 2, GH])
        WO = sb("WO", [P, 2, GC, D])
        NW = sb("NW", [P, 2, GC])
        H0 = sb("H0", [P, 2, GW])
        XTOK = sb("XTOK", [P, 2, NT, GW])
        SQ = sb("SQ", [P, 2, NT])
        CH = sb("CH", [P, GC, NPC])
        XP = sb("XP", [P, 2, 2, D + TAPS - 1])
        CV = sb("CV", [P, 2, 2, D])
        TH = sb("TH", [P, 2, 2, D])
        M = sb("M", [P, 2, GH, P])
        SZ = sb("SZ", [P, 2, GW])
        Y0 = sb("Y0", [P, 2, GW])
        Y1 = sb("Y1", [P, 2, GW])
        XD = sb("XD", [P, 2, GW])
        XS = sb("XS", [P, GW])
        H1 = sb("H1", [P, GW])
        OUT = sb("OUT", [P, NT, D])
        SS = sb("SS", [P, NT])
        junk = sb("junk", [P, GW], BF16)
        with ExitStack() as mixer_only:
            WZ, WX, RB, E, G, GTR = (mixer_only.enter_context(nc.sbuf_tensor(name, shape, FP32)) for name, shape in (
                ("WZ", [P, 2, KD, GW]), ("WX", [P, KD, GW]),
                ("RB", [P, 2, GH, P]),
                ("E", [P, 2, GH, P]), ("G", [P, 2, GW]), ("GTR", [P, 2, GW])))
        XH, XL = sb("XH", [P, KD, T], FP32R), sb("XL", [P, KD, T], FP32R)
        UH, UL = sb("UH", [P, 2, 512], FP32R), sb("UL", [P, 2, 512], FP32R)
        DH, DL = sb("DH", [P, 2, D], FP32R), sb("DL", [P, 2, D], FP32R)
        FH, FL = sb("FH", [P, 2, 512], FP32R), sb("FL", [P, 2, 512], FP32R)
        BT = RB[:, :, :, :].rearrange("p a h t -> p (a h t)")
        dtr = XD[:, :, :].rearrange("p a n -> p (a n)")[:, 0:NT * NH].rearrange("p (t h) -> p t h", t=NT)
        dta = G[:, :, :].rearrange("p a n -> p (a n)")[:, 0:NT * NH].rearrange("p (t h) -> p t h", t=NT)
        CUMT = Y0[0:NH, :, :].rearrange("p a n -> p (a n)")

        SM = sb("SM", [P, KD, 24])
        WG = sb("WG", [8, 8])
        BD = sb("BD", [8, D])
        WU = [sb(f"WU{n}", [P, 512]) for n in range(2)]
        WD = [sb(f"WD{n}", [P, D]) for n in range(2)]
        FT = M[:, 0, :, :].rearrange("p (a h) t -> p a (h t)", a=2)
        FG = M[:, 1, :, :].rearrange("p (a h) t -> p a (h t)", a=2)
        BIAS = sb("BIAS", [P, 2])
        LG = sb("LG", [P, NT, 20])
        LR = sb("LR", [P, NT, 20])
        MX = sb("MX", [P, NT, 8])
        SUM = sb("SUM", [P, NT])
        CW = sb("CW", [P, 20, NT])
        CWP = sb("CWP", [P, 2, NT])
        TT = SZ[0:8, :, :].rearrange("p a n -> p (a n)")
        SCT = TT
        W3 = sb("W3", [P, KD, D + P])
        WO3 = sb("WO3", [64, D])
        T3 = sb("T3", [64, 2])
        GATE = sb("GATE", [P, 2, D])
        KS, WKV, ST = BT[0:64, :], CT[0:64, :], GT[0:64, :, :].rearrange("p t s -> p (t s)")
        xtok = XTOK[:, :, :, :].rearrange("p a t n -> p (a t n)")
        DEC = xtok[:, 0:LH * SW].rearrange("p (h t) -> p h t", h=LH)
        W5 = xtok[:, LH * SW:].rearrange("p (k n) -> p k n", k=KD)
        WO5 = XS[:, :].rearrange("p (k n) -> p k n", k=KD)
        DMASK = sb("DMASK", [P, 2 * P])
        SLOPE = sb("SLOPE", [P, LH])
        XB = XD[:, 0, :].rearrange("p (k t) -> p k t", k=KD)
        QT = SZ[:, 0, :].rearrange("p (g t) -> p g t", g=2)
        KT = SZ[:, 1, :].rearrange("p (g t) -> p g t", g=2)
        QH = [b[:, :, :, :].rearrange("p a (h c) t -> p (a h) (c t)", c=2) for b in (E, M)]
        SCO = RB[:, :, :, :].rearrange("p a h t -> p (a h t)")[:, 0:4 * SW].rearrange("p (a h t) -> p a h t", a=2, h=2)
        V5 = Y0[:, :, :].rearrange("p c (h n) -> p c h n", h=LH)
        UT, UO, OSQ = Y1[:, 0, :], Y1[:, 1, :], G[:, 0, :]
        sso = sb("sso", [P, 2])
        blockb = sb("blockb", [P, 4 * P], BF16)
        XA = sb("XA", [P, NT * AW])
        XE = RB[:, :, :, :].rearrange("p a (k j) t -> p a k j t", k=KD)
        MXS = sb("MXS", [P, 2, 8])
        RS = sb("RS", [P, 2, 8])
        AV = sb("AV", [P, 2, 8, LD])

        consts_loaded, x_loaded, rows_loaded, cols_loaded = sem("consts_loaded"), sem("x_loaded"), sem("rows_loaded"), sem("cols_loaded")
        wb_loaded, wx_loaded, chan_loaded = sem("wb_loaded"), sem("wx_loaded"), sem("chan_loaded")
        wz_loaded, wo_loaded, h0_loaded = sem("wz_loaded"), sem("wo_loaded"), sem("h0_loaded")
        out_stored = sem("out_stored")
        dve_self, act_self, pool_self = sem("dve_self"), sem("act_self"), sem("pool_self")
        stats_ready, rstd_ready, xn_ready, xt_in_psum, xt_ready = (
            sem(n) for n in ("stats_ready", "rstd_ready", "xn_ready", "xt_in_psum", "xt_ready"))
        masks_ready = sem("masks_ready")
        bc_in_psum, bc_ready, bdt_in_psum, b_ready = (
            sem(n) for n in ("bc_in_psum", "bc_ready", "bdt_in_psum", "b_ready"))
        gt_in_psum, gt_ready, softplus_step, da_ready, cum_in_psum, cum_ready, ea_ready = (
            sem(n) for n in ("gt_in_psum", "gt_ready", "softplus_step", "da_ready", "cum_in_psum", "cum_ready", "ea_ready"))
        group_ready, wo_ready = sem("group_ready"), sem("wo_ready")
        up_in_psum, xp_ready, conv_begun, conv_tap, conv_done, tanh_done, xc_ready, xc_in_psum, xtok_ready = (
            sem(n) for n in ("up_in_psum", "xp_ready", "conv_begun", "conv_tap", "conv_done", "tanh_done",
                             "xc_ready", "xc_in_psum", "xtok_ready"))
        cumt_in_psum, cumt_ready, cumt_stored = (
            sem(n) for n in ("cumt_in_psum", "cumt_ready", "cumt_stored"))
        rb_loaded = [sem("rb0_loaded"), sem("rb1_loaded")]
        nw_loaded, masked = sem("nw_loaded"), sem("masked")
        decay_ready, mix_ready, xs_ready, xd_ready = (
            sem(n) for n in ("decay_ready", "mix_ready", "xs_ready", "xd_ready"))
        z_in_psum, y_in_psum, i_in_psum, s_in_psum = (
            sem(n) for n in ("z_in_psum", "y_in_psum", "i_in_psum", "s_in_psum"))
        ztanh_ready, zsilu_ready, y0_ready, y1_ready, h1_ready, y_ready, gated_ready = (
            sem(n) for n in ("ztanh_ready", "zsilu_ready", "y0_ready", "y1_ready", "h1_ready", "y_ready", "gated_ready"))
        g_in_psum, gtr_ready, o_in_psum, o_added, squares_ready, squares_added = (
            sem(n) for n in ("g_in_psum", "gtr_ready", "o_in_psum", "o_added", "squares_ready", "squares_added"))
        h1_begun = sem("h1_begun")
        ss_ready, rms_ready = sem("ss_ready"), sem("rms_ready")
        layer_done = sem("layer_done")
        small_loaded, SMALL = sem("small_loaded"), 8 * 16
        wu_loaded = [sem("wu0_loaded"), sem("wu1_loaded")]
        wd_loaded = [sem("wd0_loaded"), sem("wd1_loaded")]
        hidden_in_psum, act_ready, gate_ready, down_in_psum, down_added = (
            sem(n) for n in ("hidden_in_psum", "act_ready", "gate_ready", "down_in_psum", "down_added"))
        hop_in_psum, hop_ready, logits_in_psum, logits_ready, weights_ready = (
            sem(n) for n in ("hop_in_psum", "hop_ready", "logits_in_psum", "logits_ready", "weights_ready"))
        scores_in_psum, scores_ready, bias_in_psum, bias_added = (
            sem(n) for n in ("scores_in_psum", "scores_ready", "bias_in_psum", "bias_added"))
        xh_ready, xl_ready, fh_ready, fl_ready = sem("xh_ready"), sem("xl_ready"), sem("fh_ready"), sem("fl_ready")
        uh_ready, ul_ready, dh_ready, dl_ready = (
            [sem(f"{n}{slot}_ready") for slot in range(2)] for n in ("uh", "ul", "dh", "dl"))
        gate_tanh, gate_set, kept_ready, shift_in_psum = sem("gate_tanh"), sem("gate_set"), sem("kept_ready"), sem("shift_in_psum")
        kv_in_psum, time_ready, kexp_ready, states_ready, out3_in_psum = (
            sem(n) for n in ("kv_in_psum", "time_ready", "kexp_ready", "states_ready", "out3_in_psum"))
        w5_loaded, permuted = sem("w5_loaded"), sem("permuted")
        dec_begun, dec_ready = sem("dec_begun"), sem("dec_ready")
        xb_ready, q_in_psum, k_in_psum, v_in_psum, u_in_psum = (
            sem(n) for n in ("xb_ready", "q_in_psum", "k_in_psum", "v_in_psum", "u_in_psum"))
        qtanh_ready, q_ready, ktanh_ready, k_ready, v_ready, u_ready = (
            sem(n) for n in ("qtanh_ready", "q_ready", "ktanh_ready", "k_ready", "v_ready", "u_ready"))
        qh_ready = [sem("qh0_ready"), sem("qh1_ready")]
        sc_in_psum, p_ready, o5_in_psum, osq_ready, oss_in_psum, oeps_ready, or_ready, uo_ready, out5_in_psum, x5_ready = (
            sem(n) for n in ("sc_in_psum", "p_ready", "o5_in_psum", "osq_ready", "oss_in_psum", "oeps_ready", "or_ready", "uo_ready",
                             "out5_in_psum", "x5_ready"))
        v_cleared = sem("v_cleared")
        silu_ready, pair_ready, biased_ready = sem("silu_ready"), sem("pair_ready"), sem("biased_ready")
        max_ready, recip_ready, av_ready = sem("max_ready"), sem("recip_ready"), sem("av_ready")
        xe_ready, xa_ready, s7_in_psum, s7_ready, e7_ready, et7_ready, av_in_psum, x7_ready = (
            sem(n) for n in ("xe_ready", "xa_ready", "s7_in_psum", "s7_ready", "e7_ready", "et7_ready", "av_in_psum", "x7_ready"))

        cum_rows = nc.dram_tensor("cum_rows", (NH, NT, P), FP32, kind="Internal").ap()

        def after(eng, sem, count):
            if not isinstance(count, int) or count > 0:
                eng.wait_ge(sem, count)

        def groups_of(eng, group):
            group(0, 0)
            with eng.Fori(0, (NG - 2) // 2) as i:
                group(2 * i + 1, 1)
                group(2 * i + 2, 0)
            group(NG - 1, 1)

        def at(i, n):
            return slice(i, i + n) if isinstance(i, int) else bass.ds(i, n)

        def sequences_of(eng, sequence):
            sequence(0)
            with eng.Fori(1, NB - 1) as b:
                sequence(b)
            sequence(NB - 1)

        def pairs_of(eng, f, pair):
            pair(0)
            with eng.Fori(1, f.pairs - 1) as i:
                pair(i)
            pair(f.pairs - 1)

        def split_product(ins_of, high, low, start=True, stop=True):
            (sh, mh), (sl, ml) = high, low
            ins_of(sh, mh, start, False)
            ins_of(sl, mh, False, False)
            return ins_of(sh, ml, False, stop)

        block = ctx.enter_context(nc.Block())

        @block.sync
        def _(sp):
            sp.dma_start(K[:, :], consts).then_inc(consts_loaded, 16)
            sp.dma_start(X[:, :, :], x.rearrange("(t p) d -> p t d", p=P)).then_inc(x_loaded, 16)
            sp.dma_start(WB[:, :, :], wbcdt).then_inc(wb_loaded, 16)
            sp.dma_start(COL[:, :, :], cols).then_inc(cols_loaded, 16)
            sp.dma_start(ROW[:, :], rows[0:3 * NH].partition_broadcast(P)).then_inc(rows_loaded, 16)

            def load_conv(g):
                sp.dma_start(WX[:, :, :], wx[g]).then_inc(wx_loaded, 16)
                sp.dma_start(CH[:, :, :], chan[g]).then_inc(chan_loaded, 16)

            def load_heads(g, slot):
                sp.dma_start(WZ[:, slot, :, :], wz[g]).then_inc(wz_loaded, 16)
                sp.dma_start(WO[:, slot, :, :], wout[g]).then_inc(wo_loaded, 16)
                sp.dma_start(NW[:, slot, :], inw[g]).then_inc(nw_loaded, 16)
                sp.dma_start(H0[:, slot, :], h0[g]).then_inc(h0_loaded, 16)

            def load_decays(g, c):
                src = cum_rows[bass.ds(g * GH, GH), c, :] if not isinstance(g, int) else cum_rows[g * GH:g * GH + GH, c, :]
                sp.dma_start(RB[:, c % 2, :, :], src.partition_broadcast(P)).then_inc(rb_loaded[c % 2], 16)

            load_conv(0)
            load_heads(0, 0)
            sp.wait_ge(cumt_ready, 2)
            sp.dma_start(cum_rows.rearrange("h t p -> h (t p)"), CUMT).then_inc(cumt_stored, 16)
            sp.wait_ge(cumt_stored, 16)
            sp.wait_ge(gt_in_psum, 2)
            load_decays(0, 0)
            load_decays(0, 1)

            def group(g, slot):
                last = isinstance(g, int) and g == NG - 1
                if not last:
                    sp.wait_ge(xc_ready, (g + 1) * NT)
                    load_conv(g + 1)
                for c in range(NT):
                    n = g * NT + c
                    if c == 2 and not last:
                        after(sp, o_added, n - 2)
                        load_heads(g + 1, 1 - slot)
                    sp.wait_ge(masked, n + 1)
                    if c < NT - 2:
                        load_decays(g, c + 2)
                    elif not last:
                        load_decays(g + 1, c + 2 - NT)

            groups_of(sp, group)
            sp.dma_start(SM[:, :, :], small).then_inc(small_loaded, 16)
            sp.dma_start(WG[:, :], wg6).then_inc(small_loaded, 16)
            sp.dma_start(BD[:, :], bd6).then_inc(small_loaded, 16)
            sp.dma_start(W3[:, :, :], w3).then_inc(small_loaded, 16)
            sp.dma_start(WO3[:, :], wo3).then_inc(small_loaded, 16)
            sp.dma_start(T3[:, :], t3).then_inc(small_loaded, 16)
            sp.dma_start(GATE[:, 0, :], rows[3 * NH:3 * NH + D].partition_broadcast(P)).then_inc(small_loaded, 16)
            sp.dma_start(SLOPE[:, :], rows[3 * NH + D:3 * NH + D + LH].partition_broadcast(P)).then_inc(small_loaded, 16)

            def load_experts(f, wu, wd):
                def up(e, slot):
                    sp.dma_start(WU[slot][:, 0:f.width], wu[e]).then_inc(wu_loaded[slot], 16)

                def down(e, slot):
                    sp.dma_start(WD[slot][:, :], wd[e]).then_inc(wd_loaded[slot], 16)

                for slot in range(2):
                    if f.s0:
                        sp.wait_ge(ul_ready[slot], f.p0)
                        sp.wait_ge(dl_ready[slot], f.p0)
                    up(slot, slot)
                    down(slot, slot)
                with sp.Fori(0, f.pairs - 1) as i:
                    for slot in range(2):
                        sp.wait_ge(ul_ready[slot], f.p0 + i + 1)
                        up(2 * i + 2 + slot, slot)
                        sp.wait_ge(dl_ready[slot], f.p0 + i + 1)
                        down(2 * i + 2 + slot, slot)

            load_experts(F2, wu2, wd2)
            sp.wait_ge(layer_done, 1)
            sp.dma_start(W5, w5).then_inc(w5_loaded, 16)
            sp.dma_start(WO5, wo5).then_inc(w5_loaded, 16)
            load_experts(F4, wu2, wd2)
            sp.wait_ge(layer_done, 4)
            for seg in range(4):
                for par in range(2):
                    r0 = 64 * (seg % 2) + par
                    sp.dma_start(OUT[32 * seg:32 * seg + 32, par::2, :],
                                 X[r0:r0 + 63:2, seg // 2::2, :]).then_inc(permuted, 16)
            load_experts(F6, wu6, wd6)
            load_experts(F8, wu6, wd6)
            sp.wait_ge(layer_done, 8)
            rows_of = out.rearrange("(b s j a) d -> b a (s j) d", b=NB, s=4, a=2)
            for t in range(NT):
                sp.dma_start(rows_of[t // 2, t % 2], X[:, t, :]).then_inc(out_stored, 16)
            sp.wait_ge(out_stored, 16 * NT)

        @block.gpsimd
        def _(pool):
            chain = Chain(pool, pool_self)

            def norm_scales(layer):
                for q in range(2):
                    s = slice(4 * q, 4 * q + 4)
                    pool.wait_ge(stats_ready, 2 * layer + q + 1)
                    chain.link(pool.tensor_scalar(rstd[:, s], mv[:, s, 1], LN_EPS, None, ALU.add))
                    ins = pool.tensor_tensor(rstd[:, s], rstd[:, s], half[:, s], op=ALU.pow)
                    if layer:
                        ins.then_inc(rstd_ready, 1)
                    else:
                        chain.link(ins)
                        chain.link(pool.tensor_tensor(rms[:, s], rstd[:, s], rstd[:, s], op=ALU.mult))
                        chain.link(pool.tensor_tensor(rms[:, s], rms[:, s], mv[:, s, 1], op=ALU.mult))
                        chain.link(pool.tensor_scalar(rms[:, s], rms[:, s], LN_EPS, None, ALU.add))
                        chain.link(pool.tensor_tensor(rms[:, s], rms[:, s], half[:, s], op=ALU.pow))
                        pool.tensor_tensor(rms[:, s], rms[:, s], rstd[:, s], op=ALU.mult).then_inc(rstd_ready, 1)

            def weights_up(f, pair, slot):
                w = 512 if f.gated else 256
                pool.wait_ge(uh_ready[slot], pair + 1)
                pool.tensor_tensor(UL[:, slot, 0:w], WU[slot][:, 0:w], UH[:, slot, 0:w].bitcast(FP32), op=ALU.subtract).then_inc(ul_ready[slot], 1)

            def weights_down(pair, slot):
                pool.wait_ge(dh_ready[slot], pair + 1)
                pool.tensor_tensor(DL[:, slot, :], WD[slot][:, :], DH[:, slot, :].bitcast(FP32), op=ALU.subtract).then_inc(dl_ready[slot], 1)

            def first_weights(f):
                for slot in range(2):
                    weights_up(f, f.p0, slot)
                    weights_down(f.p0, slot)

            def low_features(f):
                for q in range(4):
                    pool.wait_ge(xh_ready, 4 * f.n + q + 1)
                    s = slice(q * D, q * D + D)
                    pool.tensor_tensor(XL[:, :, s], XT[:, :, s], XH[:, :, s].bitcast(FP32), op=ALU.subtract).then_inc(xl_ready, 1)

            def decays(first_head, end):
                for h in range(first_head, end):
                    ins = pool.tensor_scalar(DEC[:, h, 0:D], dist, SLOPE[:, h:h + 1], None, ALU.mult)
                chain.link(ins)
                pool.tensor_tensor(DEC[:, first_head:end, 0:D], DEC[:, first_head:end, 0:D],
                                   DMASK[:, :].unsqueeze(1).to_broadcast([P, end - first_head, D]), op=ALU.add).then_inc(dec_begun, 1)

            def decays_begin():
                pool.wait_ge(small_loaded, SMALL)
                pool.memset(Y0[:, :, :], 0.0).then_inc(v_cleared, 1)
                chain.link(pool.tensor_scalar(SLOPE[:, :], SLOPE[:, :], -1.0, None, ALU.mult))
                chain.link(pool.tensor_scalar(DMASK[:, :], dist, 0.0, NEG, ALU.is_lt, ALU.mult))

            def low_parts(f):
                def low(s, r):
                    pool.wait_ge(fh_ready, s + 1)
                    pool.tensor_tensor(FL[:, r % 2, :], FG[:, r % 2, :], FH[:, r % 2, :].bitcast(FP32), op=ALU.subtract).then_inc(fl_ready, 1)

                def pair(i):
                    s, p = f.s0 + 4 * i, f.p0 + i
                    first, last = isinstance(i, int) and i == 0, isinstance(i, int) and i == f.pairs - 1
                    low(s, 0)
                    if last and f.n == 0:
                        decays_begin()
                    if last and f.n == 1:
                        decays(10, 12)
                    low(s + 1, 1)
                    if not first:
                        weights_down(p, 1)
                    if last and f.gated:
                        decays(*((0, 2), (12, 14))[f.n])
                    if not last:
                        weights_up(f, p + 1, 0)
                    low(s + 2, 2)
                    if last and f.gated:
                        decays(*((2, 4), (14, 16))[f.n])
                    low(s + 3, 3)
                    if not last:
                        weights_down(p + 1, 0)
                        weights_up(f, p + 1, 1)

                pairs_of(pool, f, pair)

            chain.link(pool.memset(half[:, :], -0.5))
            chain.link(pool.memset(XA[:, :], 1.0))
            pool.memset(XN[:, :, D:], 0.0)
            pool.memset(ones[:, :], 1.0).then_inc(masks_ready, 1)
            norm_scales(0)
            pool.memset(OUT[:, :, :], 0.0)

            def heads(ap):
                return ap.rearrange("p (h d) -> p h d", h=GH)

            def mask(n, c):
                pool.wait_ge(rb_loaded[c % 2], (n - c % 2) * 8 + 16)
                after(pool, mix_ready, n - 1)
                if c % 2 == 0:
                    after(pool, xs_ready, n // 2 if isinstance(n, int) else (n - c) // 2 + c // 2)
                pool.tensor_tensor(E[:, c % 2, :, :], RB[:, c % 2, :, :], CMASK[:, :].unsqueeze(1).to_broadcast([P, GH, P]),
                                   op=ALU.add).then_inc(masked, 1)

            def skip(n, c, slot):
                after(pool, y0_ready, n - 1)
                pool.tensor_tensor(heads(XD[:, c % 2, :]), heads(XTOK[:, slot, c, :]), Dg[:, slot, :].unsqueeze(2).to_broadcast([P, GH, HD]),
                                   op=ALU.mult).then_inc(xd_ready, 1)

            def to_end(g, c, slot):
                pool.wait_ge(decay_ready, g * NT + c + 1)
                after(pool, s_in_psum, g * NB + c // 2)
                pool.tensor_tensor(heads(XS[:, :]), heads(XTOK[:, slot, c, :]), E[:, c % 2, :, P - 1:P].to_broadcast([P, GH, HD]),
                                   op=ALU.mult).then_inc(xs_ready, 1)

            def gate(n, c):
                pool.wait_ge(y0_ready, n + 1)
                pool.wait_ge(y1_ready, n + 1)
                pool.tensor_tensor(Y1[:, c % 2, :], Y0[:, c % 2, :], Y1[:, c % 2, :], op=ALU.add).then_inc(y_ready, 1)
                pool.wait_ge(zsilu_ready, n + 1)
                pool.wait_ge(y_ready, n + 1)
                after(pool, g_in_psum, n - 1)
                pool.tensor_tensor(G[:, c % 2, :], Y1[:, c % 2, :], SZ[:, c % 2, :], op=ALU.mult).then_inc(gated_ready, 1)

            def norm_weights(g, slot):
                pool.wait_ge(wo_loaded, (g + 1) * 16)
                pool.wait_ge(nw_loaded, (g + 1) * 16)
                pool.tensor_tensor(WO[:, slot, :, :], WO[:, slot, :, :],
                                   NW[:, slot, :].unsqueeze(2).to_broadcast([P, GC, D]), op=ALU.mult).then_inc(wo_ready, 1)

            def group(g, slot):
                first, last = isinstance(g, int) and g == 0, isinstance(g, int) and g == NG - 1
                for c in range(NT):
                    n = g * NT + c
                    if c % 2 == 0:
                        to_end(g, c, slot)
                    if not (first and c == 0):
                        gate(n - 1, (c - 1) % NT)
                    if c == 4 and not last:
                        norm_weights(g + 1, 1 - slot)
                    if not (last and c == NT - 1):
                        mask(n + 1, (c + 1) % NT)
                        if c == NT - 1:
                            pool.wait_ge(group_ready, g + 2)
                            pool.wait_ge(xtok_ready, (g + 2) * NT)
                        skip(n + 1, (c + 1) % NT, slot if c < NT - 1 else 1 - slot)

            norm_weights(0, 0)
            pool.wait_ge(masks_ready, 2)
            mask(0, 0)
            pool.wait_ge(group_ready, 1)
            pool.wait_ge(xtok_ready, NT)
            skip(0, 0, 0)
            groups_of(pool, group)
            gate(NG * NT - 1, NT - 1)
            pool.wait_ge(ss_ready, 1)
            chain.link(pool.tensor_scalar(SS[:, :], SS[:, :], 1.0 / DI, LN_EPS, ALU.mult, ALU.add))
            pool.tensor_tensor(SS[:, :], SS[:, :], half[:, :], op=ALU.pow).then_inc(rms_ready, 1)

            first_weights(F2)
            norm_scales(1)
            low_features(F2)
            low_parts(F2)
            norm_scales(2)
            pool.wait_ge(gate_set, 1)
            for t in range(NT):
                pool.wait_ge(xn_ready, NT * 2 + t + 1)
                pool.tensor_tensor(OUT[:, t, :], XN[:, t, 0:D], GATE[:, 1, :], op=ALU.mult).then_inc(kept_ready, 1)
            norm_scales(3)
            decays(4, 10)
            for f in range(4, 9):
                feed = {4: F4, 6: F6, 8: F8}.get(f)
                if feed:
                    first_weights(feed)
                norm_scales(f)
                if feed:
                    low_features(feed)
                    low_parts(feed)
                if f == 5:
                    def heads_alone(b):
                        pool.wait_ge(q_ready, b + 1)
                        pool.tensor_tensor(QH[1], QT[:, 1, :].unsqueeze(1).to_broadcast([P, 8, D]),
                                           own_head.unsqueeze(2).to_broadcast([P, 8, D]), op=ALU.mult).then_inc(qh_ready[1], 1)

                    def norm_out(b):
                        pool.wait_ge(oeps_ready, b + 1)
                        pool.tensor_tensor(sso[:, :], sso[:, :], half[:, 0:2], op=ALU.pow).then_inc(or_ready, 1)

                    def sequence(b):
                        if not (isinstance(b, int) and b == 0):
                            norm_out(b - 1)
                        if not (isinstance(b, int) and b == NB - 1):
                            pool.wait_ge(sc_in_psum, 8 * b + 8)
                            heads_alone(b + 1)

                    heads_alone(0)
                    sequences_of(pool, sequence)
                    norm_out(NB - 1)
                if f == 7:
                    heads = XN[:, :, 0:D].rearrange("p t (h a d) -> p t h a d", a=2, d=LD)
                    for t in range(NT):
                        pool.wait_ge(xn_ready, NT * 7 + t + 1)
                        xa = XA[:, t * AW:(t + 1) * AW].rearrange("p (h d) -> p h d", h=8)
                        pool.tensor_copy(xa[:, :, 0:LD], heads[:, t, :, t % 2, :]).then_inc(xa_ready, 1)
                    for t in range(NT):
                        pool.wait_ge(xt_ready, 4 * 7 + t // 2 + 1)
                        if t >= 2:
                            pool.wait_ge(s7_in_psum, t - 1)
                        pool.tensor_tensor(XE[:, t % 2, :, :, :], XT[:, :, t * P:t * P + P].unsqueeze(2).to_broadcast([P, KD, 4, P]),
                                           own_rows.unsqueeze(1).unsqueeze(3).to_broadcast([P, KD, 4, P]), op=ALU.mult).then_inc(xe_ready, 1)

        @block.scalar
        def _(act):
            chain = Chain(act, act_self)

            def xt_out(layer, scale=None, bias=None, feed=None):
                for q in range(NT // 2):
                    act.wait_ge(xt_in_psum, 4 * layer + q + 1)
                    for k in range(KD):
                        ins = act.activation(XT[:, k, q * 256:q * 256 + 256], PS[6 + q % 2][:, k * 256:k * 256 + 256],
                                             ACT.Identity, bias=bias(k) if bias else 0.0, scale=scale(k) if scale else 1.0)
                    ins.then_inc(xt_ready, 1)
                    if feed:
                        act.wait_ge(xt_ready, 4 * layer + q + 1)
                        s = slice(q * D, q * D + D)
                        act.copy(XH[:, :, s], XT[:, :, s]).then_inc(xh_ready, 1)

            act.wait_ge(cols_loaded, 16)
            xt_out(0, scale=lambda k: COL[:, 0, k:k + 1])

            def conv_in(m, u, bank=0):
                if u == 0:
                    act.wait_ge(chan_loaded, m * 2 + 16)
                act.wait_ge(up_in_psum, m + 1)
                after(act, conv_done, m - 1)
                act.copy(XP[:, u % 2, :, 0:TAPS - 1], CH[:, u // 2, TAPS + 1:2 * TAPS].unsqueeze(1).to_broadcast([P, 2, TAPS - 1]))
                act.copy(XP[:, u % 2, :, TAPS - 1:], PS[bank].rearrange("p (b t) -> p b t", b=2)).then_inc(xp_ready, 1)
                act.wait_ge(xp_ready, m + 1)
                after(act, xc_ready, m - 1)
                act.activation(CV[:, u % 2, :, :], XP[:, u % 2, :, TAPS - 1:], ACT.Identity,
                               scale=CH[:, u // 2, TAPS - 1:TAPS], bias=CH[:, u // 2, TAPS:TAPS + 1]).then_inc(conv_begun, 1)

            def conv_tanh(m, u):
                act.wait_ge(conv_done, m + 1)
                after(act, xc_in_psum, m - 1)
                act.activation(TH[:, u % 2, :, :], CV[:, u % 2, :, :], ACT.Tanh, scale=0.5).then_inc(tanh_done, 1)

            def tokens_out(m, u, slot, bank=1):
                act.wait_ge(xc_in_psum, m + 1)
                act.activation(XTOK[:, slot, 4 * (u % 2):4 * (u % 2) + 4, (u // 2) * P:(u // 2) * P + P],
                               PS[bank].rearrange("p (t c) -> p t c", t=4), ACT.Copy, scale=0.5).then_inc(xtok_ready, 1)

            def b_and_c_out(n):
                act.wait_ge(bc_in_psum, n + 1)
                act.copy((BT, CT)[n // 2][:, (n % 2) * 512:(n % 2) * 512 + 512], PS[n]).then_inc(bc_ready, 1)

            def softplus():
                act.wait_ge(rows_loaded, 16)
                act.activation(eA[:, :], ROW[:, NH:2 * NH], ACT.Exp).then_inc(ea_ready, 1)
                act.wait_ge(softplus_step, 1)
                chain.link(act.activation(dta[:, :, :], dta[:, :, :], ACT.Exp, scale=-1.0))
                act.activation(dta[:, :, :], dta[:, :, :], ACT.Ln, bias=1.0).then_inc(softplus_step, 1)

            def cumulative_out():
                act.wait_ge(cum_in_psum, 2)
                for q in range(2):
                    act.wait_ge(cumt_in_psum, q + 1)
                    act.copy(CUMT[:, q * 512:q * 512 + 512], PS[2 + q][0:NH, :]).then_inc(cumt_ready, 1)
                act.activation(ncum[:, :, :].rearrange("p t h -> p (t h)"), PS[0][:, 0:NT * NH], ACT.Copy, scale=-1.0).then_inc(cum_ready, 1)
                act.activation(ecum[:, :, :].rearrange("p t h -> p (t h)"), PS[0][:, 0:NT * NH], ACT.Exp).then_inc(cum_ready, 1)
                act.activation(eend[:, :, :].rearrange("p t h -> p (t h)"), PS[1][:, 0:NT * NH], ACT.Exp).then_inc(cum_ready, 1)

            for u in range(NT + 3):
                if u >= 3:
                    tokens_out(u - 3, u - 3, 0, 4 + (u - 3) % 2)
                if u < NT:
                    conv_in(u, u, 6 + u % 2)
                if 1 <= u <= NT:
                    conv_tanh(u - 1, u - 1)
                if u < 4:
                    b_and_c_out(u)
                if u == 5:
                    softplus()
                if u == 6:
                    for q in range(2):
                        act.wait_ge(gt_in_psum, q + 1)
                        act.copy(GT[:, 4 * q:4 * q + 4, :].rearrange("p t s -> p (t s)"), PS[2 + q]).then_inc(gt_ready, 1)
                if u == 8:
                    cumulative_out()

            def decay(n, c, slot):
                act.wait_ge(masked, n + 1)
                for h in range(GH):
                    ins = act.activation(E[:, c % 2, h, :], E[:, c % 2, h, :], ACT.Exp, bias=GRP[:, slot, 0, c, h:h + 1])
                ins.then_inc(decay_ready, 1)

            def gated_out(n, c):
                act.wait_ge(g_in_psum, n + 1)
                after(act, o_in_psum, n - 1)
                act.copy(GTR[:, c % 2, :], PS[6]).then_inc(gtr_ready, 1)

            def squares(n, c, slot):
                act.wait_ge(y_ready, n + 1)
                after(act, squares_ready, n)
                act.activation(junk[:, :], Y1[:, c % 2, :], ACT.Square, accum_out=SQ[:, slot, c:c + 1]).then_inc(squares_ready, 1)

            def group(g, slot):
                first, last = isinstance(g, int) and g == 0, isinstance(g, int) and g == NG - 1
                for c in range(NT):
                    n = g * NT + c
                    if first and c == 0:
                        act.wait_ge(group_ready, 1)
                        decay(0, 0, 0)
                    act.wait_ge(z_in_psum, n + 1)
                    after(act, gated_ready, n - 1)
                    act.activation(SZ[:, c % 2, :], PS[4], ACT.Tanh, scale=0.5).then_inc(ztanh_ready, 1)
                    if not last:
                        conv_in(n + NT, c)
                    if c and not last:
                        tokens_out(n + NT - 1, c - 1, 1 - slot)
                    if not (first and c == 0):
                        squares(n - 1, (c - 1) % NT, slot if c else 1 - slot)
                    if not (first and c == 0):
                        gated_out(n - 1, (c - 1) % NT)
                    if not last:
                        conv_tanh(n + NT, c)
                    if not (last and c == NT - 1):
                        if c == NT - 1:
                            act.wait_ge(group_ready, g + 2)
                        decay(n + 1, (c + 1) % NT, slot if c < NT - 1 else 1 - slot)
                if not last:
                    tokens_out(n + NT, NT - 1, 1 - slot)

            groups_of(act, group)
            n = NG * NT - 1
            gated_out(n, NT - 1)
            squares(n, NT - 1, 1)

            def weights_up(f, pair, slot):
                w = 512 if f.gated else 256
                act.wait_ge(wu_loaded[slot], 16 * (pair + 1))
                if not f.gated:
                    act.copy(BIAS[:, slot:slot + 1], WU[slot][:, 256:257])
                act.copy(UH[:, slot, 0:w], WU[slot][:, 0:w]).then_inc(uh_ready[slot], 1)

            def weights_down(pair, slot):
                act.wait_ge(wd_loaded[slot], 16 * (pair + 1))
                act.copy(DH[:, slot, :], WD[slot][:, :]).then_inc(dh_ready[slot], 1)

            def first_weights(f):
                if f.n == 0:
                    act.wait_ge(o_in_psum, NG * NT)
                else:
                    act.wait_ge(down_in_psum, f.s0)
                    if not f.gated:
                        act.wait_ge(layer_done, f.norm - 1)
                for slot in range(2):
                    weights_up(f, f.p0, slot)
                    weights_down(f.p0, slot)

            def experts(f):
                if not f.gated:
                    for q in range(2):
                        act.wait_ge(hop_in_psum, 2 * (f.n - 2) + q + 1)
                        act.activation(TT[:, q * 512:q * 512 + 512], PS[4 + q][0:8, :], ACT.Tanh).then_inc(hop_ready, 1)

                def router_exp():
                    act.wait_ge(logits_ready, 2 * f.n + 1)
                    act.activation(LR[:, :, 0:f.routed], LR[:, :, 0:f.routed], ACT.Exp).then_inc(logits_ready, 1)

                def early(s):
                    return isinstance(s, int) and s < f.s0 + 2

                def hidden(s, r):
                    act.wait_ge(hidden_in_psum, s + 1)
                    if not early(s):
                        act.wait_ge(gate_ready, s - 1)
                    if f.gated:
                        act.activation(FT[:, r % 2, :], PS[2 * (r % 2)], ACT.Tanh, scale=0.5).then_inc(act_ready, 1)
                    else:
                        if not early(s):
                            act.wait_ge(fl_ready, s - 1)
                        act.wait_ge(uh_ready[r // 2], f.p0 + (s - f.s0) // 4 + 1 if isinstance(s, int) else (s - r) // 4 + 1)
                        act.activation(FG[:, r % 2, :], PS[2 * (r % 2)], ACT.Identity,
                                       bias=BIAS[:, r // 2:r // 2 + 1]).then_inc(biased_ready, 1)
                        act.wait_ge(biased_ready, s - F6.s0 + 1)
                        act.activation(FT[:, r % 2, :], FG[:, r % 2, :], ACT.Tanh, scale=0.5).then_inc(act_ready, 1)

                def high(s, r):
                    act.wait_ge(gate_ready, s + 1)
                    if not early(s):
                        act.wait_ge(down_in_psum, s - 1)
                    act.copy(FH[:, r % 2, :], FG[:, r % 2, :]).then_inc(fh_ready, 1)

                def pair(i):
                    s, p = f.s0 + 4 * i, f.p0 + i
                    first, last = isinstance(i, int) and i == 0, isinstance(i, int) and i == f.pairs - 1
                    hidden(s, 0)
                    high(s, 0)
                    hidden(s + 1, 1)
                    high(s + 1, 1)
                    if first:
                        router_exp()
                    if not first:
                        act.wait_ge(down_in_psum, s)
                        weights_down(p, 1)
                    if not last:
                        weights_up(f, p + 1, 0)
                    hidden(s + 2, 2)
                    high(s + 2, 2)
                    hidden(s + 3, 3)
                    high(s + 3, 3)
                    if not last:
                        act.wait_ge(down_in_psum, s + 2)
                        weights_down(p + 1, 0)
                        weights_up(f, p + 1, 1)
                    if first and not f.gated:
                        for q in range(2):
                            act.wait_ge(scores_in_psum, 2 * (f.n - 2) + q + 1)
                            act.copy(SCT[:, q * 512:q * 512 + 512], PS[1 + 2 * q][0:8, :]).then_inc(scores_ready, 1)

                pairs_of(act, f, pair)

            first_weights(F2)
            xt_out(1, feed=F2)
            experts(F2)
            act.wait_ge(small_loaded, SMALL)
            act.activation(GATE[:, 0, :], GATE[:, 0, :], ACT.Tanh, scale=0.5).then_inc(gate_tanh, 1)
            act.wait_ge(small_loaded, SMALL)
            act.activation(T3[:, :], T3[:, :], ACT.Exp).then_inc(gate_tanh, 1)
            xt_out(2)
            xt_out(3, scale=lambda k: COL[:, 1, k:k + 1], bias=lambda k: COL[:, 2, k:k + 1])
            act.wait_ge(time_ready, 1)
            for q in range(2):
                s = slice(q * 512, q * 512 + 512)
                act.wait_ge(kv_in_psum, q + 1)
                act.activation(KS[:, s], PS[q][0:64, :], ACT.Tanh, scale=0.5).then_inc(kexp_ready, 1)
                act.wait_ge(kexp_ready, 2 * q + 1)
                act.activation(KS[:, s], KS[:, s], ACT.Exp, scale=T3[:, 1:2], bias=T3[:, 1:2]).then_inc(kexp_ready, 1)
            first_weights(F4)
            xt_out(4, feed=F4)
            experts(F4)
            act.wait_ge(dec_begun, 6)
            act.activation(DEC[:, :, D:], DEC[:, :, 0:P], ACT.Exp).then_inc(dec_ready, 1)
            act.wait_ge(dec_ready, 1)
            act.activation(DEC[:, :, 0:D], DEC[:, :, 0:D], ACT.Exp).then_inc(dec_ready, 1)
            xt_out(5)
            act.wait_ge(xt_ready, 4 * 6)
            act.wait_ge(v_cleared, 1)

            def features(b):
                act.copy(XB, XT[:, :, at(b * D, D)]).then_inc(xb_ready, 1)

            def queries(b):
                act.wait_ge(q_in_psum, b + 1)
                act.activation(QT, PS[6].rearrange("p (g t) -> p g t", g=2), ACT.Tanh, scale=0.5).then_inc(qtanh_ready, 1)

            def heads_alone(b):
                act.wait_ge(q_ready, b + 1)
                for j in range(8):
                    ins = act.activation(QH[0][:, j, :], QT[:, 0, :], ACT.Copy, scale=own_head[:, j:j + 1])
                    if j % 2:
                        ins.then_inc(qh_ready[0], 1)

            def keys(b):
                act.wait_ge(k_in_psum, b + 1)
                act.activation(KT, PS[7].rearrange("p (g t) -> p g t", g=2), ACT.Tanh, scale=0.5).then_inc(ktanh_ready, 1)

            def values_out(b):
                act.wait_ge(v_in_psum, b + 1)
                v = PS[5].rearrange("p (c h a d) -> p c h a d", c=2, a=2, d=LD)
                for par in range(2):
                    ins = act.activation(V5[:, :, par::2, par * LD:par * LD + LD], v[:, :, :, par, :], ACT.Copy, scale=0.25)
                ins.then_inc(v_ready, 1)

            def gates_out(b):
                act.wait_ge(u_in_psum, b + 1)
                act.copy(UT, PS[6]).then_inc(u_ready, 1)

            def sequence(b):
                last = isinstance(b, int) and b == NB - 1
                if not last:
                    features(b + 1)
                    act.wait_ge(qh_ready[0], 4 * b + 4)
                    act.wait_ge(qh_ready[1], b + 1)
                    queries(b + 1)
                    act.wait_ge(sc_in_psum, 8 * b + 4)
                    heads_alone(b + 1)
                    act.wait_ge(sc_in_psum, 8 * b + 8)
                    keys(b + 1)
                act.wait_ge(o5_in_psum, 8 * b + 8)
                after(act, oss_in_psum, b)
                act.activation(OSQ, PS[4], ACT.Square, scale=1.0 / 16).then_inc(osq_ready, 1)
                if not last:
                    values_out(b + 1)
                    act.wait_ge(uo_ready, b + 1)
                    gates_out(b + 1)

            features(0)
            queries(0)
            keys(0)
            heads_alone(0)
            values_out(0)
            gates_out(0)
            sequences_of(act, sequence)
            first_weights(F6)
            xt_out(6, feed=F6)
            experts(F6)
            xt_out(7)
            for n in range(NT):
                act.wait_ge(s7_ready, n + 1)
                act.activation(E[:, n % 2, :, :], E[:, n % 2, :, :], ACT.Exp, scale=0.25).then_inc(e7_ready, 1)
            first_weights(F8)
            xt_out(8, feed=F8)
            experts(F8)

        @block.vector
        def _(dve):
            chain = Chain(dve, dve_self)

            def statistics(q, src=X):
                for t in range(4 * q, 4 * q + 4):
                    ins = dve.bn_stats(bn[:, t, :], src[:, t, :])
                chain.link(ins)
                for t in range(4 * q, 4 * q + 4):
                    ins = dve.bn_aggr(mv[:, t, :], bn[:, t, :])
                ins.then_inc(stats_ready, 1)

            def layer_norm(layer, src=X, begun=False):
                for q in range(1 if begun else 0, 2):
                    statistics(q, src)
                for t in range(NT):
                    if t % 4 == 0:
                        dve.wait_ge(rstd_ready, 2 * layer + t // 4 + 1)
                    dve.tensor_scalar(XN[:, t, 0:D], src[:, t, :], mv[:, t, 0:1], (rstd if layer else rms)[:, t:t + 1],
                                      ALU.subtract, ALU.mult).then_inc(xn_ready, 1)

            dve.wait_ge(consts_loaded, 16)
            dve.tensor_copy(identb[:, :], ident)
            dve.tensor_scalar(CMASK[:, :], tri, 1.0, -NEG, ALU.subtract, ALU.mult).then_inc(masks_ready, 1)
            dve.wait_ge(x_loaded, 16)
            layer_norm(0)
            for t in range(NT):
                ins = dve.tensor_scalar(XTOK[:, 1, t, 0:D], X[:, t, :], mv[:, t, 0:1], rstd[:, t:t + 1], ALU.subtract, ALU.mult)
            chain.link(ins)
            dve.tensor_tensor(X[:, :, :], X[:, :, :], XTOK[:, 1, :, 0:D], op=ALU.add)

            def heads(ap):
                return ap.rearrange("p (h d) -> p h d", h=GH)

            def conv_taps(m, u):
                dve.wait_ge(conv_begun, m + 1)
                for tap in range(TAPS - 1):
                    if tap:
                        dve.wait_ge(conv_tap, (TAPS - 2) * m + tap)
                    dve.scalar_tensor_tensor(CV[:, u % 2, :, :], XP[:, u % 2, :, tap:tap + D], CH[:, u // 2, tap:tap + 1],
                                             CV[:, u % 2, :, :], ALU.mult, ALU.add).then_inc(conv_done if tap == TAPS - 2 else conv_tap, 1)

            def conv_silu(m, u):
                dve.wait_ge(tanh_done, m + 1)
                dve.scalar_tensor_tensor(TH[:, u % 2, :, :], TH[:, u % 2, :, :], 1.0, CV[:, u % 2, :, :],
                                         ALU.add, ALU.mult).then_inc(xc_ready, 1)

            def group_scalars(g, slot):
                at = bass.ds(g * GH, GH) if not isinstance(g, int) else slice(g * GH, g * GH + GH)
                row = bass.ds(g * GH + 2 * NH, GH) if not isinstance(g, int) else slice(2 * NH + g * GH, 2 * NH + g * GH + GH)
                dve.tensor_copy(Dg[:, slot, :], ROW[:, row])
                for k, src in enumerate((ncum, ecum, eend)):
                    ins = dve.tensor_copy(GRP[:, slot, k, :, :], src[:, :, at])
                ins.then_inc(group_ready, 1)
                dve.wait_ge(group_ready, g + 1)

            def add_out(n, c):
                dve.wait_ge(o_in_psum, n + 1)
                dve.tensor_tensor(OUT[:, c, :], PS[7][:, 0:D], OUT[:, c, :], op=ALU.add).then_inc(o_added, 1)

            def add_squares(g, slot):
                dve.wait_ge(squares_ready, (g + 1) * NT)
                dve.tensor_tensor(SS[:, :], SQ[:, slot, :], SS[:, :], op=ALU.add).then_inc(squares_added, 1)
                dve.wait_ge(squares_added, g + 1)

            def group(g, slot):
                first, last = isinstance(g, int) and g == 0, isinstance(g, int) and g == NG - 1
                dve.wait_ge(h0_loaded, (g + 1) * 16)
                for c in range(NT):
                    n = g * NT + c
                    dve.wait_ge(decay_ready, n + 1)
                    after(dve, y_in_psum, n - 1)
                    dve.tensor_tensor(M[:, c % 2, :, :], E[:, c % 2, :, :],
                                      GT[:, c, :].unsqueeze(1).to_broadcast([P, GH, P]), op=ALU.mult).then_inc(mix_ready, 1)
                    dve.wait_ge(ztanh_ready, n + 1)
                    dve.scalar_tensor_tensor(SZ[:, c % 2, :], SZ[:, c % 2, :], 1.0, PS[4],
                                             ALU.add, ALU.mult).then_inc(zsilu_ready, 1)
                    if not (first and c < 2):
                        add_out(n - 2, (c - 2) % NT)
                    if c % 2 == 0:
                        after(dve, i_in_psum, n)
                        dve.tensor_tensor(heads(H1[:, :]), heads(H0[:, slot, :]), GRP[:, slot, 2, c, :].unsqueeze(2).to_broadcast([P, GH, HD]),
                                          op=ALU.mult).then_inc(h1_begun, 1)
                    if not last:
                        conv_taps(n + NT, c)
                    if c == 2 and not first:
                        add_squares(g - 1, 1 - slot)
                    dve.wait_ge(y_in_psum, n + 1)
                    dve.wait_ge(xd_ready, n + 1)
                    after(dve, y_ready, n - 1)
                    dve.tensor_tensor(Y0[:, c % 2, :], PS[2], XD[:, c % 2, :], op=ALU.add).then_inc(y0_ready, 1)
                    if c % 2 == 0:
                        dve.wait_ge(s_in_psum, g * NB + c // 2 + 1)
                        dve.wait_ge(h1_begun, g * NB + c // 2 + 1)
                        dve.tensor_tensor(H1[:, :], PS[5], H1[:, :], op=ALU.add).then_inc(h1_ready, 1)
                    if c == NT - 2 and not last:
                        group_scalars(g + 1, 1 - slot)
                    if not last:
                        conv_silu(n + NT, c)
                    dve.wait_ge(i_in_psum, n + 1)
                    after(dve, squares_ready, n - 1)
                    after(dve, gated_ready, n - 1)
                    dve.tensor_tensor(heads(Y1[:, c % 2, :]), heads(PS[3]),
                                      GRP[:, slot, 1, c, :].unsqueeze(2).to_broadcast([P, GH, HD]), op=ALU.mult).then_inc(y1_ready, 1)

            def step_sizes_in(q):
                dve.wait_ge(bdt_in_psum, q + 1)
                b = PS[q].rearrange("p (t n) -> p t n", t=2)
                dve.tensor_copy(BN[:, q, :], b[:, 0, 0:NS])
                if q == 0:
                    dve.wait_ge(rows_loaded, 16)
                return dve.tensor_tensor(dtr[:, 2 * q:2 * q + 2, :], b[:, :, NS:NS + NH],
                                         ROW[:, 0:NH].unsqueeze(1).to_broadcast([P, 2, NH]), op=ALU.add).then_inc(b_ready, 1)

            for u in range(NT + 1):
                if u < NT:
                    conv_taps(u, u)
                if u:
                    conv_silu(u - 1, u - 1)
                if 1 <= u <= 4:
                    step_sizes_in(u - 1)
                if u == 4:
                    dve.wait_ge(b_ready, 4)
                    dve.scalar_tensor_tensor(dta[:, :, :], dtr[:, :, :], -1.0, dtr[:, :, :], ALU.mult, ALU.max).then_inc(softplus_step, 1)
                if u == 6:
                    dve.wait_ge(softplus_step, 2)
                    chain.link(dve.scalar_tensor_tensor(dtr[:, :, :], dtr[:, :, :], 0.0, dta[:, :, :], ALU.max, ALU.add))
                    dve.wait_ge(ea_ready, 1)
                    dve.scalar_tensor_tensor(dA[:, :, :], dtr[:, :, :], -1.0, eA[:, :].unsqueeze(1).to_broadcast([P, NT, NH]),
                                             ALU.mult, ALU.mult).then_inc(da_ready, 1)
                if u == 7:
                    dve.wait_ge(gt_ready, 2)
                    for q in range(2):
                        dve.tensor_tensor(GT[:, 4 * q:4 * q + 4, :], GT[:, 4 * q:4 * q + 4, :],
                                          tri.unsqueeze(1).to_broadcast([P, 4, P]), op=ALU.mult)
                    chain.link(dve.memset(SS[:, :], 0.0))
            dve.wait_ge(cum_ready, 3)
            group_scalars(0, 0)
            groups_of(dve, group)
            add_out(NG * NT - 2, NT - 2)
            add_out(NG * NT - 1, NT - 1)
            add_squares(NG - 1, 1)
            dve.sem_inc(ss_ready, 1)
            dve.wait_ge(rms_ready, 1)
            chain.link(dve.tensor_scalar(SS[:, :], SS[:, :], 0.5, None, ALU.mult))
            for t in range(NT):
                ins = dve.scalar_tensor_tensor(X[:, t, :], OUT[:, t, :], SS[:, t:t + 1], X[:, t, :], ALU.mult, ALU.add)
            ins.then_inc(layer_done, 1)

            def route(f):
                n, w, k = f.routed, f.routed + 8 - f.top, f.top
                chain.link(dve.memset(LG[:, :, n:w], TINY))
                dve.wait_ge(logits_in_psum, f.n + 1)
                chain.link(dve.tensor_copy(LG[:, :, 0:n], PS[4][:, 0:NT * n].rearrange("p (t e) -> p t e", t=NT)))
                for t in range(NT):
                    ins = dve.max(MX[:, t, :], LG[:, t, 0:n])
                chain.link(ins)
                dve.tensor_tensor(LR[:, :, 0:n], LG[:, :, 0:n], MX[:, :, 0:1].to_broadcast([P, NT, n]),
                                  op=ALU.subtract).then_inc(logits_ready, 1)
                chain.link(dve.memset(MX[:, :, k:8], TINY))
                for t in range(NT):
                    ins = dve.match_replace(LG[:, t, 0:w], MX[:, t, :], LG[:, t, 0:w], TAKEN)
                chain.link(ins)
                chain.link(dve.tensor_scalar(LG[:, :, 0:n], LG[:, :, 0:n], TAKEN, None, ALU.is_equal))
                dve.wait_ge(logits_ready, 2 * f.n + 2)
                chain.link(dve.tensor_tensor(LR[:, :, 0:n], LR[:, :, 0:n], LG[:, :, 0:n], op=ALU.mult))
                chain.link(dve.tensor_reduce(SUM[:, :], LR[:, :, 0:n], AX.X, ALU.add))
                chain.link(dve.reciprocal(SUM[:, :], SUM[:, :]))
                ins = dve.tensor_tensor(LR[:, :, 0:n], LR[:, :, 0:n], SUM[:, :].unsqueeze(2).to_broadcast([P, NT, n]), op=ALU.mult)
                if not f.gated:
                    ins.then_inc(weights_ready, 1)
                    dve.wait_ge(weights_ready, f.n - 1)
                else:
                    chain.link(ins)
                share = k / (k + 1) if f.shared else 1.0
                ins = dve.tensor_scalar(CW[:, 0:n, :], LR[:, :, 0:n].rearrange("p t e -> p e t"), 0.5 * share, None, ALU.mult)
                if f.shared:
                    chain.link(ins)
                    ins = dve.memset(CW[:, n:n + f.shared, :], 0.5 / (k + 1))
                chain.link(ins)

            def experts(f):
                def add_biases():
                    dve.wait_ge(down_added, f.s0 + 4 * f.pairs - 2)
                    for q in range(4):
                        dve.wait_ge(bias_in_psum, 4 * (f.n - 2) + q + 1)
                        ins = dve.tensor_tensor(X[:, 2 * q:2 * q + 2, :].rearrange("p t d -> p (t d)"), PS[1 + 2 * (q % 2)],
                                                X[:, 2 * q:2 * q + 2, :].rearrange("p t d -> p (t d)"), op=ALU.add)
                        ins.then_inc(bias_added, 1)
                    dve.wait_ge(bias_added, 4 * (f.n - 1))

                def gate(s, r):
                    dve.wait_ge(act_ready, s + 1)
                    if not (isinstance(s, int) and s < f.s0 + 2):
                        dve.wait_ge(fl_ready, s - 1)
                    if f.gated:
                        dve.scalar_tensor_tensor(FT[:, r % 2, :], FT[:, r % 2, :], 1.0, PS[2 * (r % 2)],
                                                 ALU.add, ALU.mult).then_inc(silu_ready, 1)
                        dve.wait_ge(silu_ready, s + 1)
                        dve.tensor_tensor(FG[:, r % 2, :], PS[2 * (r % 2) + 1], FT[:, r % 2, :], op=ALU.mult).then_inc(gate_ready, 1)
                    else:
                        dve.scalar_tensor_tensor(FG[:, r % 2, :], FT[:, r % 2, :], 1.0, FG[:, r % 2, :],
                                                 ALU.add, ALU.mult).then_inc(gate_ready, 1)

                def add(s, r):
                    dve.wait_ge(down_in_psum, s + 1)
                    if not (isinstance(s, int) and s < f.s0 + 2):
                        dve.wait_ge(down_added, s - 1)
                    for t in range(4):
                        tile = 4 * (r % 2) + t
                        ins = dve.scalar_tensor_tensor(X[:, tile, :], PS[4 + 2 * (r % 2) + t // 2][:, (t % 2) * D:(t % 2) * D + D],
                                                       CWP[:, r // 2, tile:tile + 1], X[:, tile, :], ALU.mult, ALU.add)
                    ins.then_inc(down_added, 1)

                def pair_weights(i):
                    dve.tensor_copy(CWP[:, :, :], CW[:, at(2 * i, 2), :]).then_inc(pair_ready, 1)
                    dve.wait_ge(pair_ready, f.p0 + i + 1)

                def pair(i):
                    s = f.s0 + 4 * i
                    first = isinstance(i, int) and i == 0
                    for r in range(2):
                        gate(s + r, r)
                        if not first:
                            add(s + r - 2, r + 2)
                    if first:
                        route(f)
                    else:
                        dve.wait_ge(down_added, s)
                    pair_weights(i)
                    for r in range(2, 4):
                        gate(s + r, r)
                        add(s + r - 2, r - 2)

                pairs_of(dve, f, pair)
                if not f.gated:
                    add_biases()
                end = f.s0 + 4 * f.pairs
                add(end - 2, 2)
                if f.n < 3:
                    dve.wait_ge(down_added, end - 1)
                    statistics(0)
                add(end - 1, 3)
                dve.wait_ge(down_added, end)
                dve.sem_inc(layer_done, 1)

            dve.wait_ge(layer_done, 1)
            layer_norm(1)
            experts(F2)
            dve.wait_ge(gate_tanh, 2)
            chain.link(dve.tensor_scalar(GATE[:, 0, :], GATE[:, 0, :], 0.5, 0.5, ALU.mult, ALU.add))
            dve.tensor_scalar(GATE[:, 1, :], GATE[:, 0, :], -1.0, 1.0, ALU.mult, ALU.add).then_inc(gate_set, 1)
            dve.tensor_scalar(T3[:, 1:2], T3[:, 1:2], -0.5, None, ALU.mult).then_inc(time_ready, 1)
            layer_norm(2, begun=True)
            for q in range(4):
                dve.wait_ge(shift_in_psum, q + 1)
                if q == 0:
                    dve.wait_ge(gate_set, 1)
                dve.wait_ge(kept_ready, 2 * q + 2)
                chain.link(dve.tensor_tensor(SZ[:, q % 2, :].rearrange("p (t d) -> p t d", t=2), PS[q].rearrange("p (t d) -> p t d", t=2),
                                             GATE[:, 0, :].unsqueeze(1).to_broadcast([P, 2, D]), op=ALU.mult))
                ins = dve.tensor_tensor(OUT[:, 2 * q:2 * q + 2, :].rearrange("p t d -> p (t d)"), SZ[:, q % 2, :],
                                        OUT[:, 2 * q:2 * q + 2, :].rearrange("p t d -> p (t d)"), op=ALU.add)
            chain.link(ins)
            layer_norm(3, OUT)
            for q in range(2):
                s = slice(q * 512, q * 512 + 512)
                dve.wait_ge(kexp_ready, 2 * q + 2)
                ins = dve.tensor_tensor(WKV[:, s], PS[2 + q][0:64, :], KS[:, s], op=ALU.mult)
                chain.link(ins)
                for b in range(2 * q, 2 * q + 2):
                    dve.tensor_tensor_scan(ST[:, b * D:b * D + D], T3[:, 0:1].to_broadcast([64, D]), WKV[:, b * D:b * D + D],
                                           0.0, ALU.mult, ALU.add).then_inc(states_ready, 1)
            for q in range(4):
                dve.wait_ge(out3_in_psum, q + 1)
                ins = dve.tensor_tensor(X[:, 2 * q:2 * q + 2, :].rearrange("p t d -> p (t d)"), PS[4 + q],
                                        X[:, 2 * q:2 * q + 2, :].rearrange("p t d -> p (t d)"), op=ALU.add)
            ins.then_inc(layer_done, 1)
            dve.wait_ge(layer_done, 3)
            layer_norm(4)
            experts(F4)
            dve.wait_ge(layer_done, 4)
            layer_norm(5, begun=True)
            dve.wait_ge(permuted, 16 * 8)
            dve.wait_ge(dec_ready, 2)

            def queries(b):
                dve.wait_ge(qtanh_ready, b + 1)
                dve.scalar_tensor_tensor(QT, QT, 1.0, PS[6].rearrange("p (g t) -> p g t", g=2), ALU.add, ALU.mult).then_inc(q_ready, 1)

            def keys(b):
                dve.wait_ge(ktanh_ready, b + 1)
                dve.scalar_tensor_tensor(KT, KT, 1.0, PS[7].rearrange("p (g t) -> p g t", g=2), ALU.add, ALU.mult).then_inc(k_ready, 1)

            def add_rows(b):
                dve.wait_ge(oss_in_psum, b + 1)
                dve.tensor_scalar(sso[:, :], PS[7][:, 0:2], 1e-6, None, ALU.add).then_inc(oeps_ready, 1)
                dve.wait_ge(or_ready, b + 1)
                dve.wait_ge(out5_in_psum, b + 1)
                for par in range(2):
                    tile = at(2 * b + par, 1)
                    ins = dve.scalar_tensor_tensor(X[:, tile, :], PS[5][:, par * D:par * D + D].unsqueeze(1), sso[:, par:par + 1],
                                                   OUT[:, tile, :], ALU.mult, ALU.add)
                ins.then_inc(x5_ready, 1)

            def sequence(b):
                first, last = isinstance(b, int) and b == 0, isinstance(b, int) and b == NB - 1
                for s in range(8):
                    dve.wait_ge(sc_in_psum, 8 * b + s + 1)
                    if s >= 2:
                        dve.wait_ge(o5_in_psum, 8 * b + s - 1)
                    dve.tensor_tensor(SCO[:, s % 2, :, :], BANKS[:, 2 * (s % 2):2 * (s % 2) + 2, 0:SW],
                                      DEC[:, 2 * s:2 * s + 2, :], op=ALU.mult).then_inc(p_ready, 1)
                    if s == 1 and not first:
                        add_rows(b - 1)
                    if s == 3 and not last:
                        queries(b + 1)
                if not last:
                    keys(b + 1)
                dve.wait_ge(o5_in_psum, 8 * b + 8)
                dve.wait_ge(u_ready, b + 1)
                dve.wait_ge(osq_ready, b + 1)
                dve.tensor_tensor(UO, PS[4], UT, op=ALU.mult).then_inc(uo_ready, 1)

            queries(0)
            keys(0)
            sequences_of(dve, sequence)
            add_rows(NB - 1)
            dve.wait_ge(x5_ready, NB)
            dve.sem_inc(layer_done, 1)
            layer_norm(6)
            experts(F6)
            dve.tensor_scalar(blockb[:, 0:P], blk, 1.0, -NEG, ALU.subtract, ALU.mult)
            for n in range(1, 4):
                ins = dve.tensor_scalar(blockb[:, n * P:n * P + P], blk, 1.0, -NEG, ALU.subtract, ALU.mult)
            ins.then_inc(masks_ready, 1)
            layer_norm(7, begun=True)
            heads = X[:, :, :].rearrange("p t (h a d) -> p t h a d", a=2, d=LD)

            def less_max(n):
                dve.wait_ge(s7_in_psum, n + 1)
                sc = BANKS[:, 2 * (n % 2):2 * (n % 2) + 2, :].rearrange("p k (j t) -> p (k j) t", j=4)
                dve.tensor_reduce(MXS[:, n % 2, :], sc, AX.X, ALU.max).then_inc(max_ready, 1)
                dve.wait_ge(max_ready, n + 1)
                if n >= 2:
                    dve.wait_ge(et7_ready, n - 1)
                dve.tensor_tensor(E[:, n % 2, :, :], sc, MXS[:, n % 2, :].unsqueeze(2).to_broadcast([P, 8, P]),
                                  op=ALU.subtract).then_inc(s7_ready, 1)

            def transposed(n):
                dve.wait_ge(e7_ready, n + 1)
                if n >= 2:
                    dve.wait_ge(av_in_psum, n - 1)
                dve.transpose(M[:, n % 2, :, :].rearrange("p h k -> p (h k)"), E[:, n % 2, :, :].rearrange("p h k -> p (h k)")).then_inc(et7_ready, 1)

            def add_values(n):
                c = n % 2
                dve.wait_ge(av_in_psum, n + 1)
                av = PS[4 + c][:, 0:AW].rearrange("p (h d) -> p h d", h=8)
                dve.reciprocal(RS[:, c, :], av[:, :, LD]).then_inc(recip_ready, 1)
                dve.wait_ge(recip_ready, n + 1)
                dve.tensor_tensor(AV[:, c, :, :], av[:, :, 0:LD], RS[:, c, :].unsqueeze(2).to_broadcast([P, 8, LD]),
                                  op=ALU.mult).then_inc(av_ready, 1)
                dve.wait_ge(av_ready, n + 1)
                xh = heads[:, n, :, c, :]
                dve.tensor_tensor(xh, xh, AV[:, c, :, :], op=ALU.add).then_inc(x7_ready, 1)

            less_max(0)
            for n in range(NT):
                if n < NT - 1:
                    less_max(n + 1)
                transposed(n)
                if n:
                    add_values(n - 1)
            add_values(NT - 1)
            dve.wait_ge(x7_ready, NT)
            dve.sem_inc(layer_done, 1)
            layer_norm(8)
            experts(F8)

        @block.tensor
        def _(pe):
            def transpose_xn(layer, odd_from=0):
                for q in range(NT // 2):
                    if q >= 2:
                        pe.wait_ge(xt_ready, 4 * layer + q - 1)
                    for t in range(2 * q, 2 * q + 2):
                        pe.wait_ge(xn_ready, NT * layer + t + 1)
                        for k in range(KD):
                            ins = pe.transpose(PS[6 + q % 2][:, k * 256 + (t % 2) * P:k * 256 + (t % 2) * P + P],
                                               XN[:, t, k * P + (t % 2) * odd_from:k * P + (t % 2) * odd_from + P], ident)
                    ins.then_inc(xt_in_psum, 1)

            pe.wait_ge(consts_loaded, 16)
            transpose_xn(0)
            def up(m, u, bank=0):
                if u == 0:
                    pe.wait_ge(wx_loaded, m * 2 + 16)
                after(pe, xp_ready, m - 1 if isinstance(m, int) and m < NT else m)
                for k in range(KD):
                    ins = pe.matmul(PS[bank], WX[:, k, (u // 2) * P:(u // 2) * P + P], XT[:, k, (u % 2) * 512:(u % 2) * 512 + 512],
                                    start=k == 0, stop=k == KD - 1)
                ins.then_inc(up_in_psum, 1)

            def to_tokens(m, u, bank=1):
                pe.wait_ge(xc_ready, m + 1)
                after(pe, xtok_ready, m - 1 if isinstance(m, int) and m < NT else m)
                for t in range(4):
                    ins = pe.transpose(PS[bank][:, t * P:t * P + P], TH[:, u % 2, t // 2, (t % 2) * P:(t % 2) * P + P], ident)
                ins.then_inc(xc_in_psum, 1)

            def b_and_c(n):
                for k in range(KD):
                    ins = pe.matmul(PS[n], WB[:, k, (n // 2) * (NS + NH):(n // 2) * (NS + NH) + NS],
                                    XT[:, k, (n % 2) * 512:(n % 2) * 512 + 512], start=k == 0, stop=k == KD - 1)
                ins.then_inc(bc_in_psum, 1)

            def step_sizes(q):
                pe.wait_ge(bc_ready, q + 1)
                for t in range(2 * q, 2 * q + 2):
                    for k in range(KD):
                        ins = pe.matmul(PS[q][:, (t % 2) * 256:(t % 2) * 256 + NS + NH], XT[:, k, t * P:t * P + P],
                                        WB[:, k, 0:NS + NH], start=k == 0, stop=k == KD - 1)
                ins.then_inc(bdt_in_psum, 1)

            def b_times_c():
                pe.wait_ge(b_ready, 4)
                for q in range(2):
                    for t in range(4 * q, 4 * q + 4):
                        ins = pe.matmul(PS[2 + q][:, (t % 4) * P:(t % 4) * P + P], BT[:, t * P:t * P + P],
                                        CT[:, t * P:t * P + P], start=True, stop=True)
                    ins.then_inc(gt_in_psum, 1)

            def cumulative():
                pe.wait_ge(da_ready, 1)
                pe.wait_ge(masks_ready, 2)
                for n, lower in enumerate((tri, ones[:, :])):
                    pe.matmul(PS[n][:, 0:NT * NH], lower, dA[:, :, :].rearrange("p t h -> p (t h)"),
                              start=True, stop=True).then_inc(cum_in_psum, 1)
                pe.wait_ge(gt_ready, 2)
                for t in range(NT):
                    ins = pe.matmul(PS[2 + t // 4][0:NH, (t % 4) * P:(t % 4) * P + P], dA[:, t, :], tri, start=True, stop=True)
                    if t % 4 == 3:
                        ins.then_inc(cumt_in_psum, 1)

            pe.wait_ge(xt_ready, 4)
            for u in range(NT + 2):
                if u < NT:
                    up(u, u, 6 + u % 2)
                if u == 0:
                    pe.wait_ge(wb_loaded, 16)
                if u < 4:
                    b_and_c(u)
                if 1 <= u <= 4:
                    step_sizes(u - 1)
                if u == 5:
                    b_times_c()
                if u >= 2:
                    to_tokens(u - 2, u - 2, 4 + u % 2)
                if u == 7:
                    cumulative()
            pe.wait_ge(xtok_ready, NT)
            pe.wait_ge(cum_ready, 3)

            def gated_transposed(n, c):
                pe.wait_ge(gated_ready, n + 1)
                after(pe, gtr_ready, n)
                for k in range(GC):
                    ins = pe.transpose(PS[6][:, k * P:k * P + P], G[:, c % 2, k * P:k * P + P], ident)
                ins.then_inc(g_in_psum, 1)

            def project_out(n, c, slot):
                pe.wait_ge(gtr_ready, n + 1)
                after(pe, o_added, n)
                for k in range(GC):
                    ins = pe.matmul(PS[7][:, 0:D], GTR[:, c % 2, k * P:k * P + P], WO[:, slot, k, :], start=k == 0, stop=k == GC - 1)
                ins.then_inc(o_in_psum, 1)

            def values(c, slot):
                for h in range(GH):
                    cols_ = slice(h * HD, h * HD + HD)
                    ins = pe.matmul(PS[2][:, cols_], M[:, c % 2, h, :], XTOK[:, slot, c, cols_], start=True, stop=True)
                ins.then_inc(y_in_psum, 1)

            def group(g, slot):
                first, last = isinstance(g, int) and g == 0, isinstance(g, int) and g == NG - 1
                pe.wait_ge(wz_loaded, (g + 1) * 16)
                pe.wait_ge(h0_loaded, (g + 1) * 16)
                pe.wait_ge(wo_ready, g + 1)
                for c in range(NT):
                    n = g * NT + c
                    after(pe, zsilu_ready, n)
                    for k in range(KD):
                        ins = pe.matmul(PS[4], XT[:, k, c * P:c * P + P], WZ[:, slot, k, :], start=k == 0, stop=k == KD - 1)
                    ins.then_inc(z_in_psum, 1)
                    if not last:
                        up(n + NT, c)
                    if c and not last:
                        to_tokens(n + NT - 1, c - 1)
                    if c == 0:
                        pe.wait_ge(xtok_ready, (g + 1) * NT)
                    pe.wait_ge(mix_ready, n + 1)
                    after(pe, y0_ready, n)
                    values(c, slot)
                    if not (first and c == 0):
                        gated_transposed(n - 1, (c - 1) % NT)
                    if c % 2 == 0:
                        pe.wait_ge(xs_ready, g * NB + c // 2 + 1)
                        after(pe, h1_ready, g * NB + c // 2)
                        pe.matmul(PS[5], BN[:, c // 2, :], XS[:, :], start=True, stop=True).then_inc(s_in_psum, 1)
                    else:
                        pe.wait_ge(h1_ready, g * NB + c // 2 + 1)
                    after(pe, y1_ready, n)
                    pe.matmul(PS[3], CT[:, c * P:c * P + P], H1[:, :] if c % 2 else H0[:, slot, :], start=True, stop=True).then_inc(i_in_psum, 1)
                    if not (first and c == 0):
                        project_out(n - 1, (c - 1) % NT, slot if c else 1 - slot)
                if not last:
                    to_tokens(n + NT, NT - 1)

            groups_of(pe, group)
            n = NG * NT - 1
            gated_transposed(n, NT - 1)
            project_out(n, NT - 1, 1)

            def experts(f):
                def router_hidden():
                    for q in range(2):
                        for k in range(KD):
                            ins = pe.matmul(PS[4 + q][0:8, :], SM[:, k, 16:24], XT[:, k, q * 512:q * 512 + 512], start=k == 0, stop=k == KD - 1)
                        ins.then_inc(hop_in_psum, 1)

                def router():
                    if f.gated:
                        logits = [(XT[:, k, t * P:t * P + P], SM[:, k, 0:16]) for t in range(NT) for k in range(KD)]
                    else:
                        pe.wait_ge(hop_ready, 2 * (f.n - 1))
                        logits = [(TT[:, t * P:t * P + P], WG[:, :]) for t in range(NT)]
                    m = f.routed
                    per = len(logits) // NT
                    for n, (l, r) in enumerate(logits):
                        ins = pe.matmul(PS[4][:, n // per * m:n // per * m + m], l, r, start=n % per == 0, stop=n % per == per - 1)
                    ins.then_inc(logits_in_psum, 1)

                def scores_transposed():
                    pe.wait_ge(weights_ready, f.n - 1)
                    for t in range(NT):
                        ins = pe.transpose(PS[1 + 2 * (t // 4)][0:8, (t % 4) * P:(t % 4) * P + P], LR[:, t, 0:8], ident)
                        if t % 4 == 3:
                            ins.then_inc(scores_in_psum, 1)

                def bias_products():
                    pe.wait_ge(scores_ready, 2 * (f.n - 1))
                    for q in range(4):
                        if q >= 2:
                            pe.wait_ge(bias_added, 4 * (f.n - 2) + q - 1)
                        for t in range(2 * q, 2 * q + 2):
                            ins = pe.matmul(PS[1 + 2 * (q % 2)][:, (t % 2) * D:(t % 2) * D + D], SCT[:, t * P:t * P + P], BD[:, :], start=True, stop=True)
                        ins.then_inc(bias_in_psum, 1)

                def product(to):
                    return lambda stationary, moving, start, stop: pe.matmul(
                        to, stationary, moving, start=start, stop=stop)

                def up(s, r, pair):
                    pe.wait_ge(ul_ready[r // 2], pair + 1)
                    if isinstance(s, int) and s < f.s0 + 2:
                        pe.wait_ge(xl_ready, 4 * f.n + 2 * (s - f.s0) + 2)
                    else:
                        pe.wait_ge(gate_ready, s - 1)
                    for w in range(2 if f.gated else 1):
                        for k in range(KD):
                            c, half_ = slice((2 * w + k) * P, (2 * w + k) * P + P), slice((r % 2) * 512, (r % 2) * 512 + 512)
                            ins = split_product(product(PS[2 * (r % 2) + w]), (UH[:, r // 2, c], XH[:, k, half_]),
                                                (UL[:, r // 2, c], XL[:, k, half_]), start=k == 0, stop=k == KD - 1)
                    ins.then_inc(hidden_in_psum, 1)

                def down(s, r, pair):
                    pe.wait_ge(dl_ready[r // 2], pair + 1)
                    pe.wait_ge(fl_ready, s + 1)
                    if not (isinstance(s, int) and s < f.s0 + 2):
                        pe.wait_ge(down_added, s - 1)
                    for t in range(4):
                        ins = split_product(product(PS[4 + 2 * (r % 2) + t // 2][:, (t % 2) * D:(t % 2) * D + D]),
                                            (FH[:, r % 2, t * P:t * P + P], DH[:, r // 2, :]),
                                            (FL[:, r % 2, t * P:t * P + P], DL[:, r // 2, :]))
                    ins.then_inc(down_in_psum, 1)

                def pair(i):
                    s, p = f.s0 + 4 * i, f.p0 + i
                    first = isinstance(i, int) and i == 0
                    for r in range(4):
                        up(s + r, r, p)
                        if first and r == 2:
                            pe.wait_ge(logits_ready, 2 * f.n + 1)
                        if not (first and r < 2):
                            down(s + r - 2, (r + 2) % 4, p if r >= 2 else p - 1)
                        if first and r == 1:
                            router()
                    if first and not f.gated:
                        scores_transposed()

                if f.n == 0:
                    pe.wait_ge(small_loaded, SMALL)
                pe.wait_ge(xt_ready, 4 * (f.norm + 1))
                if not f.gated:
                    router_hidden()
                pairs_of(pe, f, pair)
                if not f.gated:
                    bias_products()
                for r in range(2, 4):
                    down(f.s0 + 4 * (f.pairs - 1) + r, r, f.p0 + f.pairs - 1)

            transpose_xn(1)
            experts(F2)
            transpose_xn(2)
            pe.wait_ge(xt_ready, 4 * 3)
            pe.wait_ge(small_loaded, SMALL)
            for q in range(4):
                for t in range(2 * q, 2 * q + 2):
                    for k in range(KD):
                        ins = pe.matmul(PS[q][:, (t % 2) * D:(t % 2) * D + D], XT[:, k, (t ^ 1) * P:(t ^ 1) * P + P],
                                        W3[:, k, 0:D], start=k == 0, stop=k == KD - 1)
                ins.then_inc(shift_in_psum, 1)
            transpose_xn(3)
            pe.wait_ge(xt_ready, 4 * 4)
            for q in range(2):
                for n in range(2):
                    for k in range(KD):
                        ins = pe.matmul(PS[2 * n + q][0:64, :], W3[:, k, D + 64 * n:D + 64 * n + 64],
                                        XT[:, k, q * 512:q * 512 + 512], start=k == 0, stop=k == KD - 1)
                ins.then_inc(kv_in_psum, 1)
            pe.wait_ge(small_loaded, SMALL)
            for q in range(4):
                pe.wait_ge(states_ready, q + 1)
                for t in range(2 * q, 2 * q + 2):
                    ins = pe.matmul(PS[4 + q][:, (t % 2) * D:(t % 2) * D + D], ST[:, t * P:t * P + P], WO3[:, :], start=True, stop=True)
                ins.then_inc(out3_in_psum, 1)
            transpose_xn(4)
            experts(F4)
            transpose_xn(5)
            pe.wait_ge(w5_loaded, 2 * 16)
            def project(bank, first_col, signal):
                for g in range(2):
                    for k in range(KD):
                        ins = pe.matmul(PS[bank][:, g * D:g * D + D], W5[:, k, first_col + g * P:first_col + g * P + P], XB[:, k, :],
                                        start=k == 0, stop=k == KD - 1)
                ins.then_inc(signal, 1)

            def project_values():
                for c in range(2):
                    for k in range(KD):
                        ins = pe.matmul(PS[5][:, c * D:c * D + D], XB[:, k, c * P:c * P + P], W5[:, k, 2 * D:3 * D],
                                        start=k == 0, stop=k == KD - 1)
                ins.then_inc(v_in_psum, 1)

            def scores(b, s):
                pe.wait_ge(qh_ready[s // 4], 4 * b + s + 1 if s < 4 else b + 1)
                for j in range(2):
                    q = QH[s // 4][:, (2 * s + j) % 8, :]
                    bank = PS[2 * (s % 2) + j]
                    pe.matmul(bank[:, 0:D], KT[:, s // 4, 0:P], q, start=True, stop=True)
                    ins = pe.matmul(bank[:, D:SW], KT[:, s // 4, P:D], q[:, P:D], start=True, stop=True)
                ins.then_inc(sc_in_psum, 1)

            def attend(b, s):
                pe.wait_ge(p_ready, 8 * b + s + 1)
                rows_ = slice(32 * (s % 4), 32 * (s % 4) + 32)
                o = PS[4][rows_, (s // 4) * D:(s // 4) * D + D]
                for c in range(2):
                    for j in range(2):
                        ins = pe.matmul(o[:, c * P:], V5[:, c, 2 * s + j, :], SCO[:, s % 2, j, c * D:c * P + D],
                                        start=c == 0 and j == 0, stop=c == 1 and j == 1,
                                        skip_group_check=True)
                ins.then_inc(o5_in_psum, 1)

            def out_rows(b):
                pe.wait_ge(osq_ready, b + 1)
                osq = OSQ.rearrange("p (g t a) -> p g t a", g=2, a=2)
                for par in range(2):
                    for g in range(2):
                        ins = pe.matmul(PS[7][:, par:par + 1], osq[:, g, :, par], ones[:, 0:1], start=g == 0, stop=g == 1)
                ins.then_inc(oss_in_psum, 1)
                pe.wait_ge(uo_ready, b + 1)
                uo = UO.rearrange("p (g t a) -> p g t a", g=2, a=2)
                for par in range(2):
                    for g in range(2):
                        ins = pe.matmul(PS[5][:, par * D:par * D + D], uo[:, g, :, par], WO5[:, g, :], start=g == 0, stop=g == 1)
                ins.then_inc(out5_in_psum, 1)

            def sequence(b):
                first, last = isinstance(b, int) and b == 0, isinstance(b, int) and b == NB - 1
                pe.wait_ge(k_ready, b + 1)
                for s in range(8):
                    scores(b, s)
                    if s == 0:
                        pe.wait_ge(v_ready, b + 1)
                        if not first:
                            out_rows(b - 1)
                    else:
                        attend(b, s - 1)
                    if not last:
                        if s == 1:
                            pe.wait_ge(xb_ready, b + 2)
                            pe.wait_ge(u_ready, b + 1)
                            project(6, 0, q_in_psum)
                        if s == 2:
                            if not first:
                                pe.wait_ge(oeps_ready, b)
                            project(7, D, k_in_psum)
                        if s == 4:
                            if not first:
                                pe.wait_ge(x5_ready, b)
                            project_values()
                        if s == 5:
                            pe.wait_ge(q_ready, b + 2)
                            project(6, 3 * D, u_in_psum)
                attend(b, 7)

            pe.wait_ge(xb_ready, 1)
            project(6, 0, q_in_psum)
            project(7, D, k_in_psum)
            project_values()
            pe.wait_ge(q_ready, 1)
            project(6, 3 * D, u_in_psum)
            sequences_of(pe, sequence)
            out_rows(NB - 1)
            pe.wait_ge(x5_ready, NB)
            transpose_xn(6)
            experts(F6)
            transpose_xn(7, odd_from=LD)
            pe.wait_ge(masks_ready, 3)
            pe.wait_ge(xa_ready, NT)

            def scores7(n):
                pe.wait_ge(xe_ready, n + 1)
                if n >= 2:
                    pe.wait_ge(s7_ready, n - 1)
                for k in range(KD):
                    bank = PS[2 * (n % 2) + k]
                    pe.matmul(bank, identb[:, :], blockb[:, :], start=True, stop=False)
                    ins = pe.matmul(bank, XT[:, k, n * P:n * P + P], XE[:, n % 2, k, :, :].rearrange("p j t -> p (j t)"), start=False, stop=True)
                ins.then_inc(s7_in_psum, 1)

            def values7(n):
                pe.wait_ge(et7_ready, n + 1)
                if n >= 2:
                    pe.wait_ge(av_ready, n - 1)
                for h in range(8):
                    first, end = h * (LD + 1), (h + 1) * (LD + 1)
                    ins = pe.matmul(PS[4 + n % 2][:, first:end], M[:, n % 2, h, :], XA[:, n * AW + first:n * AW + end], start=True, stop=True)
                ins.then_inc(av_in_psum, 1)

            scores7(0)
            scores7(1)
            for n in range(NT):
                if n < NT - 2:
                    scores7(n + 2)
                values7(n)
            transpose_xn(8)
            experts(F8)


def kernel(**inputs):
    import numpy as np
    import concourse.bacc as bacc
    from concourse.bass_utils import run_bass_kernel_spmd

    a = {n: np.asarray(v) for n, v in inputs.items()}
    t = lambda m: np.ascontiguousarray(m.T)

    def blocks(m):
        return np.ascontiguousarray(m.reshape(KD, P, -1).transpose(1, 0, 2))

    def groups(m):
        return np.ascontiguousarray(m.reshape(KD, P, NG, GW).transpose(2, 1, 0, 3))

    win = t(a["L0_attn_a_in_proj_w"])
    idx = np.arange(P)
    consts = np.concatenate([
        np.eye(P), idx[:, None] <= idx[None, :], np.arange(2 * P)[None, :] - idx[:, None],
        idx[:, None] // 32 == idx[None, :] // 32, idx[:, None] // LD == np.arange(8)[None, :],
        idx[:, None] // LD == 2 * np.arange(4)[None, :]], axis=1).astype(np.float32)
    b, c, dt = win[:, 2 * DI:2 * DI + NS], win[:, 2 * DI + NS:2 * DI + 2 * NS], win[:, 2 * DI + 2 * NS:]
    chan = np.concatenate([a["L0_attn_a_conv_w"], a["L0_attn_a_conv_b"][:, None], a["L0_attn_a_conv_state"][0]], axis=1)
    def rows_of(w):
        return w.reshape(-1, KD, P, P).transpose(0, 2, 1, 3).reshape(-1, P, KD * P)

    def experts_up(routed, shared):
        return np.concatenate([rows_of(a[routed]), rows_of(a[shared].reshape(D, 4, P).transpose(1, 0, 2))])

    col = lambda v: v.reshape(KD, P).T
    arrays = {
        "x": a["L0_attn_a_x"].reshape(T, D),
        "consts": consts,
        "rows": np.concatenate([a["L0_attn_a_dt_bias"], a["L0_attn_a_A_log"], a["L0_attn_a_D_param"], a["L0_attn_b_gate"],
                                a["L1_attn_a_slope_rate"].reshape(-1)]),
        "cols": np.stack([col(a["L0_attn_a_norm_w"]), col(a["L0_attn_b_ln_gamma"]), col(a["L0_attn_b_ln_beta"])], axis=1),
        "wx": groups(win[:, DI:2 * DI]),
        "wz": groups(win[:, 0:DI]),
        "wbcdt": blocks(np.concatenate([b, dt, c], axis=1)),
        "wout": t(a["L0_attn_a_out_proj_w"]).reshape(NG, GC, P, D).transpose(0, 2, 1, 3),
        "chan": chan.reshape(NG, GC, P, NPC).transpose(0, 2, 1, 3),
        "inw": a["L0_attn_a_inner_norm_w"].reshape(NG, GC, P).transpose(0, 2, 1),
        "h0": a["L0_attn_a_ssm_state"][0].reshape(NG, GH, NS, HD).transpose(0, 2, 1, 3).reshape(NG, NS, GW),
        "small": np.concatenate([blocks(a["L0_ffn_w_router"]), blocks(t(a["L1_ffn_Wg1"]))], axis=2),
        "w3": np.concatenate([blocks(t(a[f"L0_attn_b_W_{n}"])) for n in ("shift", "key", "value")], axis=2),
        "wo3": t(a["L0_attn_b_W_output"]),
        "t3": np.stack([a["L0_attn_b_time_decay"], a["L0_attn_b_time_first"]], axis=1),
        "wu2": np.concatenate([experts_up("L0_ffn_we1", "L0_ffn_ws1"), experts_up("L0_ffn_we3", "L0_ffn_ws3")], axis=2),
        "wd2": np.concatenate([a["L0_ffn_we2"], a["L0_ffn_ws2"].reshape(4, P, D)]),
        "wu6": np.concatenate([rows_of(a["L1_ffn_Wup"].transpose(0, 2, 1)), a["L1_ffn_bup"][:, :, None]], axis=2),
        "wd6": a["L1_ffn_Wdown"].transpose(0, 2, 1),
        "wg6": t(a["L1_ffn_Wg2"]),
        "bd6": a["L1_ffn_bdown"],
        "w5": blocks(t(a["L1_attn_a_W_qkvu"])),
        "wo5": blocks(t(a["L1_attn_a_W_out"])),
    }
    nc = bacc.Bacc("TRN2", target_bir_lowering=False, num_devices=1)
    arrays = {f"in_{n}": np.ascontiguousarray(v) for n, v in arrays.items()}
    args = {n[3:]: nc.dram_tensor(n, v.shape, mybir.dt.from_np(v.dtype), kind="ExternalInput").ap() for n, v in arrays.items()}
    out = nc.dram_tensor("out_x", (T, D), FP32, kind="ExternalOutput").ap()
    mixer_program(nc, out=out, **args)
    r = run_bass_kernel_spmd(nc, [arrays], core_ids=[0])
    return r.results[0]["out_x"].reshape(4, 256, 256)
```
